# Optimizing a Trainium2 kernel written in Bass

```python
import numpy as np
import jax
import jax.numpy as jnp

def _softmax(x, axis=-1):
    return jax.nn.softmax(x, axis=axis)

def _gelu(x):
    return jax.nn.gelu(x, approximate=True)

def _silu(x):
    return jax.nn.silu(x)

def _sigmoid(x):
    return jax.nn.sigmoid(x)

def _layernorm(x, axis=-1, eps=1e-05):
    m = jnp.mean(x, axis=axis, keepdims=True)
    v = jnp.var(x, axis=axis, keepdims=True)
    return (x - m) / jnp.sqrt(v + eps)

def _scatter_add(tgt, idx, src, axis=0):
    return tgt.at[idx].add(src)

def _segment_sum(src, seg, n):
    return jax.ops.segment_sum(src, seg, n)
kernel_name = 'mk_gps_d1_gnn_r16_fa4546'

def setup_inputs(seed: int=0):
    np.random.seed(seed)
    _w = jnp.asarray

    def _rec_inputs():
        import jax
        import jax.numpy as jnp
        _gk = jax.random.key(seed)
        x = -0.0003713 + 1 * jax.random.normal(jax.random.fold_in(_gk, 1), (3125, 256), jnp.float32)
        _s = jax.random.randint(jax.random.fold_in(_gk, 2), (50000,), 0, 3125, jnp.int32)
        _d = jax.random.randint(jax.random.fold_in(_gk, 3), (50000,), 0, 3125, jnp.int32)
        _loop = jnp.arange(3125, dtype=jnp.int32)
        src = jnp.concatenate([_s, _d, _loop])
        dst = jnp.concatenate([_d, _s, _loop])
        _o = jnp.argsort(dst, stable=True)
        src = src[_o]
        dst = dst[_o]
        return (x, src, dst)
    x, src, dst = _rec_inputs()

    def _L0_gnn_setup():
        import jax, jax.numpy as jnp
        import numpy as np
        N, F, H, D = (3125, 256, 4, 64)
        E = 50000
        LN_EPS = 1e-05

        def _layernorm(x, g, b):
            mu = jnp.mean(x, axis=-1, keepdims=True)
            var = jnp.mean(jnp.square(x - mu), axis=-1, keepdims=True)
            return (x - mu) * jax.lax.rsqrt(var + LN_EPS) * g + b
        key = jax.random.key(seed)
        ks = jax.random.split(key, 12)
        s = 1.0 / np.sqrt(F)
        return {'feat': jax.random.normal(ks[0], (N, F), dtype=jnp.float32), 'src': jax.random.randint(ks[1], (E,), 0, N, dtype=jnp.int32), 'dst': jax.random.randint(ks[2], (E,), 0, N, dtype=jnp.int32), 'Wq': jax.random.uniform(ks[3], (F, H * D), jnp.float32, -s, s), 'Wk': jax.random.uniform(ks[4], (F, H * D), jnp.float32, -s, s), 'Wv': jax.random.uniform(ks[5], (F, H * D), jnp.float32, -s, s), 'ln_g': jnp.ones((F,), jnp.float32), 'ln_b': jnp.zeros((F,), jnp.float32), 'W1': jax.random.uniform(ks[6], (F, 4 * F), jnp.float32, -s, s), 'b1': jnp.zeros((4 * F,), jnp.float32), 'alpha': jnp.full((4 * F,), 0.25, jnp.float32), 'W2': jax.random.uniform(ks[7], (4 * F, F), jnp.float32, -s / 2.0, s / 2.0), 'b2': jnp.zeros((F,), jnp.float32)}
    _L0_gnn_all = _L0_gnn_setup()
    _L0_gnn_in = {k: v for k, v in _L0_gnn_all.items() if k in ('Wq', 'Wk', 'Wv', 'ln_g', 'ln_b', 'W1', 'b1', 'alpha', 'W2', 'b2')}
    del _L0_gnn_all

    def _L0_mix_setup():
        import jax, jax.numpy as jnp
        import numpy as np
        A, Bc, Cc = (0.5, 1.0, 1.0)
        H = 8
        EPS = 1e-12

        def _normalize(t):
            n = jnp.linalg.norm(t, axis=-1, keepdims=True)
            return t / jnp.maximum(n, EPS)
        key = jax.random.key(seed)
        ks = jax.random.split(key, 5)
        B, N, C = (8, 128, 256)
        D = C // H
        x = jax.random.normal(ks[0], (B, N, C), dtype=jnp.float32)
        Wqkv = jax.random.normal(ks[1], (3 * H * D, C), dtype=jnp.float32) * 0.02
        bqkv = jnp.zeros((3 * H * D,), dtype=jnp.float32)
        Wproj = jax.random.normal(ks[2], (C, H * D), dtype=jnp.float32) * 0.02
        bproj = jnp.zeros((C,), dtype=jnp.float32)
        temperature = jnp.ones((1, H, 1, 1), dtype=jnp.float32)
        return {'x': x, 'Wqkv': Wqkv, 'bqkv': bqkv, 'Wproj': Wproj, 'bproj': bproj, 'temperature': temperature}
    _L0_mix_all = _L0_mix_setup()
    _L0_mix_in = {k: v for k, v in _L0_mix_all.items() if k in ('Wqkv', 'bqkv', 'Wproj', 'bproj', 'temperature')}
    del _L0_mix_all

    def _L0_ffn_setup():
        import jax, jax.numpy as jnp
        import numpy as np
        TOP_K = 2
        LN_EPS = 1e-05
        key = jax.random.key(seed)
        ks = jax.random.split(key, 8)
        B, S, D, E, H = (16, 1024, 256, 8, 1024)
        x = jax.random.normal(ks[0], (B, S, D), dtype=jnp.float32)
        Wr = jax.random.normal(ks[1], (D, E), dtype=jnp.float32) * 0.1
        br = jnp.zeros((E,), dtype=jnp.float32)
        ln_g = jnp.ones((E, D), dtype=jnp.float32)
        ln_b = jnp.zeros((E, D), dtype=jnp.float32)
        W1 = jax.random.normal(ks[2], (E, D, H), dtype=jnp.float32) * (1.0 / np.sqrt(D))
        b1 = jnp.zeros((E, H), dtype=jnp.float32)
        W2 = jax.random.normal(ks[3], (E, H, D), dtype=jnp.float32) * (1.0 / np.sqrt(H))
        b2 = jnp.zeros((E, D), dtype=jnp.float32)
        return {'x': x, 'Wr': Wr, 'br': br, 'ln_g': ln_g, 'ln_b': ln_b, 'W1': W1, 'b1': b1, 'W2': W2, 'b2': b2}
    _L0_ffn_all = _L0_ffn_setup()
    _L0_ffn_in = {k: v for k, v in _L0_ffn_all.items() if k in ('Wr', 'br', 'ln_g', 'ln_b', 'W1', 'b1', 'W2', 'b2')}
    del _L0_ffn_all
    return {'x': x, 'src': src, 'dst': dst, 'L0_gnn_Wq': _L0_gnn_in['Wq'], 'L0_gnn_Wk': _L0_gnn_in['Wk'], 'L0_gnn_Wv': _L0_gnn_in['Wv'], 'L0_gnn_ln_g': _L0_gnn_in['ln_g'], 'L0_gnn_ln_b': _L0_gnn_in['ln_b'], 'L0_gnn_W1': _L0_gnn_in['W1'], 'L0_gnn_b1': _L0_gnn_in['b1'], 'L0_gnn_alpha': _L0_gnn_in['alpha'], 'L0_gnn_W2': _L0_gnn_in['W2'], 'L0_gnn_b2': _L0_gnn_in['b2'], 'L0_mix_Wqkv': _L0_mix_in['Wqkv'], 'L0_mix_bqkv': _L0_mix_in['bqkv'], 'L0_mix_Wproj': _L0_mix_in['Wproj'], 'L0_mix_bproj': _L0_mix_in['bproj'], 'L0_mix_temperature': _L0_mix_in['temperature'], 'L0_ffn_Wr': _L0_ffn_in['Wr'], 'L0_ffn_br': _L0_ffn_in['br'], 'L0_ffn_ln_g': _L0_ffn_in['ln_g'], 'L0_ffn_ln_b': _L0_ffn_in['ln_b'], 'L0_ffn_W1': _L0_ffn_in['W1'], 'L0_ffn_b1': _L0_ffn_in['b1'], 'L0_ffn_W2': _L0_ffn_in['W2'], 'L0_ffn_b2': _L0_ffn_in['b2']}

def reference(x, src, dst, L0_gnn_Wq, L0_gnn_Wk, L0_gnn_Wv, L0_gnn_ln_g, L0_gnn_ln_b, L0_gnn_W1, L0_gnn_b1, L0_gnn_alpha, L0_gnn_W2, L0_gnn_b2, L0_mix_Wqkv, L0_mix_bqkv, L0_mix_Wproj, L0_mix_bproj, L0_mix_temperature, L0_ffn_Wr, L0_ffn_br, L0_ffn_ln_g, L0_ffn_ln_b, L0_ffn_W1, L0_ffn_b1, L0_ffn_W2, L0_ffn_b2):
    import jax
    import jax.numpy as jnp

    def _L0_gnn_ref(feat, src, dst, Wq, Wk, Wv, ln_g, ln_b, W1, b1, alpha, W2, b2):
        import jax, jax.numpy as jnp
        import numpy as np
        N, F, H, D = (3125, 256, 4, 64)
        E = 50000
        LN_EPS = 1e-05

        def _layernorm(x, g, b):
            mu = jnp.mean(x, axis=-1, keepdims=True)
            var = jnp.mean(jnp.square(x - mu), axis=-1, keepdims=True)
            return (x - mu) * jax.lax.rsqrt(var + LN_EPS) * g + b
        feat_c = jax.lax.stop_gradient(feat)
        q = (feat @ Wq).reshape(N, H, D)
        k = (feat_c @ Wk).reshape(N, H, D)
        v = (feat_c @ Wv).reshape(N, H, D)
        e = jnp.einsum('ehd,ehd->eh', k[src], q[dst]) / jnp.sqrt(jnp.float32(H * D))
        emax = jax.ops.segment_max(e, dst, num_segments=N)
        ex = jnp.exp(e - emax[dst])
        denom = jax.ops.segment_sum(ex, dst, num_segments=N)
        a = ex / denom[dst]
        m = v[src] * a[..., None]
        ft2 = jax.ops.segment_sum(m, dst, num_segments=N).reshape(N, F)
        rst = ft2 + feat
        rst = _layernorm(rst, ln_g, ln_b)
        h = rst @ W1 + b1
        h = jnp.where(h > 0, h, alpha * h)
        ffn = h @ W2 + b2
        rst = _layernorm(rst + ffn, ln_g, ln_b)
        return rst

    def _L0_mix_ref(x, Wqkv, bqkv, Wproj, bproj, temperature):
        import jax, jax.numpy as jnp
        import numpy as np
        A, Bc, Cc = (0.5, 1.0, 1.0)
        H = 8
        EPS = 1e-12

        def _normalize(t):
            n = jnp.linalg.norm(t, axis=-1, keepdims=True)
            return t / jnp.maximum(n, EPS)
        B, N, C = x.shape
        D = C // H
        scale = float(D) ** 0.25
        qkv = (x @ Wqkv.T + bqkv).reshape(B, N, 3, H, D)
        qkv = jnp.transpose(qkv, (2, 0, 3, 1, 4))
        q, k, v = (qkv[0], qkv[1], qkv[2])
        q = q * scale
        v1 = jnp.concatenate([jnp.ones((B, H, N, 1), dtype=v.dtype), v], axis=-1)
        qn = _normalize(q) * (scale * temperature)
        kn = _normalize(k) * scale
        vN = v1 / N
        kv_mod = jnp.einsum('bhni,bhnj,bhne->bhije', kn, kn, vN)
        kv = jnp.einsum('bhnd,bhne->bhde', kn, vN)
        vsum = jnp.sum(vN, axis=-2)[:, :, None, :]
        y = A * jnp.einsum('bhni,bhnj,bhije->bhne', qn, qn, kv_mod) + scale ** 2 * Bc * jnp.einsum('bhnd,bhde->bhne', qn, kv) + scale ** 4 * Cc * vsum
        y_norm, y = (y[..., :1], y[..., 1:])
        y = y / y_norm
        out = jnp.transpose(y, (0, 2, 1, 3)).reshape(B, N, H * D)
        return out @ Wproj.T + bproj

    def _L0_ffn_ref(x, Wr, br, ln_g, ln_b, W1, b1, W2, b2):
        import jax, jax.numpy as jnp
        import numpy as np
        TOP_K = 2
        LN_EPS = 1e-05
        B, S, D = x.shape
        N = B * S
        xt = x.reshape(N, D)
        logits = xt @ Wr + br
        probs = jax.nn.softmax(logits, axis=-1)
        top_p, top_idx = jax.lax.top_k(probs, TOP_K)
        weights = top_p / top_p.sum(axis=-1, keepdims=True)
        mu = xt.mean(axis=-1, keepdims=True)
        var = ((xt - mu) ** 2).mean(axis=-1, keepdims=True)
        xn = (xt - mu) * jax.lax.rsqrt(var + LN_EPS)
        xe = xn[None, :, :] * ln_g[:, None, :] + ln_b[:, None, :]
        h = jax.nn.gelu(jnp.einsum('end,edh->enh', xe, W1) + b1[:, None, :], approximate=False)
        y = jnp.einsum('enh,ehd->end', h, W2) + b2[:, None, :]
        y_tok = jnp.transpose(y, (1, 0, 2))
        sel = jnp.take_along_axis(y_tok, top_idx[:, :, None], axis=1)
        out = (weights[:, :, None] * sel).sum(axis=1)
        return out.reshape(B, S, D)
    xn = _layernorm(x, axis=-1)
    x = x + _L0_gnn_ref(xn, src, dst, L0_gnn_Wq, L0_gnn_Wk, L0_gnn_Wv, L0_gnn_ln_g, L0_gnn_ln_b, L0_gnn_W1, L0_gnn_b1, L0_gnn_alpha, L0_gnn_W2, L0_gnn_b2) + _L0_mix_ref(xn[None], L0_mix_Wqkv, L0_mix_bqkv, L0_mix_Wproj, L0_mix_bproj, L0_mix_temperature)[0]
    x = x + _L0_ffn_ref(_layernorm(x, axis=-1)[None], L0_ffn_Wr, L0_ffn_br, L0_ffn_ln_g, L0_ffn_ln_b, L0_ffn_W1, L0_ffn_b1, L0_ffn_W2, L0_ffn_b2)[0]
    return x

_drawn_inputs = setup_inputs


def setup_inputs(seed=0):
    import zlib

    import numpy as np

    out = dict(_drawn_inputs(seed))
    spreads = {'L0_gnn_ln_g': (1.0, 0.2),
     'L0_gnn_ln_b': (0.0, 0.1),
     'L0_gnn_b1': (0.0, 0.283),
     'L0_gnn_alpha': (0.25, 0.6),
     'L0_gnn_b2': (0.0, 0.1),
     'L0_mix_bqkv': (0.0, 0.308),
     'L0_mix_bproj': (0.0, 0.1),
     'L0_mix_temperature': (1.0, 0.6),
     'L0_ffn_br': (0.0, 0.1),
     'L0_ffn_ln_g': (1.0, 0.2),
     'L0_ffn_ln_b': (0.0, 0.315),
     'L0_ffn_b1': (0.0, 0.313),
     'L0_ffn_b2': (0.0, 0.1)}
    factors = {'L0_gnn_Wq': 3.249, 'L0_gnn_Wk': 3.223, 'L0_mix_Wqkv': 32.173}
    for name, (base, spread) in spreads.items():
        noise = np.random.default_rng([zlib.crc32(name.encode()), seed]).standard_normal(out[name].shape)
        drawn = base * np.exp(spread * noise) if base else spread * noise
        out[name] = jnp.asarray(drawn.astype(out[name].dtype))
    for name, factor in factors.items():
        out[name] = (out[name] * factor).astype(out[name].dtype)
    return out
```

```python
from contextlib import ExitStack

import numpy as np

import concourse.bass as bass
from concourse import mybir

F32 = mybir.dt.float32
BF16 = mybir.dt.bfloat16
I32 = mybir.dt.int32
ALU = mybir.AluOpType
ACT = mybir.ActivationFunctionType
AX = mybir.AxisListType
ds = bass.ds

N = 3125
F = 256
FC = F // 128
TP = 125
NT = N // TP
U = 5
HG = 4
DG = F // HG
HM = 8
DM = F // HM
NPAIR = DM * (DM - 1) // 2
PB = 124
NPB = NPAIR // PB
V1 = DM + 1
EDGES = 2 * 50000 + N
EJ = 4
GE = EJ * 128
N_GROUPS = -(-EDGES // GE)
G_PAD = 208
E_PAD = G_PAD * GE
ET_PAD = G_PAD * EJ
N_STEPS = N_GROUPS + NT - 1
KR = 4
CHUNKS = 32
CE = E_PAD // CHUNKS
NEX = 8
HID = 4 * F
HB = HID // 128
MT = 256
NMT = (2 * N + NEX * (MT - 1)) // MT
ROWS = NMT * MT
BIG = 1e30
EPS = 1e-5
SCALE = float(DM) ** 0.25
PAD_DST = 4000


class Shared:
    pass


class Order:

    def __init__(self, eng, sem, base=0):
        self.eng, self.sem, self.base, self.n = eng, sem, base, 0

    def __call__(self, ins):
        ins.then_inc(self.sem, 1)
        self.n += 1
        self.eng.wait_ge(self.sem, self.base + self.n)


def bcast(ap, *shape):
    return ap.broadcast_to(list(shape))


def over_tiles(eng, body, n=NT, unroll=U):
    rounds = n // unroll
    with eng.Fori(0, rounds - 1) as i:
        for j in range(unroll):
            body(i * unroll + j, j, i, False)
    for j in range(unroll):
        body((rounds - 1) * unroll + j, j, rounds - 1, j == unroll - 1)


def wait(eng, sem, value):
    if not isinstance(value, int) or value > 0:
        eng.wait_ge(sem, value)


def psum_turn(u, j):
    return u if j == 0 else u - 1


class Memory:

    def __init__(self, nc):
        self.nc, self.stack, self.held = nc, ExitStack(), []

    def __enter__(self):
        self.stack.__enter__()
        return self

    def __exit__(self, *e):
        self.stack.__exit__(*e)
        for sem in self.held:
            self.nc.gpsimd.sem_clear(sem)
            self.nc.release_semaphore(sem)

    def sb(self, name, shape, dt=F32):
        return self.stack.enter_context(self.nc.sbuf_tensor(name, list(shape), dt))

    def ps(self, name, shape, dt=F32):
        return self.stack.enter_context(self.nc.psum_tensor(name, list(shape), dt))

    def sem(self, name):
        self.held.append(self.nc.alloc_semaphore(name))
        return self.held[-1]

    def gather_sems(self, name, n):
        return [self.nc.alloc_semaphore(f"{name}{i}") for i in range(n)]

    def sems(self, name, n):
        return [self.sem(f"{name}{i}") for i in range(n)]

    def block(self):
        return self.stack.enter_context(self.nc.Block())


def finish_stats(dve, order, st, mean, var, tmp):
    m_even, m_odd, q_even, q_odd = (st[:, :, i] for i in (1, 4, 2, 5))
    order(dve.tensor_tensor(tmp[:, 0, :], m_even, m_odd, ALU.add))
    order(dve.tensor_scalar(mean[:, :], tmp[:, 0, :], 0.5, None, ALU.mult))
    order(dve.tensor_tensor(tmp[:, 1, :], m_even, m_odd, ALU.subtract))
    order(dve.tensor_tensor(tmp[:, 2, :], tmp[:, 1, :], tmp[:, 1, :], ALU.mult))
    order(dve.tensor_tensor(tmp[:, 3, :], q_even, q_odd, ALU.add))
    order(dve.tensor_scalar(tmp[:, 4, :], tmp[:, 3, :], 1.0 / F, EPS, ALU.mult, ALU.add))
    return dve.scalar_tensor_tensor(var[:, :], tmp[:, 2, :], 0.25, tmp[:, 4, :], ALU.mult, ALU.add)


def stage_project(nc, a, t):
    with Memory(nc) as m:
        wall = m.sb("wall", [128, FC, 6 * F])
        mix_bias = m.sb("mix_bias", [TP, 3 * F])
        mean, rstd = m.sb("mean", [TP, NT]), m.sb("rstd", [TP, NT])

        with Memory(nc) as s:
            wst = s.sb("wst", [128, 6, F])
            wpst = s.sb("wpst", [128, FC, F])
            edge_i = s.sb("edge_i", [G_PAD // 2, 2, 2, GE], I32)
            edge_f = s.sb("edge_f", [G_PAD // 2, 2, 2, GE])
            zeros = s.sb("zeros", [128, 4096])
            st, var = s.sb("st", [TP, NT, 6]), s.sb("var", [TP, NT])
            std, tmp = s.sb("std", [TP, NT]), s.sb("tmp", [TP, 5, NT])
            first_dst = s.sb("first_dst", [1, N_GROUPS])
            win_end = s.sb("win_end", [NT, 1])
            win_id = s.sb("win_id", [NT, 1])
            count = s.sb("count", [1, N_STEPS])
            before = s.sb("before", [NT, N_GROUPS])
            last_group = s.sb("last_group", [NT, 3])
            passed = s.sb("passed", [NT, N_STEPS])
            count_w = s.sb("count_w", [NT, N_STEPS])
            row = s.sb("row", [1, 3, N_STEPS])
            tp = [s.ps(f"tp{i}", [128, 512]) for i in range(4)]
            first_ps = s.ps("first_ps", [NT, N_GROUPS])
            step_ps = s.ps("step_ps", [1, N_STEPS])
            group_ps = s.ps("group_ps", [1, N_GROUPS])
            x_in, w_in, c_in, pad_in, zero_out = s.sem("x_in"), s.sem("w_in"), s.sem("c_in"), s.sem("pad_in"), s.sem("zero_out")
            edge_in = s.sem("edge_in")
            memsets, edge_float, turned, drained = s.sem("memsets"), s.sem("edge_float"), s.sem("turned"), s.sem("drained")
            stats_done = s.sem("stats_done0")
            dve_order, var_ready, std_ready = s.sem("dve_order"), s.sem("var_ready"), s.sem("std_ready")
            first_row, firsts, before_ready, passed_ready, steps_ready = (
                s.sem(x) for x in ("first_row", "firsts", "before_ready", "passed_ready", "steps_ready"))
            banks = []
            for kind in range(2):
                for half in range(2):
                    banks.append(("edge", kind, half))
            for k in range(FC):
                for third in range(2):
                    banks.append(("mix", k, third))
            for k in range(FC):
                banks.append(("proj", k, 0))
            block = s.block()

            @block.sync
            def _(sp):
                for kind, (pad, given) in enumerate(((t.dst_pad, a["dst"]), (t.src_pad, a["src"]))):
                    sp.dma_start(pad[1:1 + EDGES].rearrange("(p c) -> p c", p=TP),
                                 given.rearrange("(p c) -> p c", p=TP)).then_inc(pad_in, 16)
                    sp.dma_start(pad[0:1].rearrange("(p c) -> p c", p=1),
                                 a["c_head"][kind:kind + 1, :]).then_inc(pad_in, 16)
                    sp.dma_start(pad[1 + EDGES:].rearrange("(p c) -> p c", p=1),
                                 a["c_tail"][kind:kind + 1, :]).then_inc(pad_in, 16)
                sp.dma_start(t.x_all[:, :, :], a["x"].rearrange("(t p) f -> p t f", p=TP)).then_inc(x_in, 16)
                for name, ap in (("c_ident", t.ident), ("c_identb", t.identb), ("c_win_node", t.win_node),
                                 ("c_win_end", win_end), ("c_win_id", win_id), ("c_count", count)):
                    sp.dma_start(ap[:, :], a[name]).then_inc(c_in, 16)
                sp.dma_start(count_w[:, :], a["c_count"][0, :].partition_broadcast(NT)).then_inc(c_in, 16)
                sp.dma_start(t.iota_n[:, :], a["c_iota"][0, :].partition_broadcast(128)).then_inc(c_in, 16)
                sp.wait_ge(pad_in, 6 * 16)
                for kind, pad in enumerate((t.dst_pad, t.src_pad)):
                    sp.dma_start(edge_i[:, kind, :, :],
                                 pad[1:1 + E_PAD].rearrange("(h g c) -> g h c", h=2, c=GE)).then_inc(edge_in, 16)
                sp.wait_ge(memsets, 2)
                for i in range(ROWS * F // (128 * 4096)):
                    sp.dma_start(t.x_rows.rearrange("(i p r) f -> i p (r f)", p=128, r=4096 // F)[i],
                                 zeros[:, :]).then_inc(zero_out, 16)
                sp.wait_ge(zero_out, ROWS * F // (128 * 4096) * 16)

            @block.gpsimd
            def _(pool):
                pool.memset(t.ones[:, :], 1.0).then_inc(memsets, 1)
                pool.memset(zeros[:, :], 0.0).then_inc(memsets, 1)

            @block.scalar
            def _(act):
                act.dma_start(wst[:, :, :], a["L0_mix_Wqkv"].rearrange("(o p) f -> p o f", p=128)).then_inc(w_in, 16)
                act.dma_start(wpst[:, :, :], a["L0_mix_Wproj"].rearrange("(o p) f -> p o f", p=128)).then_inc(w_in, 16)
                for i, name in enumerate(("L0_gnn_Wq", "L0_gnn_Wk", "L0_gnn_Wv")):
                    act.dma_start(wall[:, :, i * F:(i + 1) * F],
                                  a[name].rearrange("(k p) n -> p k n", p=128)).then_inc(w_in, 16)
                act.dma_start(mix_bias[:, :], a["L0_mix_bqkv"].partition_broadcast(TP)).then_inc(w_in, 16)
                act.wait_ge(var_ready, 1)
                act.activation(std[:, :], var[:, :], ACT.Sqrt).then_inc(std_ready, 1)
                act.wait_ge(w_in, 6 * 16)

            @block.tensor
            def _(pe):
                pe.wait_ge(c_in, 8 * 16)
                for i, (what, b, c) in enumerate(banks):
                    if i >= 4:
                        pe.wait_ge(drained, i - 3)
                    if what == "edge":
                        pe.wait_ge(edge_float, 1 + b)
                        for j in range(EJ):
                            last = pe.transpose(tp[i % 4][:, j * 104:(j + 1) * 104],
                                                edge_f[:, b, c, j * 128:(j + 1) * 128], t.ident[0:104, 0:104])
                    elif what == "mix":
                        pe.wait_ge(w_in, 6 * 16)
                        for j in range(3):
                            last = pe.transpose(tp[i % 4][:, j * 128:(j + 1) * 128],
                                                wst[:, 3 * c + j, b * 128:(b + 1) * 128], t.ident[:, :])
                    else:
                        for j in range(2):
                            last = pe.transpose(tp[i % 4][:, j * 128:(j + 1) * 128],
                                                wpst[:, j, b * 128:(b + 1) * 128], t.ident[:, :])
                    last.then_inc(turned, 1)
                pe.wait_ge(memsets, 1)
                pe.wait_ge(first_row, 1)
                pe.matmul(first_ps[:, :], t.ones[0:1, 0:NT], first_dst[:, :], start=True, stop=True).then_inc(firsts, 1)
                pe.wait_ge(before_ready, 1)
                pe.matmul(group_ps[:, :], t.ones[0:NT, 0:1], before[:, :], start=True, stop=True)
                pe.wait_ge(passed_ready, 1)
                pe.matmul(step_ps[:, :], t.ones[0:NT, 0:1], passed[:, :], start=True, stop=True).then_inc(steps_ready, 1)

            @block.vector
            def _(dve):
                order = Order(dve, dve_order)
                dve.wait_ge(edge_in, 32)
                for kind in range(2):
                    dve.tensor_copy(edge_f[:, kind, :, :], edge_i[:, kind, :, :]).then_inc(edge_float, 1)
                dve.wait_ge(x_in, 16)
                with dve.Fori(0, NT) as u:
                    dve.bn_stats(st[:, u, :], t.x_all[:, u, :]).then_inc(stats_done, 1)
                for i, (what, b, c) in enumerate(banks):
                    dve.wait_ge(turned, i + 1)
                    if what == "edge":
                        to = (t.dst_all, t.src_all)[b][:, c * 104:(c + 1) * 104, :]
                        src = tp[i % 4][:, 0:EJ * 104].rearrange("p (j g) -> p g j", j=EJ)
                    elif what == "mix":
                        at = 3 * F + 3 * c * 128
                        to, src = wall[:, b, at:at + 384], tp[i % 4][:, 0:384]
                    else:
                        to, src = t.wproj[:, b, :], tp[i % 4][:, 0:F]
                    dve.tensor_copy(to, src).then_inc(drained, 1)
                dve.wait_ge(drained, len(banks))
                dve.wait_ge(stats_done, NT)
                finish_stats(dve, order, st, mean, var, tmp).then_inc(var_ready, 1)
                dve.tensor_copy(first_dst[:, :], t.dst_all[0:1, 0:N_GROUPS, 0]).then_inc(first_row, 1)
                dve.wait_ge(firsts, 1)
                order(dve.tensor_scalar(before[:, :], first_ps[:, :], win_end[:, :], None, ALU.is_lt))
                dve.sem_inc(before_ready, 1)
                order(dve.tensor_reduce(last_group[:, 0:1], before[:, :], AX.X, ALU.add))
                order(dve.tensor_scalar(last_group[:, 1:2], last_group[:, 0:1], -1.0, 0.0, ALU.add, ALU.max))
                order(dve.tensor_tensor(last_group[:, 2:3], last_group[:, 1:2], win_id[:, :], ALU.add))
                order(dve.tensor_scalar(passed[:, :], count_w[:, :], last_group[:, 2:3], None, ALU.is_gt))
                dve.sem_inc(passed_ready, 1)
                dve.wait_ge(steps_ready, 1)
                order(dve.tensor_copy(row[:, 0, :], step_ps[:, :]))
                order(dve.tensor_tensor(row[:, 1, :], count[:, :], row[:, 0, :], ALU.subtract))
                order(dve.tensor_copy(t.step_w[:, :], row[:, 0, :]))
                order(dve.tensor_copy(t.step_g[:, :], row[:, 1, :]))
                order(dve.tensor_scalar(t.step_slot[:, :], t.step_g[:, :], KR - 1, None, ALU.bitwise_and))
                order(dve.tensor_scalar(row[:, 2, 0:N_GROUPS], group_ps[:, :], -1.0, float(NT + 1),
                                        ALU.mult, ALU.add))
                order(dve.tensor_tensor(row[:, 2, 0:N_GROUPS], row[:, 2, 0:N_GROUPS], count[:, 0:N_GROUPS], ALU.add))
                order(dve.memset(t.need_steps[:, 0:KR], 0))
                order(dve.tensor_copy(t.need_steps[:, KR:], row[:, 2, 1:N_GROUPS - KR + 1]))
                dve.wait_ge(std_ready, 1)
                order(dve.reciprocal(rstd[:, :], std[:, :]))

        with Memory(nc) as s:
            xn_t = [s.sb(f"xn_t{j}", [TP, F]) for j in range(U)]
            xnT = [s.sb(f"xnT{j}", [128, FC, TP]) for j in range(U)]
            kv_t = [s.sb(f"kv_t{j}", [TP, 2 * F]) for j in range(U)]
            mix_t = [s.sb(f"mix_t{j}", [TP, 3 * F]) for j in range(U)]
            q3_t = [s.sb(f"q3_t{j}", [TP, 3, F], BF16) for j in range(U)]
            rest = [s.sb(f"rest{j}", [TP, F]) for j in range(U)]
            turn_ps = [s.ps(f"turn_ps{i}", [128, FC, TP]) for i in range(2)]
            proj_ps = [s.ps(f"proj_ps{i}", [128, 6 * F]) for i in range(2)]
            xn_ready, turned, xnT_ready, proj_ready = (
                s.sem(x) for x in ("xn_ready", "turned", "xnT_ready", "proj_ready"))
            kv_ready, hi_ready, rest_ready, mid_ready, q3_ready, mix_ready = (
                s.sem(x) for x in ("kv_ready", "hi_ready", "rest_ready", "mid_ready", "q3_ready", "mix_ready"))
            xn_out, kv_out, q3_out, mix_out = (s.sems(x, U) for x in ("xn_out", "kv_out", "q3_out", "mix_out"))
            block = s.block()

            @block.sync
            def _(sp):
                def body(u, j, i, last):
                    sp.wait_ge(xn_ready, u + 1)
                    sp.dma_start(t.xn_all[:, u, :], xn_t[j][:, :]).then_inc(xn_out[j], 16)
                    sp.wait_ge(kv_ready, u + 1)
                    sp.dma_start(t.k_tab[ds(u * TP, TP), :], kv_t[j][:, 0:F]).then_inc(kv_out[j], 16)
                    sp.dma_start(t.v_tab[ds(u * TP, TP), :], kv_t[j][:, F:2 * F]).then_inc(kv_out[j], 16)
                    sp.wait_ge(mix_ready, u + 1)
                    sp.dma_start(t.mix_qkv[ds(u * TP, TP), :], mix_t[j][:, :]).then_inc(mix_out[j], 16)
                    sp.wait_ge(q3_ready, u + 1)
                    sp.dma_start(t.q3[:, u, :], q3_t[j][:, :, :].rearrange("p a f -> p (a f)")).then_inc(q3_out[j], 16)
                over_tiles(sp, body)
                for j in range(U):
                    for s_, per in ((xn_out, 16), (kv_out, 32), (q3_out, 16), (mix_out, 16)):
                        sp.wait_ge(s_[j], per * (NT // U))

            @block.vector
            def _(dve):
                def normalise(u, j, i):
                    wait(dve, xn_out[j], i * 16)
                    dve.tensor_scalar(xn_t[j][:, :], t.x_all[:, u, :], mean[:, ds(u, 1)], rstd[:, ds(u, 1)],
                                      ALU.subtract, ALU.mult).then_inc(xn_ready, 1)

                def body(u, j, i, last):
                    if not last:
                        normalise(u + 1, (j + 1) % U, i + (j + 1) // U)
                    dve.wait_ge(hi_ready, u + 1)
                    dve.tensor_tensor(rest[j][:, :], proj_ps[j % 2][0:TP, 0:F], q3_t[j][:, 0, :],
                                      ALU.subtract).then_inc(rest_ready, 1)
                    wait(dve, mix_out[j], i * 16)
                    dve.tensor_tensor(mix_t[j][:, :], proj_ps[j % 2][0:TP, 3 * F:6 * F], mix_bias[:, :],
                                      ALU.add).then_inc(mix_ready, 1)
                    dve.wait_ge(mid_ready, u + 1)
                    dve.tensor_tensor(q3_t[j][:, 2, :], rest[j][:, :], q3_t[j][:, 1, :],
                                      ALU.subtract).then_inc(q3_ready, 1)
                normalise(0, 0, 0)
                over_tiles(dve, body)

            @block.scalar
            def _(act):
                def turn_out(u, j):
                    act.wait_ge(turned, u + 1)
                    act.activation(xnT[j][:, :, :], turn_ps[j % 2][:, :, :], ACT.Copy).then_inc(xnT_ready, 1)

                def body(u, j, i, last):
                    if not last:
                        turn_out(u + 1, (j + 1) % U)
                    wait(act, kv_out[j], i * 32)
                    act.wait_ge(proj_ready, u + 1)
                    act.activation(kv_t[j][:, :], proj_ps[j % 2][0:TP, F:3 * F], ACT.Copy).then_inc(kv_ready, 1)
                    wait(act, q3_out[j], i * 16)
                    act.activation(q3_t[j][:, 0, :], proj_ps[j % 2][0:TP, 0:F], ACT.Copy).then_inc(hi_ready, 1)
                    act.wait_ge(rest_ready, u + 1)
                    act.activation(q3_t[j][:, 1, :], rest[j][:, :], ACT.Copy).then_inc(mid_ready, 1)
                turn_out(0, 0)
                over_tiles(act, body)

            @block.tensor
            def _(pe):
                def turn(u, j):
                    pe.wait_ge(xn_ready, u + 1)
                    wait(pe, xnT_ready, psum_turn(u, j))
                    for k in range(FC):
                        last = pe.transpose(turn_ps[j % 2][:, k, :], xn_t[j][:, k * 128:(k + 1) * 128],
                                            t.ident[0:TP, 0:TP])
                    last.then_inc(turned, 1)

                def body(u, j, i, last):
                    if not last:
                        turn(u + 1, (j + 1) % U)
                    pe.wait_ge(xnT_ready, u + 1)
                    wait(pe, mix_ready, psum_turn(u, j))
                    for k in range(FC):
                        for b in range(3):
                            mm = pe.matmul(proj_ps[j % 2][0:TP, b * 512:(b + 1) * 512], xnT[j][:, k, :],
                                           wall[:, k, b * 512:(b + 1) * 512], start=(k == 0), stop=(k == FC - 1))
                    mm.then_inc(proj_ready, 1)
                turn(0, 0)
                over_tiles(pe, body)


def gather_programs(block, s, t, table, ring, idx, idx_ready, idx_free, landed_slot, landed, steps_done):
    @block.scalar
    def _(act):
        act.sem_inc(idx_free, KR)

        def stage(g, slot):
            act.wait_ge(idx_free, g + 2)
            act.sem_inc(s.carrier, 1)
            act.activation(idx[slot][:, :], t.src_all[:, g, :], ACT.Copy).then_inc(idx_ready, 1)
        with act.Fori(0, N_GROUPS // KR) as i:
            for slot in range(KR):
                stage(i * KR + slot, slot)
        for g in range(N_GROUPS // KR * KR, N_GROUPS):
            stage(g, g % KR)

    @block.gpsimd
    def _(pool):
        def fetch(g, slot, i):
            need = pool.value_load(t.need_steps[0:1, ds(g, 1)], min_val=0, max_val=N_STEPS)
            pool.wait_ge(idx_ready, g + 1)
            pool.wait_ge(steps_done, need)
            pool.sem_inc(s.carrier, 1)
            for j in range(EJ):
                pool.indirect_dma_start(out=ring[:, slot, j, :], out_offset=None, in_=table,
                                        in_offset=bass.IndirectOffsetOnAxis(ap=idx[slot][:, j:j + 1], axis=0)
                                        ).then_inc(landed_slot[slot], 16)
            former = (slot - 1) % KR
            wait(pool, landed_slot[former], (i if slot == 0 else i + 1) * 16 * EJ)
            pool.sem_inc(landed, 1)
            pool.sem_inc(idx_free, 1)

        with pool.Fori(0, N_GROUPS // KR) as i:
            for slot in range(KR):
                fetch(i * KR + slot, slot, i)
        for g in range(N_GROUPS // KR * KR, N_GROUPS):
            fetch(g, g % KR, g // KR)
        end = N_GROUPS - 1
        pool.wait_ge(landed_slot[end % KR], (end // KR + 1) * 16 * EJ)
        pool.sem_inc(landed, 1)
        pool.wait_ge(steps_done, N_STEPS + 1)


def over_steps(eng, body):
    with eng.Fori(0, N_STEPS // 2 - 1) as i:
        for par in range(2):
            body(i * 2 + par, par, i, False)
    for par in range(2):
        body(N_STEPS - 2 + par, par, N_STEPS // 2 - 1, par == 1)


def load_step(eng, table, s, most):
    return eng.value_load(table[0:1, ds(s, 1)], min_val=0, max_val=most)


def stage_scores(nc, a, t):
    with Memory(nc) as s:
        ring = s.sb("k_ring", [128, KR, EJ, F])
        idx = [s.sb(f"k_idx{i}", [128, EJ], I32) for i in range(KR)]
        dst_row = [s.sb(f"dst_row{i}", [TP, GE], I32) for i in range(2)]
        spread = [s.sb(f"spread{i}", [TP, GE], BF16) for i in range(2)]
        prod = s.sb("prod", [128, EJ * F])
        score = s.sb("score", [128, EJ, HG])
        q_ps = [s.ps(f"q_ps{i}", [128, EJ * F]) for i in range(2)]
        s.carrier = s.sem("k_carrier")
        idx_ready, idx_free, landed, steps_done = (s.sem(x) for x in ("k_idx_ready", "k_idx_free", "k_landed", "k_steps_done"))
        landed_slot = s.gather_sems("k_landed_slot", KR)
        row_in = s.sems("dst_row_in", 2)
        spread_ready, q_ready, dve_order = s.sem("spread_ready"), s.sem("q_ready"), s.sem("k_dve_order")
        block = s.block()
        gather_programs(block, s, t, t.k_tab, ring, idx, idx_ready, idx_free, landed_slot, landed, steps_done)

        @block.sync
        def _(sp):
            def body(n, par, i, last):
                g = load_step(sp, t.step_g, n, N_GROUPS - 1)
                sp.wait_ge(spread_ready, n)
                sp.dma_start(dst_row[par][:, :], t.dst_pad[ds(g * GE + 1, GE)].partition_broadcast(TP)
                             ).then_inc(row_in[par], 16)
            over_steps(sp, body)

        @block.tensor
        def _(pe):
            def body(n, par, i, last):
                w = load_step(pe, t.step_w, n, NT - 1)
                pe.wait_ge(spread_ready, n + 2)
                pe.wait_ge(steps_done, n)
                for j in range(EJ):
                    for part in range(3):
                        mm = pe.matmul(q_ps[par][:, j * F:(j + 1) * F], spread[par][:, j * 128:(j + 1) * 128],
                                       t.q3[:, w, part * F:(part + 1) * F], start=(part == 0), stop=(part == 2))
                mm.then_inc(q_ready, 1)
            over_steps(pe, body)

        @block.vector
        def _(dve):
            def spread_rows(n, par, i):
                w = load_step(dve, t.step_w, n, NT - 1)
                dve.wait_ge(row_in[par], i * 16 + 16)
                dve.tensor_scalar(spread[par][:, :], dst_row[par][:, :], t.win_node[:, ds(w, 1)], None,
                                  ALU.is_equal).then_inc(spread_ready, 1)

            def body(n, par, i, last):
                if not last:
                    spread_rows(n + 1, 1 - par, i + par)
                g = load_step(dve, t.step_g, n, N_GROUPS - 1)
                slot = load_step(dve, t.step_slot, n, KR - 1)
                order = Order(dve, dve_order, n * 2 + 1)
                dve.wait_ge(q_ready, n + 1)
                dve.wait_ge(landed, g + 2)
                dve.tensor_tensor(prod[:, :], ring[:, slot, :, :].rearrange("p j f -> p (j f)"), q_ps[par][:, :],
                                  ALU.mult).then_inc(steps_done, 1)
                dve.wait_ge(steps_done, n + 2)
                order(dve.tensor_reduce(score[:, :, :], prod[:, :].rearrange("p (j h d) -> p j h d", j=EJ, h=HG),
                                        AX.X, ALU.add))
                at = t.e_all[:, :, ds(g * EJ, EJ)]
                order(dve.tensor_tensor(at, at, score[:, :, :].rearrange("p j h -> p h j"), ALU.add))
            dve.sem_inc(steps_done, 1)
            dve.sem_inc(spread_ready, 1)
            dve.memset(t.e_all[:, :, :], 0.0).then_inc(dve_order, 1)
            dve.wait_ge(dve_order, 1)
            spread_rows(0, 0, 0)
            over_steps(dve, body)



def stage_edge_softmax(nc, a, t):
    NB = HG * ET_PAD // 104
    NR = NB // 4
    with Memory(nc) as s:
        eT = s.sb("eT", [104, NB, 128])
        dst = s.sb("es_dst", [128, CE + 2], I32)
        pen = s.sb("pen", [128, CE + 1])
        e = s.sb("es_e", [128, CE])
        fwd, bwd = s.sb("es_fwd", [128, CE]), s.sb("es_bwd", [128, CE])
        ends = s.sb("ends", [128, 6])
        rows = s.sb("es_rows", [1, 4, 128])
        carry = s.sb("carry", [1, 2, 129])
        start = s.sb("es_start", [128, 2])
        tp = [s.ps(f"es_tp{i}", [128, 512]) for i in range(4)]
        row_ps, start_ps = s.ps("row_ps", [1, 4, 128]), s.ps("start_ps", [128, 2])
        turned, drained, e_out, e_in, dst_in = (s.sem(x) for x in ("es_turned", "es_drained", "e_out", "e_in", "es_dst_in"))
        dve_order, ends_ready, rows_ready, carry_ready, start_ready = (
            s.sem(x) for x in ("es_order", "ends_ready", "es_rows_ready", "carry_ready", "es_start_ready"))
        less_max, exp_ready, ex_out, ex_in = (s.sem(x) for x in ("less_max", "exp_ready", "ex_out", "ex_in"))
        block = s.block()

        @block.sync
        def _(sp):
            for h in range(HG):
                at = slice(h * CHUNKS, (h + 1) * CHUNKS)
                for first, col, width in ((1, 1, CE), (0, 0, 1), (CE + 1, CE + 1, 1)):
                    src = t.dst_pad[0:E_PAD] if first == 0 else t.dst_pad[1:1 + E_PAD] if first == 1 else t.dst_pad[2:2 + E_PAD]
                    src = src.rearrange("(k c) -> k c", c=CE)
                    src = src if first == 1 else src[:, 0:1] if first == 0 else src[:, CE - 1:CE]
                    sp.dma_start(dst[at, col:col + width], src, allow_slow_non_contiguous=True).then_inc(dst_in, 16)
            sp.wait_ge(drained, NR)
            sp.dma_start(t.e_dram.rearrange("h (b t p) -> t (h b) p", t=104, p=128), eT[:, :, :]).then_inc(e_out, 16)
            sp.wait_ge(e_out, 16)
            sp.dma_start(e[:, :], t.e_dram.rearrange("h (k c) -> (h k) c", c=CE)).then_inc(e_in, 16)
            sp.wait_ge(exp_ready, 1)
            sp.dma_start(t.ex_dram.rearrange("h (k c) -> (h k) c", c=CE), fwd[:, :]).then_inc(ex_out, 16)
            sp.wait_ge(ex_out, 16)
            sp.dma_start(eT[:, :, :], t.ex_dram.rearrange("h (b t p) -> t (h b) p", t=104, p=128)).then_inc(ex_in, 16)

        @block.tensor
        def _(pe):
            for r in range(NR):
                if r >= 4:
                    pe.wait_ge(drained, r - 3)
                for i in range(4):
                    b = 4 * r + i
                    mm = pe.transpose(tp[r % 4][0:104, i * 128:(i + 1) * 128], t.e_flat[:, b * 104:(b + 1) * 104], t.ident[:, :])
                mm.then_inc(turned, 1)
            pe.wait_ge(ends_ready, 1)
            for i in range(4):
                mm = pe.transpose(row_ps[:, i, :], ends[:, i:i + 1], t.ident[:, :])
            mm.then_inc(rows_ready, 1)
            pe.wait_ge(carry_ready, 1)
            pe.transpose(start_ps[:, 0:1], carry[:, 0, 0:128], t.ident[0:1, 0:1])
            pe.transpose(start_ps[:, 1:2], carry[:, 1, 1:129], t.ident[0:1, 0:1]).then_inc(start_ready, 1)
            pe.wait_ge(ex_in, 16)
            for r in range(NR):
                pe.wait_ge(drained, NR + r - 3)
                for i in range(4):
                    mm = pe.transpose(tp[r % 4][:, i * 104:(i + 1) * 104], eT[:, 4 * r + i, :], t.ident[0:104, 0:104])
                mm.then_inc(turned, 1)

        @block.scalar
        def _(act):
            act.preload_act_table(ACT.Exp)
            for r in range(NR):
                act.wait_ge(turned, r + 1)
                act.activation(eT[:, 4 * r:4 * r + 4, :], tp[r % 4][0:104, :].rearrange("t (b p) -> t b p", b=4),
                               ACT.Copy).then_inc(drained, 1)
            act.wait_ge(less_max, 1)
            act.activation(fwd[:, :], bwd[:, :], ACT.Exp, scale=1.0 / float(F) ** 0.5).then_inc(exp_ready, 1)
            for r in range(NR):
                act.wait_ge(turned, NR + r + 1)
                act.activation(t.e_flat[:, 4 * r * 104:(4 * r + 4) * 104], tp[r % 4][:, 0:416], ACT.Copy).then_inc(drained, 1)

        @block.vector
        def _(dve):
            order = Order(dve, dve_order)
            dve.wait_ge(dst_in, 3 * HG * 16)
            order(dve.tensor_tensor(pen[:, :], dst[:, 1:CE + 2], dst[:, 0:CE + 1], ALU.is_equal))
            order(dve.tensor_scalar(pen[:, :], pen[:, :], -1.0, BIG, ALU.add, ALU.mult))
            order(dve.tensor_tensor(ends[:, 4:5], dst[:, 1:2], dst[:, CE:CE + 1], ALU.is_equal))
            order(dve.tensor_scalar(ends[:, 5:6], ends[:, 4:5], -1.0, BIG, ALU.add, ALU.mult))
            order(dve.tensor_tensor(ends[:, 2:3], ends[:, 5:6], pen[:, 0:1], ALU.add))
            order(dve.tensor_tensor(ends[:, 3:4], ends[:, 5:6], pen[:, CE:CE + 1], ALU.add))
            order(dve.memset(carry[:, :, :], -BIG))
            dve.wait_ge(e_in, 16)
            scan = dve.tensor_tensor_scan
            order(scan(fwd[:, :], pen[:, 0:CE], e[:, :], -BIG, ALU.add, ALU.max))
            order(scan(bwd[:, ::-1], pen[:, CE:0:-1], e[:, ::-1], -BIG, ALU.add, ALU.max))
            order(dve.tensor_copy(ends[:, 0:1], fwd[:, CE - 1:CE]))
            order(dve.tensor_copy(ends[:, 1:2], bwd[:, 0:1]))
            dve.sem_inc(ends_ready, 1)
            dve.wait_ge(rows_ready, 1)
            order(dve.tensor_copy(rows[:, :, :], row_ps[:, :, :]))
            order(scan(carry[:, 0, 1:129], rows[:, 2, :], rows[:, 0, :], -BIG, ALU.add, ALU.max))
            order(scan(carry[:, 1, 127::-1], rows[:, 3, ::-1], rows[:, 1, ::-1], -BIG, ALU.add, ALU.max))
            dve.sem_inc(carry_ready, 1)
            dve.wait_ge(start_ready, 1)
            order(dve.tensor_copy(start[:, :], start_ps[:, :]))
            order(scan(fwd[:, :], pen[:, 0:CE], e[:, :], start[:, 0:1], ALU.add, ALU.max))
            order(scan(bwd[:, ::-1], pen[:, CE:0:-1], e[:, ::-1], start[:, 1:2], ALU.add, ALU.max))
            order(dve.tensor_tensor(fwd[:, :], fwd[:, :], bwd[:, :], ALU.max))
            dve.tensor_tensor(bwd[:, :], e[:, :], fwd[:, :], ALU.subtract).then_inc(less_max, 1)


def stage_aggregate(nc, a, t):
    FD = F + HG
    with Memory(nc) as s:
        ring = s.sb("v_ring", [128, KR, EJ, F])
        idx = [s.sb(f"v_idx{i}", [128, EJ], I32) for i in range(KR)]
        hot = [s.sb(f"hot{i}", [128, EJ, TP]) for i in range(2)]
        val = [s.sb(f"val{i}", [128, EJ, FD]) for i in range(2)]
        sum_ps = [s.ps(f"sum_ps{i}", [TP, FD]) for i in range(2)]
        s.carrier = s.sem("v_carrier")
        idx_ready, idx_free, landed = (s.sem(x) for x in ("v_idx_ready", "v_idx_free", "v_landed"))
        landed_slot = s.gather_sems("v_landed_slot", KR)
        val_ready, sum_ready, sum_read, cleared = s.sem("val_ready"), s.sem("sum_ready"), s.sem("sum_read"), s.sem("cleared")
        block = s.block()
        gather_programs(block, s, t, t.v_tab, ring, idx, idx_ready, idx_free, landed_slot, landed, val_ready)

        @block.tensor
        def _(pe):
            def body(n, par, i, last):
                pe.wait_ge(val_ready, n + 2)
                pe.wait_ge(sum_read, n)
                for j in range(EJ):
                    mm = pe.matmul(sum_ps[par][:, :], hot[par][:, j, :], val[par][:, j, :], start=(j == 0), stop=(j == EJ - 1))
                mm.then_inc(sum_ready, 1)
            over_steps(pe, body)

        @block.vector
        def _(dve):
            def weigh(n, par):
                w = load_step(dve, t.step_w, n, NT - 1)
                g = load_step(dve, t.step_g, n, N_GROUPS - 1)
                slot = load_step(dve, t.step_slot, n, KR - 1)
                ex = t.e_all[:, :, ds(g * EJ, EJ)].rearrange("p h j -> p j h")
                dve.tensor_tensor(hot[par][:, :, :], bcast(t.iota_n[:, ds(w * TP, TP)].unsqueeze(1), 128, EJ, TP),
                                  bcast(t.dst_all[:, g, :].unsqueeze(2), 128, EJ, TP), ALU.is_equal)
                dve.tensor_scalar(val[par][:, :, F:FD], ex, 1.0, None, ALU.mult)
                dve.wait_ge(landed, g + 2)
                dve.tensor_tensor(val[par][:, :, 0:F].rearrange("p j (h d) -> p j h d", h=HG),
                                  ring[:, slot, :, :].rearrange("p j (h d) -> p j h d", h=HG),
                                  bcast(ex.unsqueeze(3), 128, EJ, HG, DG), ALU.mult).then_inc(val_ready, 1)

            def add_up(n, par):
                w = load_step(dve, t.step_w, n, NT - 1)
                dve.wait_ge(sum_ready, n + 1)
                dve.wait_ge(sum_read, n + 1)
                at = t.acc[:, w, :]
                dve.tensor_tensor(at, at, sum_ps[par][:, :], ALU.add).then_inc(sum_read, 1)

            def body(n, par, i, last):
                if not last:
                    weigh(n + 1, 1 - par)
                add_up(n, par)
            dve.memset(t.acc[:, :, :], 0.0).then_inc(cleared, 1)
            dve.wait_ge(cleared, 1)
            dve.sem_inc(sum_read, 1)
            dve.sem_inc(val_ready, 1)
            weigh(0, 0)
            over_steps(dve, body)


class Unit:

    def __init__(self, s, name, loaded, src, grow, factor):
        self.loaded, self.src, self.grow, self.factor = loaded, src, grow, factor
        self.sq = [s.sb(f"{name}_sq{j}", [TP, F]) for j in range(U)]
        self.nrm = [s.sb(f"{name}_nrm{j}", [TP, 5, HM]) for j in range(U)]
        self.unit = [s.sb(f"{name}_unit{j}", [TP, F]) for j in range(U)]
        self.rest = [s.sb(f"{name}_rest{j}", [TP, F]) for j in range(U)]
        self.parts = [s.sb(f"{name}_parts{j}", [TP, HM, 3, DM], BF16) for j in range(U)]
        self.turned_parts = [s.sb(f"{name}_T{j}", [3 * DM, HM, 128], BF16) for j in range(U)]
        self.turn_ps = s.ps(f"{name}_turn_ps", [3 * DM, HM, 128], BF16)
        (self.order, self.squared, self.rooted, self.scaled, self.rounded, self.rest_ready, self.middle, self.split,
         self.turned, self.ready) = (s.sem(f"{name}_{x}") for x in (
             "order", "squared", "rooted", "scaled", "rounded", "rest_ready", "middle", "split", "turned", "ready"))

    def heads(self, ap):
        return ap.rearrange("p (h d) -> p h d", h=HM)

    def dve_squares(self, dve, u, j, i):
        order = Order(dve, self.order, u * 4)
        dve.wait_ge(self.loaded[j], i * 16 + 16)
        order(dve.tensor_tensor(self.sq[j][:, :], self.src(j), self.src(j), ALU.mult))
        order(dve.tensor_reduce(self.nrm[j][:, 0, :], self.heads(self.sq[j][:, :]), AX.X, ALU.add))
        dve.tensor_scalar(self.nrm[j][:, 1, :], self.nrm[j][:, 0, :], self.grow, 1e-24, ALU.mult, ALU.max
                          ).then_inc(self.squared, 1)

    def act_root(self, act, u, j):
        act.wait_ge(self.squared, u + 1)
        act.activation(self.nrm[j][:, 2, :], self.nrm[j][:, 1, :], ACT.Sqrt).then_inc(self.rooted, 1)

    def dve_scale(self, dve, u, j):
        order = Order(dve, self.order, u * 4 + 2)
        dve.wait_ge(self.rooted, u + 1)
        order(dve.reciprocal(self.nrm[j][:, 3, :], self.nrm[j][:, 2, :]))
        order(dve.tensor_tensor(self.nrm[j][:, 4, :], self.nrm[j][:, 3, :], self.factor, ALU.mult))
        dve.tensor_tensor(self.heads(self.unit[j][:, :]), self.heads(self.src(j)),
                          bcast(self.nrm[j][:, 4, :].unsqueeze(2), TP, HM, DM), ALU.mult).then_inc(self.scaled, 1)

    def act_round(self, act, u, j):
        act.wait_ge(self.scaled, u + 1)
        act.activation(self.parts[j][:, :, 0, :], self.heads(self.unit[j][:, :]), ACT.Copy).then_inc(self.rounded, 1)

    def dve_rest(self, dve, u, j):
        dve.wait_ge(self.rounded, u + 1 + U)
        dve.tensor_tensor(self.heads(self.rest[j][:, :]), self.heads(self.unit[j][:, :]), self.parts[j][:, :, 0, :],
                          ALU.subtract).then_inc(self.rest_ready, 1)

    def act_middle(self, act, u, j):
        act.wait_ge(self.rest_ready, u + 1)
        act.activation(self.parts[j][:, :, 1, :], self.heads(self.rest[j][:, :]), ACT.Copy).then_inc(self.middle, 1)

    def dve_last(self, dve, u, j):
        dve.wait_ge(self.middle, u + 1)
        dve.tensor_tensor(self.parts[j][:, :, 2, :], self.heads(self.rest[j][:, :]), self.parts[j][:, :, 1, :],
                          ALU.subtract).then_inc(self.split, 1)

    def pe_turn(self, pe, u, j, identb):
        pe.wait_ge(self.split, u + 1)
        wait(pe, self.ready, u)
        for h in range(HM):
            mm = pe.transpose(self.turn_ps[:, h, 0:TP], self.parts[j][:, h, :, :].rearrange("p a d -> p (a d)"),
                              identb[0:TP, 0:TP])
        return mm

    def act_turn_out(self, act, u, j):
        act.wait_ge(self.turned, u + 1)
        act.activation(self.turned_parts[j][:, :, 0:TP], self.turn_ps[:, :, 0:TP], ACT.Copy).then_inc(self.ready, 1)


def stage_mix(nc, a, t):
    W = HM * V1
    HW = W // 2
    with Memory(nc) as m:
        pair3 = m.sb("pair3", [3 * DM, NPAIR], BF16)
        pair4 = m.sb("pair4", [128, NPAIR])
        pairT = m.sb("pairT", [PB, NPB, DM])
        g_acc = m.sb("g_acc", [PB, HM, NPB, V1])
        slv_acc = m.sb("slv_acc", [128, 3, 2, HW])
        coef = m.sb("coef", [128, 2, 2, HW])
        k_factor, q_factor = m.sb("k_factor", [TP, HM]), m.sb("q_factor", [TP, HM])
        proj_bias = m.sb("proj_bias", [TP, F])

        with Memory(nc) as s:
            kv = [s.sb(f"kv{j}", [TP, 2 * F]) for j in range(U)]
            ksq = [s.sb(f"ksq{j}", [TP, F]) for j in range(U)]
            v1 = [s.sb(f"v1{j}", [TP, HM, V1]) for j in range(U)]
            phi = [s.sb(f"phi{i}", [TP, NPAIR]) for i in range(2)]
            f_ps = [s.ps(f"kf_ps{i}", [TP, NPAIR]) for i in range(2)]
            g_ps = [s.ps(f"g_ps{i}", [PB, NPB, V1]) for i in range(2)]
            slv_ps = [s.ps(f"slv_ps{i}", [128, 2, HW]) for i in range(3)]
            c_in, kv_in = s.sem("mixc_in"), s.sems("mkv_in", U)
            ksq_ready, v1_ready, f_ready, phi_ready, g_ready, g_read, slv_ready, slv_read, cleared = (
                s.sem("k_" + x) for x in ("sq", "v1", "f", "phi", "g", "g_read", "slv", "slv_read", "cleared"))
            k = Unit(s, "mk", kv_in, lambda j: kv[j][:, 0:F], 1.0, k_factor[:, :])
            block = s.block()

            @block.sync
            def _(sp):
                for ap, src in ((pair3, a["c_pair3"]), (pair4, a["c_pair4"]),
                                (q_factor, a["L0_mix_temperature"][0, :, 0, 0].partition_broadcast(TP)),
                                (proj_bias, a["L0_mix_bproj"].partition_broadcast(TP))):
                    sp.dma_start(ap[:, :], src).then_inc(c_in, 16)
                sp.dma_start(pairT[:, :, :], a["c_pairT"]).then_inc(c_in, 16)

                def body(u, j, i, last):
                    sp.wait_ge(k.rounded, u + 1)
                    sp.dma_start(kv[j][:, :], t.mix_qkv[ds(u * TP, TP), F:3 * F]).then_inc(kv_in[j], 16)
                over_tiles(sp, body)

            @block.vector
            def _(dve):
                dve.memset(g_acc[:, :, :, :], 0.0)
                dve.memset(slv_acc[:, :, :, :], 0.0)
                dve.memset(coef[:, :, :, :], 0.0)
                dve.memset(k_factor[:, :], SCALE)
                for j in range(U):
                    last_ = dve.memset(v1[j][:, :, 0:1], 1.0 / N)
                dve.wait_ge(c_in, 5 * 16)
                dve.tensor_scalar(q_factor[:, :], q_factor[:, :], SCALE * SCALE, None, ALU.mult).then_inc(cleared, 1)
                dve.wait_ge(cleared, 1)
                dve.sem_inc(g_read, 1)

                def add_pairs(u, h):
                    hh = u * HM + h
                    dve.wait_ge(g_ready, hh + 1)
                    dve.tensor_tensor(g_acc[:, h, :, :], g_acc[:, h, :, :], g_ps[h % 2][:, :, :], ALU.add).then_inc(g_read, 1)

                def body(u, j, i, last):
                    if not last:
                        nxt = (u + 1, (j + 1) % U)
                        k.dve_squares(dve, *nxt, i + (j + 1) // U)
                        k.dve_scale(dve, *nxt)
                    add_pairs(u, 0)
                    add_pairs(u, 1)
                    if not last:
                        k.dve_rest(dve, *nxt)
                    add_pairs(u, 2)
                    add_pairs(u, 3)
                    if not last:
                        k.dve_last(dve, *nxt)
                    dve.wait_ge(slv_ready, u + 1)
                    wait(dve, slv_read, u)
                    for i3 in range(3):
                        add = dve.tensor_tensor(slv_acc[:, i3, :, :], slv_acc[:, i3, :, :], slv_ps[i3][:, :, :], ALU.add)
                    add.then_inc(slv_read, 1)
                    for h in range(4, HM):
                        add_pairs(u, h)
                k.dve_squares(dve, 0, 0, 0)
                k.dve_scale(dve, 0, 0)
                k.dve_rest(dve, 0, 0)
                k.dve_last(dve, 0, 0)
                over_tiles(dve, body)

            @block.scalar
            def _(act):
                act.preload_act_table(ACT.Sqrt)
                act.sem_inc(k.rounded, U)

                def round_(u, j, i):
                    act.wait_ge(kv_in[j], i * 16 + 16)
                    act.activation(v1[j][:, :, 1:V1], kv[j][:, F:2 * F].rearrange("p (h d) -> p h d", h=HM), ACT.Copy,
                                   scale=1.0 / N).then_inc(v1_ready, 1)
                    k.act_round(act, u, j)
                    act.activation(ksq[j][:, :], k.unit[j][:, :], ACT.Square).then_inc(ksq_ready, 1)

                def square(u, h):
                    act.wait_ge(f_ready, u * HM + h + 1)
                    act.activation(phi[h % 2][:, :], f_ps[h % 2][:, :], ACT.Square).then_inc(phi_ready, 1)

                def body(u, j, i, last):
                    nxt = (u + 1, (j + 1) % U)
                    if not last:
                        k.act_root(act, *nxt)
                    square(u, 0)
                    square(u, 1)
                    if not last:
                        round_(*nxt, i + (j + 1) // U)
                    square(u, 2)
                    square(u, 3)
                    if not last:
                        k.act_middle(act, *nxt)
                    for h in range(4, HM):
                        square(u, h)
                    if not last:
                        k.act_turn_out(act, *nxt)
                act.wait_ge(cleared, 1)
                k.act_root(act, 0, 0)
                round_(0, 0, 0)
                k.act_middle(act, 0, 0)
                k.act_turn_out(act, 0, 0)
                over_tiles(act, body)

            @block.tensor
            def _(pe):
                def features(u, j, h):
                    pe.matmul(f_ps[h % 2][:, :], k.turned_parts[j][:, h, 0:TP], pair3[:, :], start=True, stop=True
                              ).then_inc(f_ready, 1)

                def pair_sums(u, j, h):
                    hh = u * HM + h
                    pe.wait_ge(phi_ready, hh + 1)
                    pe.wait_ge(g_read, hh)
                    for b in range(NPB):
                        mm = pe.matmul(g_ps[h % 2][:, b, :], phi[h % 2][:, b * PB:(b + 1) * PB], v1[j][:, h, :],
                                       start=True, stop=True)
                    mm.then_inc(g_ready, 1)

                def body(u, j, i, last):
                    pe.wait_ge(k.ready, u + 1)
                    features(u, j, 0)
                    pe.wait_ge(ksq_ready, u + 1)
                    pe.wait_ge(v1_ready, u + 1)
                    wait(pe, slv_read, u)
                    for i3, left in enumerate((ksq[j], k.unit[j], None)):
                        for half in range(2):
                            lhsT = t.ones[0:TP, :] if left is None else left[:, half * 128:(half + 1) * 128]
                            mm = pe.matmul(slv_ps[i3][:, half, :], lhsT,
                                           v1[j][:, 4 * half:4 * half + 4, :].rearrange("p h e -> p (h e)"),
                                           start=True, stop=True)
                    mm.then_inc(slv_ready, 1)
                    for h in range(1, HM):
                        features(u, j, h)
                        pair_sums(u, j, h - 1)
                    if not last:
                        k.pe_turn(pe, u + 1, (j + 1) % U, t.identb).then_inc(k.turned, 1)
                    pair_sums(u, j, HM - 1)
                k.pe_turn(pe, 0, 0, t.identb).then_inc(k.turned, 1)
                over_tiles(pe, body)

        with Memory(nc) as s:
            rs_ps = [s.ps(f"rs_ps{i}", [PB, NPB, V1]) for i in range(2)]
            m_ps = s.ps("m_ps", [128, 2, V1])
            rs_ready, m_half, m_ready, dve_order = s.sem("rs_ready"), s.sem("m_half"), s.sem("m_ready"), s.sem("coef_order")
            block = s.block()

            @block.tensor
            def _(pe):
                for h in range(HM):
                    at, cols = slice(32 * (h % 4), 32 * (h % 4) + 32), slice((h % 4) * V1, (h % 4 + 1) * V1)
                    if h >= 2:
                        pe.wait_ge(m_half, h - 1)
                    for b in range(NPB):
                        mm = pe.matmul(rs_ps[h % 2][:, b, :], pair4[at, b * PB:(b + 1) * PB], slv_acc[at, 0, h // 4, cols],
                                       start=True, stop=True)
                    mm.then_inc(rs_ready, 1)
                for h in range(HM):
                    pe.wait_ge(m_half, h + 1)
                    at = slice(32 * (h % 4), 32 * (h % 4) + 32)
                    for b in range(NPB):
                        mm = pe.matmul(m_ps[at, h // 4, :], pairT[:, b, :], g_acc[:, h, b, :], start=(b == 0), stop=(b == NPB - 1))
                    mm.then_inc(m_ready, 1)

            @block.vector
            def _(dve):
                order = Order(dve, dve_order)
                for h in range(HM):
                    dve.wait_ge(rs_ready, h + 1)
                    order(dve.tensor_tensor(g_acc[:, h, :, :], g_acc[:, h, :, :], rs_ps[h % 2][:, :, :], ALU.subtract))
                    dve.tensor_scalar(g_acc[:, h, :, :], g_acc[:, h, :, :], 0.25, None, ALU.mult).then_inc(m_half, 1)
                dve.wait_ge(m_ready, HM)
                for h in range(HM):
                    at, cols = slice(32 * (h % 4), 32 * (h % 4) + 32), slice((h % 4) * V1, (h % 4 + 1) * V1)
                    dve.scalar_tensor_tensor(coef[at, 0, h // 4, cols], slv_acc[at, 0, h // 4, cols], 0.5,
                                             m_ps[at, h // 4, :], ALU.mult, ALU.subtract)
                    dve.tensor_scalar(coef[at, 1, h // 4, cols], slv_acc[at, 1, h // 4, cols], SCALE ** 2, None, ALU.mult)
                order(dve.tensor_scalar(slv_acc[0:1, 2, :, :], slv_acc[0:1, 2, :, :], SCALE ** 4, None, ALU.mult))

        with Memory(nc) as s:
            mq = [s.sb(f"mq{j}", [TP, F]) for j in range(U)]
            qT = [s.sb(f"qT{j}", [128, 2, FC, TP]) for j in range(U)]
            phi = [s.sb(f"qphi{i}", [PB, NPB, TP]) for i in range(2)]
            inv = [s.sb(f"y_inv{j}", [TP, HM]) for j in range(U)]
            y = [s.sb(f"y{j}", [TP, F]) for j in range(U)]
            yT = [s.sb(f"yT{j}", [128, FC, TP]) for j in range(U)]
            biased = [s.sb(f"biased{j}", [TP, F]) for j in range(U)]
            qT_ps = s.ps("qT_ps", [128, FC, TP])
            f_ps = [s.ps(f"qf_ps{i}", [PB, NPB, TP]) for i in range(2)]
            y_ps = [s.ps(f"y_ps{i}", [TP, HM, V1]) for i in range(2)]
            yT_ps = s.ps("yT_ps", [128, FC, TP])
            out_ps = s.ps("out_ps", [TP, F])
            mq_in = s.sems("mq_in", U)
            qT_ready, f_ready, phi_ready, sum_ready, inv_ready, y_ready, yT_turned, yT_ready, out_ready, biased_ready, added = (
                s.sem("q_" + x) for x in ("T2", "f", "phi", "sum", "inv", "y", "yT_turned", "yT", "out", "biased", "added"))
            q = Unit(s, "mq", mq_in, lambda j: mq[j][:, :], SCALE * SCALE, q_factor[:, :])
            block = s.block()

            @block.sync
            def _(sp):
                def body(u, j, i, last):
                    sp.wait_ge(q.rounded, u + 1)
                    sp.dma_start(mq[j][:, :], t.mix_qkv[ds(u * TP, TP), 0:F]).then_inc(mq_in[j], 16)
                over_tiles(sp, body)

            @block.vector
            def _(dve):
                def body(u, j, i, last):
                    if not last:
                        nxt = (u + 1, (j + 1) % U)
                        q.dve_squares(dve, *nxt, i + (j + 1) // U)
                        q.dve_scale(dve, *nxt)
                        q.dve_rest(dve, *nxt)
                        q.dve_last(dve, *nxt)
                    dve.wait_ge(sum_ready, u + 1)
                    dve.reciprocal(inv[j][:, :], y_ps[j % 2][:, :, 0]).then_inc(inv_ready, 1)
                    dve.wait_ge(inv_ready, u + 1)
                    dve.tensor_tensor(y[j][:, :].rearrange("p (h d) -> p h d", h=HM), y_ps[j % 2][:, :, 1:V1],
                                      bcast(inv[j][:, :].unsqueeze(2), TP, HM, DM), ALU.mult).then_inc(y_ready, 1)
                    dve.wait_ge(out_ready, u + 1)
                    dve.tensor_tensor(biased[j][:, :], out_ps[:, :], proj_bias[:, :], ALU.add).then_inc(biased_ready, 1)
                    dve.wait_ge(biased_ready, u + 1)
                    dve.tensor_tensor(t.x_all[:, u, :], t.x_all[:, u, :], biased[j][:, :], ALU.add)
                q.dve_squares(dve, 0, 0, 0)
                q.dve_scale(dve, 0, 0)
                q.dve_rest(dve, 0, 0)
                q.dve_last(dve, 0, 0)
                over_tiles(dve, body)

            @block.scalar
            def _(act):
                act.preload_act_table(ACT.Sqrt)
                act.sem_inc(q.rounded, U)

                def turn_out(u, j):
                    q.act_turn_out(act, u, j)
                    act.activation(qT[j][:, 0, :, :], qT_ps[:, :, :], ACT.Square)
                    act.activation(qT[j][:, 1, :, :], qT_ps[:, :, :], ACT.Copy).then_inc(qT_ready, 1)

                def square(u, h):
                    act.wait_ge(f_ready, u * HM + h + 1)
                    act.activation(phi[h % 2][:, :, :], f_ps[h % 2][:, :, :], ACT.Square).then_inc(phi_ready, 1)

                def body(u, j, i, last):
                    nxt = (u + 1, (j + 1) % U)
                    if not last:
                        q.act_root(act, *nxt)
                    square(u, 0)
                    if not last:
                        q.act_round(act, *nxt)
                    square(u, 1)
                    square(u, 2)
                    if not last:
                        q.act_middle(act, *nxt)
                    for h in range(3, HM):
                        square(u, h)
                    act.wait_ge(yT_turned, u + 1)
                    act.activation(yT[j][:, :, :], yT_ps[:, :, :], ACT.Copy).then_inc(yT_ready, 1)
                    if not last:
                        turn_out(*nxt)
                q.act_root(act, 0, 0)
                q.act_round(act, 0, 0)
                q.act_middle(act, 0, 0)
                turn_out(0, 0)
                over_tiles(act, body)

            @block.tensor
            def _(pe):
                def turn(u, j):
                    mm = q.pe_turn(pe, u, j, t.identb)
                    wait(pe, qT_ready, u)
                    for k2 in range(FC):
                        mm = pe.transpose(qT_ps[:, k2, :], q.unit[j][:, k2 * 128:(k2 + 1) * 128], t.ident[0:TP, 0:TP])
                    mm.then_inc(q.turned, 1)

                def features(u, j, h):
                    for b in range(NPB):
                        mm = pe.matmul(f_ps[h % 2][:, b, :], pair3[:, b * PB:(b + 1) * PB], q.turned_parts[j][:, h, 0:TP],
                                       start=True, stop=True)
                    mm.then_inc(f_ready, 1)

                def node_sums(u, j, h):
                    pe.wait_ge(phi_ready, u * HM + h + 1)
                    for b in range(NPB):
                        mm = pe.matmul(y_ps[j % 2][:, h, :], phi[h % 2][:, b, :], g_acc[:, h, b, :], start=False,
                                       stop=(b == NPB - 1), skip_group_check=True)
                    return mm

                def body(u, j, i, last):
                    pe.wait_ge(qT_ready, u + 1)
                    features(u, j, 0)
                    wait(pe, y_ready, psum_turn(u, j))
                    flat = y_ps[j % 2][:, :, :].rearrange("p h e -> p (h e)")
                    pe.matmul(flat, t.ones[0:1, 0:TP], slv_acc[0:1, 2, :, :].rearrange("p a e -> p (a e)"), start=True, stop=False,
                              skip_group_check=True)
                    for kind in range(2):
                        for half in range(2):
                            pe.matmul(flat[:, half * HW:(half + 1) * HW], qT[j][:, kind, half, :], coef[:, kind, half, :],
                                      start=False, stop=False, skip_group_check=True)
                    for h in range(1, HM):
                        features(u, j, h)
                        node_sums(u, j, h - 1)
                    node_sums(u, j, HM - 1).then_inc(sum_ready, 1)
                    pe.wait_ge(y_ready, u + 1)
                    for k2 in range(FC):
                        mm = pe.transpose(yT_ps[:, k2, :], y[j][:, k2 * 128:(k2 + 1) * 128], t.ident[0:TP, 0:TP])
                    mm.then_inc(yT_turned, 1)
                    if not last:
                        turn(u + 1, (j + 1) % U)
                    pe.wait_ge(yT_ready, u + 1)
                    wait(pe, biased_ready, u)
                    for k2 in range(FC):
                        mm = pe.matmul(out_ps[:, :], yT[j][:, k2, :], t.wproj[:, k2, :], start=(k2 == 0), stop=(k2 == FC - 1))
                    mm.then_inc(out_ready, 1)
                turn(0, 0)
                over_tiles(pe, body)


def stage_graph_ffn(nc, a, t):
    with Memory(nc) as s:
        w1, w2 = s.sb("g_w1", [128, FC, HID]), s.sb("g_w2", [128, HB, F])
        cols = s.sb("g_cols", [128, 2, HB])
        cols_in = s.sb("g_cols_in", [2 * HB, 128])
        gamma, beta, b2 = s.sb("gamma", [TP, F]), s.sb("beta", [TP, F]), s.sb("g_b2", [TP, F])
        wr, br = s.sb("wr", [128, FC, NEX]), s.sb("br", [TP, NEX])
        den = [s.sb(f"den{j}", [TP, 2, HG]) for j in range(U)]
        buf = [s.sb(f"g_buf{j}", [TP, F]) for j in range(U)]
        buf2 = [s.sb(f"g_buf2{j}", [TP, F]) for j in range(U)]
        plus_b2 = [s.sb(f"plus_b2{j}", [TP, F]) for j in range(U)]
        r1 = [s.sb(f"r1{j}", [TP, F]) for j in range(U)]
        r1T = [s.sb(f"r1T{j}", [128, FC, TP]) for j in range(U)]
        hid = [s.sb(f"hid{i}", [128, HB, TP]) for i in range(U)]
        low = [s.sb(f"low{i}", [128, HB, TP]) for i in range(2)]
        st, tmp = s.sb("g_st", [TP, NT, 6]), s.sb("g_tmp", [TP, 5, NT])
        var, std = s.sb("g_var", [TP, NT]), s.sb("g_std", [TP, NT])
        mean, rstd = s.sb("g_mean", [TP, NT]), s.sb("g_rstd", [TP, NT])
        turn_ps = [s.ps(f"r1_ps{i}", [128, FC, TP]) for i in range(2)]
        hid_ps = [s.ps(f"hid_ps{i}", [128, 2, 512]) for i in range(2)]
        y_ps = [s.ps(f"gy_ps{i}", [TP, F]) for i in range(2)]
        w_in, cols_turned, cols_ready = s.sem("g_w_in"), s.sem("g_cols_turned"), s.sem("g_cols_ready")
        stat_order, stats_done, var_ready, std_ready = s.sem("stat_order"), s.sem("stats_done"), s.sem("g_var_ready"), s.sem("g_std_ready")
        res_order, norm_order, end_order, carrier = s.sem("res_order"), s.sem("norm_order"), s.sem("end_order"), s.sem("g_carrier")
        r1_ready, turned, r1T_ready, h_ready, biased, low_ready, act_ready, y_ready, y_read, sum_ready = (
            s.sem("g_" + x) for x in ("r1", "turned", "r1T", "h", "biased", "low", "act", "y", "y_read", "sum"))
        z_ready, z_turned, zT_ready, logit_ready, logit_read = (s.sem("g_" + x) for x in ("z", "z_turned", "zT", "logit", "logit_read"))
        block = s.block()
        RESIDUAL, END = 4, 4
        STAT = 7

        @block.sync
        def _(sp):
            for ap, src in ((w1, a["L0_gnn_W1"].rearrange("(k p) n -> p k n", p=128)),
                            (w2, a["L0_gnn_W2"].rearrange("(k p) n -> p k n", p=128)),
                            (wr, a["L0_ffn_Wr"].rearrange("(k p) n -> p k n", p=128))):
                sp.dma_start(ap[:, :, :], src).then_inc(w_in, 16)
            for ap, name in ((gamma, "L0_gnn_ln_g"), (beta, "L0_gnn_ln_b"), (b2, "L0_gnn_b2"), (br, "L0_ffn_br")):
                sp.dma_start(ap[:, :], a[name].partition_broadcast(TP)).then_inc(w_in, 16)
            sp.dma_start(cols_in[0:HB, :], a["L0_gnn_b1"].rearrange("(b p) -> b p", p=128)).then_inc(w_in, 16)
            sp.dma_start(cols_in[HB:2 * HB, :], a["L0_gnn_alpha"].rearrange("(b p) -> b p", p=128)).then_inc(w_in, 16)

        @block.vector
        def _(dve):
            def batched(n, mean, rstd):
                order = Order(dve, stat_order, n * STAT)
                dve.wait_ge(stats_done, (n + 1) * NT)
                finish_stats(dve, order, st, mean, var, tmp).then_inc(var_ready, 1)
                dve.wait_ge(std_ready, n + 1)
                order(dve.reciprocal(rstd[:, :], std[:, :]))

            def stats(u, src):
                dve.sem_inc(carrier, 1)
                dve.bn_stats(st[:, u, :], src).then_inc(stats_done, 1)

            dve.wait_ge(w_in, 9 * 16)
            dve.wait_ge(cols_turned, 1)
            dve.tensor_copy(cols[:, :, :], turn_ps[0][:, 0, 0:2 * HB].rearrange("p (c b) -> p c b", c=2)).then_inc(cols_ready, 1)
            dve.wait_ge(cols_ready, 1)

            def residual(u, j, i, last):
                order = Order(dve, res_order, u * RESIDUAL)
                order(dve.tensor_scalar(den[j][:, 0, :], t.acc[:, u, F:F + HG], 1e-30, None, ALU.max))
                order(dve.reciprocal(den[j][:, 1, :], den[j][:, 0, :]))
                order(dve.tensor_tensor(buf[j][:, :].rearrange("p (h d) -> p h d", h=HG),
                                        t.acc[:, u, 0:F].rearrange("p (h d) -> p h d", h=HG),
                                        bcast(den[j][:, 1, :].unsqueeze(2), TP, HG, DG), ALU.mult))
                order(dve.tensor_tensor(t.xn_all[:, u, :], buf[j][:, :], t.xn_all[:, u, :], ALU.add))
                stats(u, t.xn_all[:, u, :])
            over_tiles(dve, residual)
            batched(0, mean, rstd)

            def normal(u, j):
                order = Order(dve, norm_order, u * 2)
                order(dve.tensor_scalar(buf[j][:, :], t.xn_all[:, u, :], mean[:, ds(u, 1)], rstd[:, ds(u, 1)],
                                        ALU.subtract, ALU.mult))
                order(dve.tensor_tensor(buf2[j][:, :], buf[j][:, :], gamma[:, :], ALU.mult))
                dve.tensor_tensor(r1[j][:, :], buf2[j][:, :], beta[:, :], ALU.add).then_inc(r1_ready, 1)

            def ffn(u, j, i, last):
                dve.wait_ge(biased, u + 1)
                dve.scalar_tensor_tensor(low[j % 2][:, :, :], hid[j][:, :, :], 0.0,
                                         bcast(cols[:, 1, :].unsqueeze(2), 128, HB, TP), ALU.min, ALU.mult).then_inc(low_ready, 1)
                dve.wait_ge(low_ready, u + 1)
                dve.scalar_tensor_tensor(hid[j][:, :, :], hid[j][:, :, :], 0.0, low[j % 2][:, :, :],
                                         ALU.max, ALU.add).then_inc(act_ready, 1)
                if not (isinstance(u, int) and u + 2 >= NT):
                    normal(u + 2, (j + 2) % U)
                dve.wait_ge(y_ready, u + 1)
                dve.tensor_tensor(plus_b2[j][:, :], y_ps[j % 2][:, :], b2[:, :], ALU.add).then_inc(y_read, 1)
                dve.wait_ge(y_read, u + 1)
                dve.tensor_tensor(t.xn_all[:, u, :], plus_b2[j][:, :], r1[j][:, :], ALU.add).then_inc(sum_ready, 1)
                dve.wait_ge(sum_ready, u + 1)
                stats(u, t.xn_all[:, u, :])
            normal(0, 0)
            normal(1, 1)
            over_tiles(dve, ffn)
            batched(1, mean, rstd)

            def onto_x(u, j, i, last):
                order = Order(dve, end_order, u * END)
                order(dve.tensor_scalar(buf[j][:, :], t.xn_all[:, u, :], mean[:, ds(u, 1)], rstd[:, ds(u, 1)],
                                        ALU.subtract, ALU.mult))
                order(dve.tensor_tensor(buf2[j][:, :], buf[j][:, :], gamma[:, :], ALU.mult))
                order(dve.tensor_tensor(plus_b2[j][:, :], buf2[j][:, :], beta[:, :], ALU.add))
                order(dve.tensor_tensor(t.x_all[:, u, :], t.x_all[:, u, :], plus_b2[j][:, :], ALU.add))
                stats(u, t.x_all[:, u, :])
            over_tiles(dve, onto_x)
            batched(2, t.x_mean, t.x_rstd)

            def make_z(u, j):
                dve.tensor_scalar(r1[j][:, :], t.x_all[:, u, :], t.x_mean[:, ds(u, 1)], t.x_rstd[:, ds(u, 1)],
                                  ALU.subtract, ALU.mult).then_inc(z_ready, 1)
                dve.wait_ge(z_ready, u + 1)
                stats(u, r1[j][:, :])

            def route(u, j, i, last):
                if not last:
                    make_z(u + 1, (j + 1) % U)
                dve.wait_ge(logit_ready, u + 1)
                dve.tensor_tensor(t.logits[:, u, :], y_ps[j % 2][:, 0:NEX], br[:, :], ALU.add).then_inc(logit_read, 1)
            make_z(0, 0)
            over_tiles(dve, route)
            batched(3, t.z_mean, t.z_rstd)

        @block.scalar
        def _(act):
            act.preload_act_table(ACT.Sqrt)

            def root(n):
                act.wait_ge(var_ready, n + 1)
                act.activation(std[:, :], var[:, :], ACT.Sqrt).then_inc(std_ready, 1)

            def turn_out(u, j):
                act.wait_ge(turned, u + 1)
                act.activation(r1T[j][:, :, :], turn_ps[j % 2][:, :, :], ACT.Copy).then_inc(r1T_ready, 1)

            def bias(u, j):
                act.wait_ge(h_ready, u + 1)
                for b in range(HB):
                    one = act.activation(hid[j][:, b, :], hid_ps[j % 2][:, b // 4, (b % 4) * TP:(b % 4 + 1) * TP],
                                         ACT.Identity, bias=cols[:, 0, b:b + 1])
                one.then_inc(biased, 1)

            def body(u, j, i, last):
                if not last:
                    turn_out(u + 1, (j + 1) % U)
                    bias(u + 1, (j + 1) % U)
            root(0)
            turn_out(0, 0)
            bias(0, 0)
            over_tiles(act, body)
            root(1)
            root(2)

            def z_turn_out(u, j, i, last):
                act.wait_ge(z_turned, u + 1)
                act.activation(r1T[j][:, :, :], turn_ps[j % 2][:, :, :], ACT.Copy).then_inc(zT_ready, 1)
            over_tiles(act, z_turn_out)
            root(3)

        @block.tensor
        def _(pe):
            pe.wait_ge(w_in, 9 * 16)
            pe.transpose(turn_ps[0][:, 0, 0:2 * HB], cols_in[:, :], t.ident[0:2 * HB, 0:2 * HB]).then_inc(cols_turned, 1)
            pe.wait_ge(cols_ready, 1)

            def turn(u, j, ready, out, done):
                pe.wait_ge(ready, u + 1)
                wait(pe, out, psum_turn(u, j))
                for k in range(FC):
                    mm = pe.transpose(turn_ps[j % 2][:, k, :], r1[j][:, k * 128:(k + 1) * 128], t.ident[0:TP, 0:TP])
                mm.then_inc(done, 1)

            def hidden(u, j):
                pe.wait_ge(r1T_ready, u + 1)
                wait(pe, biased, psum_turn(u, j))
                for b in range(HB):
                    for k in range(FC):
                        mm = pe.matmul(hid_ps[j % 2][:, b // 4, (b % 4) * TP:(b % 4 + 1) * TP], w1[:, k, b * 128:(b + 1) * 128],
                                       r1T[j][:, k, :], start=(k == 0), stop=(k == FC - 1))
                mm.then_inc(h_ready, 1)

            def body(u, j, i, last):
                if not last:
                    turn(u + 1, (j + 1) % U, r1_ready, r1T_ready, turned)
                    hidden(u + 1, (j + 1) % U)
                pe.wait_ge(act_ready, u + 1)
                wait(pe, y_read, psum_turn(u, j))
                for b in range(HB):
                    mm = pe.matmul(y_ps[j % 2][:, :], hid[j][:, b, :], w2[:, b, :], start=(b == 0), stop=(b == HB - 1))
                mm.then_inc(y_ready, 1)
            turn(0, 0, r1_ready, r1T_ready, turned)
            hidden(0, 0)
            over_tiles(pe, body)

            def logits(u, j, i, last):
                if not last:
                    turn(u + 1, (j + 1) % U, z_ready, zT_ready, z_turned)
                pe.wait_ge(zT_ready, u + 1)
                wait(pe, logit_read, psum_turn(u, j))
                for k in range(FC):
                    mm = pe.matmul(y_ps[j % 2][:, 0:NEX], r1T[j][:, k, :], wr[:, k, :], start=(k == 0), stop=(k == FC - 1))
                mm.then_inc(logit_ready, 1)
            turn(0, 0, z_ready, zT_ready, z_turned)
            over_tiles(pe, logits)


def stage_experts(nc, a, t, out):
    with Memory(nc) as m:
        weight = m.sb("weight", [TP, 2, NT])
        pos = m.sb("pos", [TP, NT, 2], I32)
        tile_ex = m.sb("tile_ex", [1, NMT], I32)
        table = m.sb("ex_table", [128, NEX, HB + 2 * FC])

        with Memory(nc) as s:
            before = s.sb("e_before", [TP, NEX * NEX])
            keep = s.sb("keep", [TP, NEX * NT])
            tri = s.sb("tri", [TP, TP])
            tile_at = s.sb("tile_at", [1, NMT])
            tab_in = s.sb("tab_in", [NEX * HB + 2 * NEX * FC, 128])
            more, same = s.sb("more", [TP, NT, NEX, NEX]), s.sb("same", [TP, NT, NEX, NEX])
            rank = s.sb("rank", [TP, NT, NEX])
            pick = s.sb("pick", [TP, 3, NT, NEX])
            prod = s.sb("r_prod", [TP, 2, NT, NEX])
            best = s.sb("best", [TP, 2, NT])
            diff, p2, den = s.sb("diff", [TP, NT]), s.sb("p2", [TP, NT]), s.sb("r_den", [TP, NT])
            tot, upto, at = s.sb("tot", [TP, NEX, NT]), s.sb("upto", [TP, NEX, NT]), s.sb("at", [TP, NEX, NT])
            size, size_i = s.sb("size", [TP, 4, NEX]), s.sb("size_i", [TP, 2, NEX], I32)
            pos_f = s.sb("pos_f", [TP, 2, NT])
            past = s.sb("past", [1, NMT, NEX])
            tile_f = s.sb("tile_f", [1, 2, NMT])
            zb = [s.sb(f"zb{j}", [TP, F]) for j in range(U)]
            rows = [s.sb(f"rows{j}", [TP, F]) for j in range(U)]
            idx = [s.sb(f"s_idx{j}", [TP, 2], I32) for j in range(U)]
            pre_ps, tot_ps = s.ps("pre_ps", [TP, NT, NEX]), s.ps("tot_ps", [TP, NT, NEX])
            tab_ps = s.ps("tab_ps", [128, 128])
            c_in, dve_order, picked, counted, diff_ready, p2_ready, tab_turned = (
                s.sem("r_" + x) for x in ("c_in", "order", "picked", "counted", "diff", "p2", "tab"))
            z_again, rows_ready, idx_ready, carrier = s.sem("z_again"), s.sem("rows_ready"), s.sem("s_idx_ready"), s.sem("s_carrier")
            row_out = s.gather_sems("row_out", U)
            block = s.block()

            @block.sync
            def _(sp):
                for ap, name in ((before, "c_before"), (keep, "c_keep")):
                    sp.dma_start(ap[:, :], a[name][0, :].partition_broadcast(TP)).then_inc(c_in, 16)
                sp.dma_start(tri[:, :], a["c_tri"]).then_inc(c_in, 16)
                sp.dma_start(tile_at[:, :], a["c_tile_at"]).then_inc(c_in, 16)
                lo = NEX * HB
                sp.dma_start(tab_in[0:lo, :], a["L0_ffn_b1"].rearrange("e (b p) -> (e b) p", p=128)).then_inc(c_in, 16)
                sp.dma_start(tab_in[lo:lo + NEX * FC, :], a["L0_ffn_ln_g"].rearrange("e (k p) -> (e k) p", p=128)).then_inc(c_in, 16)
                sp.dma_start(tab_in[lo + NEX * FC:, :], a["L0_ffn_ln_b"].rearrange("e (k p) -> (e k) p", p=128)).then_inc(c_in, 16)

            @block.tensor
            def _(pe):
                pe.wait_ge(c_in, 7 * 16)
                rows_ = NEX * HB + 2 * NEX * FC
                pe.transpose(tab_ps[:, 0:rows_], tab_in[:, :], t.ident[0:rows_, 0:rows_]).then_inc(tab_turned, 1)
                pe.wait_ge(picked, 1)
                flat = pick[:, 2, :, :].rearrange("p t e -> p (t e)")
                pe.matmul(pre_ps[:, :, :].rearrange("p t e -> p (t e)"), tri[:, :], flat, start=True, stop=True)
                pe.matmul(tot_ps[:, :, :].rearrange("p t e -> p (t e)"), t.ones[0:TP, 0:TP], flat, start=True, stop=True
                          ).then_inc(counted, 1)

            @block.scalar
            def _(act):
                act.preload_act_table(ACT.Exp)
                act.wait_ge(diff_ready, 1)
                act.activation(p2[:, :], diff[:, :], ACT.Exp).then_inc(p2_ready, 1)

            @block.vector
            def _(dve):
                order = Order(dve, dve_order)
                L = t.logits
                full = (TP, NT, NEX, NEX)
                mine, other = bcast(L[:, :, :].unsqueeze(3), *full), bcast(L[:, :, :].unsqueeze(2), *full)
                dve.wait_ge(c_in, 7 * 16)
                order(dve.tensor_tensor(more[:, :, :, :], other, mine, ALU.is_gt))
                order(dve.tensor_tensor(same[:, :, :, :], other, mine, ALU.is_equal))
                flat = lambda x: x[:, :, :, :].rearrange("p t i j -> p t (i j)")
                order(dve.tensor_tensor(flat(same), flat(same), bcast(before[:, :].unsqueeze(1), TP, NT, NEX * NEX), ALU.mult))
                order(dve.tensor_tensor(flat(more), flat(more), flat(same), ALU.add))
                order(dve.tensor_reduce(rank[:, :, :], more[:, :, :, :], AX.X, ALU.add))
                order(dve.tensor_scalar(pick[:, 0, :, :], rank[:, :, :], 0.0, None, ALU.is_equal))
                order(dve.tensor_scalar(pick[:, 1, :, :], rank[:, :, :], 1.0, None, ALU.is_equal))
                order(dve.tensor_tensor(pick[:, 2, :, :], pick[:, 0, :, :], pick[:, 1, :, :], ALU.add))
                dve.sem_inc(picked, 1)
                for c in range(2):
                    order(dve.tensor_tensor(prod[:, c, :, :], L[:, :, :], pick[:, c, :, :], ALU.mult))
                order(dve.tensor_reduce(best[:, :, :], prod[:, :, :, :], AX.X, ALU.add))
                order(dve.tensor_tensor(diff[:, :], best[:, 1, :], best[:, 0, :], ALU.subtract))
                dve.sem_inc(diff_ready, 1)
                dve.wait_ge(p2_ready, 1)
                order(dve.tensor_scalar(den[:, :], p2[:, :], 1.0, None, ALU.add))
                order(dve.reciprocal(weight[:, 0, :], den[:, :]))
                order(dve.tensor_tensor(weight[:, 1, :], p2[:, :], weight[:, 0, :], ALU.mult))
                dve.wait_ge(counted, 1)
                order(dve.tensor_copy(tot[:, :, :], tot_ps[:, :, :].rearrange("p t e -> p e t")))
                order(dve.tensor_tensor_scan(upto[:, :, :].rearrange("p e t -> p (e t)"), keep[:, :],
                                             tot[:, :, :].rearrange("p e t -> p (e t)"), 0.0, ALU.mult, ALU.add))
                order(dve.tensor_scalar(size[:, 0, :], upto[:, :, NT - 1], float(MT - 1), None, ALU.add))
                order(dve.tensor_copy(size_i[:, 0, :], size[:, 0, :]))
                bits = MT.bit_length() - 1
                order(dve.tensor_scalar(size_i[:, 1, :], size_i[:, 0, :], bits, bits, ALU.logical_shift_right, ALU.logical_shift_left))
                order(dve.tensor_copy(size[:, 1, :], size_i[:, 1, :]))
                order(dve.tensor_tensor_scan(size[:, 2, :], t.ones[0:TP, 0:NEX], size[:, 1, :], 0.0, ALU.mult, ALU.add))
                order(dve.tensor_tensor(size[:, 3, :], size[:, 2, :], size[:, 1, :], ALU.subtract))
                order(dve.tensor_tensor(at[:, :, :], upto[:, :, :], tot[:, :, :], ALU.subtract))
                order(dve.tensor_tensor(at[:, :, :], at[:, :, :], bcast(size[:, 3, :].unsqueeze(2), TP, NEX, NT), ALU.add))
                order(dve.tensor_tensor(at[:, :, :], at[:, :, :], pre_ps[:, :, :].rearrange("p t e -> p e t"), ALU.add))
                for c in range(2):
                    order(dve.tensor_tensor(prod[:, c, :, :], at[:, :, :].rearrange("p e t -> p t e"), pick[:, c, :, :], ALU.mult))
                order(dve.tensor_reduce(pos_f[:, :, :], prod[:, :, :, :], AX.X, ALU.add))
                order(dve.tensor_copy(pos[:, :, :], pos_f[:, :, :].rearrange("p c t -> p t c")))
                order(dve.tensor_tensor(past[:, :, :], bcast(size[0:1, 2, :].unsqueeze(1), 1, NMT, NEX),
                                        bcast(tile_at[:, :].unsqueeze(2), 1, NMT, NEX), ALU.is_le))
                order(dve.tensor_reduce(tile_f[:, 0, :], past[:, :, :], AX.X, ALU.add))
                order(dve.tensor_scalar(tile_f[:, 1, :], tile_f[:, 0, :], float(NEX - 1), None, ALU.min))
                order(dve.tensor_copy(tile_ex[:, :], tile_f[:, 1, :]))
                dve.wait_ge(tab_turned, 1)
                lo = NEX * HB
                dve.tensor_copy(table[:, :, 0:HB], tab_ps[:, 0:lo].rearrange("p (e b) -> p e b", b=HB))
                for c in range(2):
                    dve.tensor_copy(table[:, :, HB + c * FC:HB + (c + 1) * FC],
                                    tab_ps[:, lo + c * NEX * FC:lo + (c + 1) * NEX * FC].rearrange("p (e k) -> p e k", k=FC))

                def make_rows(u, j, i, last):
                    wait(dve, row_out[j], i * 32)
                    dve.tensor_scalar(idx[j][:, :], pos[:, u, :], 0.0, None, ALU.add).then_inc(idx_ready, 1)
                    dve.tensor_scalar(zb[j][:, :], t.x_all[:, u, :], t.x_mean[:, ds(u, 1)], t.x_rstd[:, ds(u, 1)],
                                      ALU.subtract, ALU.mult).then_inc(z_again, 1)
                    dve.wait_ge(z_again, u + 1)
                    dve.tensor_scalar(rows[j][:, :], zb[j][:, :], t.z_mean[:, ds(u, 1)], t.z_rstd[:, ds(u, 1)],
                                      ALU.subtract, ALU.mult).then_inc(rows_ready, 1)
                over_tiles(dve, make_rows)

            @block.gpsimd
            def _(pool):
                def scatter(u, j, i, last):
                    pool.wait_ge(rows_ready, u + 1)
                    pool.sem_inc(carrier, 1)
                    for c in range(2):
                        pool.indirect_dma_start(out=t.x_rows, out_offset=bass.IndirectOffsetOnAxis(ap=idx[j][:, c:c + 1], axis=0),
                                                in_=rows[j][:, :], in_offset=None).then_inc(row_out[j], 16)
                over_tiles(pool, scatter)
                for j in range(U):
                    pool.wait_ge(row_out[j], NT // U * 32)

        with Memory(nc) as s:
            w1 = [s.sb(f"e_w1{i}", [128, FC, HID]) for i in range(2)]
            w2 = [s.sb(f"e_w2{i}", [128, HB, F]) for i in range(2)]
            b2 = [s.sb(f"e_b2{i}", [128, F]) for i in range(2)]
            xr = [s.sb(f"xr{i}", [128, 2, F]) for i in range(2)]
            small = [s.sb(f"small{i}", [128, HB + 2 * FC]) for i in range(2)]
            xT = [s.sb(f"e_xT{i}", [128, FC, MT]) for i in range(2)]
            hT = [s.sb(f"e_hT{i}", [128, HB, MT]) for i in range(2)]
            y = [s.sb(f"e_y{i}", [128, 2, F]) for i in range(2)]
            turn_ps = [s.ps(f"e_turn{i}", [128, FC, MT]) for i in range(2)]
            h_ps = s.ps("e_h", [128, HB, MT])
            y_ps = s.ps("e_yps", [128, 2, 512])
            w1_in, w2_in, b2_in, x_in, y_out = (s.sems("e_" + x, 2) for x in ("w1_in", "w2_in", "b2_in", "x_in", "y_out"))
            small_ready, turned, xT_ready, h_ready, h_read, y_ready, y_read = (
                s.sem("e_" + x) for x in ("small", "turned", "xT", "h", "h_read", "y", "y_read"))
            block = s.block()

            def over_experts(eng, body):
                with eng.Fori(0, NMT // 2 - 1) as i:
                    for par in range(2):
                        body(i * 2 + par, par, i, False)
                for par in range(2):
                    body(NMT - 2 + par, par, NMT // 2 - 1, par == 1)

            @block.sync
            def _(sp):
                def body(n, par, i, last):
                    ex = sp.value_load(tile_ex[0:1, ds(n, 1)], min_val=0, max_val=NEX - 1)
                    sp.wait_ge(y_read, n)
                    sp.dma_start(xr[par][:, :, :], t.x_rows[ds(n * MT, MT), :].rearrange("(s p) f -> p s f", p=128)
                                 ).then_inc(x_in[par], 16)
                    sp.dma_start(w1[par][:, :, :], a["L0_ffn_W1"].rearrange("e (k p) n -> e p k n", p=128)[ex]).then_inc(w1_in[par], 16)
                    sp.dma_start(w2[par][:, :, :], a["L0_ffn_W2"].rearrange("e (b p) n -> e p b n", p=128)[ex]).then_inc(w2_in[par], 16)
                    sp.dma_start(b2[par][:, :], a["L0_ffn_b2"][ex].partition_broadcast(128)).then_inc(b2_in[par], 16)
                over_experts(sp, body)

            @block.vector
            def _(dve):
                def prepare(n, par, i):
                    ex = dve.value_load(tile_ex[0:1, ds(n, 1)], min_val=0, max_val=NEX - 1)
                    dve.wait_ge(turned, n + 1)
                    dve.tensor_scalar(small[par][:, :], table[:, ex, :], 0.0, None, ALU.add).then_inc(small_ready, 1)
                    dve.wait_ge(small_ready, n + 1)
                    for k in range(FC):
                        one = dve.tensor_scalar(xT[par][:, k, :], turn_ps[par][:, k, :], small[par][:, HB + k:HB + k + 1],
                                                small[par][:, HB + FC + k:HB + FC + k + 1], ALU.mult, ALU.add)
                    one.then_inc(xT_ready, 1)

                def body(n, par, i, last):
                    if not last:
                        prepare(n + 1, 1 - par, i + par)
                    wait(dve, y_out[par], i * 16)
                    dve.wait_ge(b2_in[par], i * 16 + 16)
                    dve.wait_ge(y_ready, n + 1)
                    dve.tensor_tensor(y[par][:, :, :], y_ps[:, :, 0:F], bcast(b2[par][:, :].unsqueeze(1), 128, 2, F), ALU.add
                                      ).then_inc(y_read, 1)
                dve.sem_inc(y_read, 1)
                prepare(0, 0, 0)
                over_experts(dve, body)

            @block.scalar
            def _(act):
                act.preload_act_table(ACT.Gelu)
                act.sem_inc(h_read, HB // 2)

                def store(n, par):
                    act.wait_ge(y_read, n + 2)
                    act.dma_start(t.y_rows[ds(n * MT, MT), :].rearrange("(s p) f -> p s f", p=128), y[par][:, :, :]
                                  ).then_inc(y_out[par], 16)

                def gelus(n, par):
                    act.wait_ge(small_ready, n + 1)
                    for b in range(HB):
                        if b % 2 == 0:
                            act.wait_ge(h_ready, n * (HB // 2) + b // 2 + 1)
                        gelu = act.activation(hT[par][:, b, :], h_ps[:, b, :], ACT.Gelu, bias=small[par][:, b:b + 1])
                        if b % 2:
                            gelu.then_inc(h_read, 1)

                def body(n, par, i, last):
                    if not last:
                        gelus(n + 1, 1 - par)
                    store(n, par)
                gelus(0, 0)
                over_experts(act, body)
                for par in range(2):
                    act.wait_ge(y_out[par], NMT // 2 * 16)

            @block.tensor
            def _(pe):
                def turn(n, par, i):
                    pe.wait_ge(x_in[par], i * 16 + 16)
                    for half in range(2):
                        for k in range(FC):
                            mm = pe.transpose(turn_ps[par][:, k, half * 128:(half + 1) * 128], xr[par][:, half, k * 128:(k + 1) * 128],
                                              t.ident[:, :])
                    mm.then_inc(turned, 1)

                def body(n, par, i, last):
                    if not last:
                        turn(n + 1, 1 - par, i + par)
                    pe.wait_ge(w1_in[par], i * 16 + 16)
                    pe.wait_ge(xT_ready, n + 1)
                    for b in range(HB):
                        if b % 2 == 0:
                            pe.wait_ge(h_read, n * (HB // 2) + b // 2 + 1)
                        for k in range(FC):
                            mm = pe.matmul(h_ps[:, b, :], w1[par][:, k, b * 128:(b + 1) * 128], xT[par][:, k, :],
                                           start=(k == 0), stop=(k == FC - 1))
                        if b % 2:
                            mm.then_inc(h_ready, 1)
                    pe.wait_ge(w2_in[par], i * 16 + 16)
                    pe.wait_ge(y_read, n + 1)
                    for b in range(HB):
                        if b % 2 == 0:
                            pe.wait_ge(h_read, (n + 1) * (HB // 2) + b // 2 + 1)
                        for half in range(2):
                            mm = pe.matmul(y_ps[:, half, 0:F], hT[par][:, b, half * 128:(half + 1) * 128], w2[par][:, b, :],
                                           start=(b == 0), stop=(b == HB - 1))
                    mm.then_inc(y_ready, 1)
                turn(0, 0, 0)
                over_experts(pe, body)

        with Memory(nc) as s:
            idx = [s.sb(f"c_idx{j}", [TP, 2], I32) for j in range(U)]
            got = [[s.sb(f"got{c}{j}", [TP, F]) for c in range(2)] for j in range(U)]
            part = [[s.sb(f"part{c}{j}", [TP, F]) for c in range(2)] for j in range(U)]
            res = [s.sb(f"res{j}", [TP, F]) for j in range(U)]
            got_in, res_out = s.gather_sems("got_in", U), s.sems("res_out", U)
            idx_ready, used, part_order, carrier, a_carrier = (
                s.sem("c_" + x) for x in ("idx", "used", "order", "carrier", "a_carrier"))
            block = s.block()

            @block.scalar
            def _(act):
                def body(u, j, i, last):
                    act.wait_ge(used, u + 1)
                    act.sem_inc(a_carrier, 1)
                    act.activation(idx[j][:, :], pos[:, u, :], ACT.Copy).then_inc(idx_ready, 1)
                over_tiles(act, body)

            @block.gpsimd
            def _(pool):
                def body(u, j, i, last):
                    pool.wait_ge(idx_ready, u + 1)
                    pool.sem_inc(carrier, 1)
                    for c in range(2):
                        pool.indirect_dma_start(out=got[j][c][:, :], out_offset=None, in_=t.y_rows,
                                                in_offset=bass.IndirectOffsetOnAxis(ap=idx[j][:, c:c + 1], axis=0)
                                                ).then_inc(got_in[j], 16)
                over_tiles(pool, body)

            @block.vector
            def _(dve):
                dve.sem_inc(used, U)

                def body(u, j, i, last):
                    order = Order(dve, part_order, u * 2)
                    dve.wait_ge(got_in[j], i * 32 + 32)
                    order(dve.tensor_scalar(part[j][0][:, :], got[j][0][:, :], weight[:, 0, ds(u, 1)], None, ALU.mult))
                    order(dve.scalar_tensor_tensor(part[j][1][:, :], got[j][1][:, :], weight[:, 1, ds(u, 1)], part[j][0][:, :],
                                                   ALU.mult, ALU.add))
                    wait(dve, res_out[j], i * 16)
                    dve.tensor_tensor(res[j][:, :], part[j][1][:, :], t.x_all[:, u, :], ALU.add).then_inc(used, 1)
                over_tiles(dve, body)

            @block.sync
            def _(sp):
                def body(u, j, i, last):
                    sp.wait_ge(used, u + 1 + U)
                    sp.dma_start(out[ds(u * TP, TP), :], res[j][:, :]).then_inc(res_out[j], 16)
                over_tiles(sp, body)
                for j in range(U):
                    sp.wait_ge(res_out[j], NT // U * 16)


def build(nc, a, out):
    def dram(name, shape, dt=F32):
        return nc.dram_tensor(name, shape, dt, kind="Internal").ap()

    t = Shared()
    t.k_tab, t.v_tab = dram("k_tab", (N, F)), dram("v_tab", (N, F))
    t.mix_qkv = dram("mix_qkv", (N, 3 * F))
    t.dst_pad, t.src_pad = dram("dst_pad", (E_PAD + 2,), I32), dram("src_pad", (E_PAD + 2,), I32)
    t.e_dram, t.ex_dram = dram("e_dram", (HG, E_PAD)), dram("ex_dram", (HG, E_PAD))
    t.x_rows, t.y_rows = dram("x_rows", (ROWS, F)), dram("y_rows", (ROWS, F))
    with Memory(nc) as m:
        t.x_all = m.sb("x_all", [TP, NT, F])
        t.xn_all = m.sb("xn_all", [TP, NT, F])
        t.ident, t.identb = m.sb("ident", [128, 128]), m.sb("identb", [128, 128], BF16)
        t.ones = m.sb("ones", [128, 128])
        t.wproj = m.sb("wproj", [128, FC, F])
        t.logits = m.sb("logits", [TP, NT, NEX])
        t.x_mean, t.x_rstd = m.sb("x_mean", [TP, NT]), m.sb("x_rstd", [TP, NT])
        t.z_mean, t.z_rstd = m.sb("z_mean", [TP, NT]), m.sb("z_rstd", [TP, NT])
        with Memory(nc) as e:
            t.iota_n = e.sb("iota_n", [128, N])
            t.win_node = e.sb("win_node", [TP, NT])
            t.dst_all = e.sb("dst_all", [128, G_PAD, EJ])
            t.src_all = e.sb("src_all", [128, G_PAD, EJ], I32)
            t.step_g = e.sb("step_g", [1, N_STEPS], I32)
            t.step_w = e.sb("step_w", [1, N_STEPS], I32)
            t.step_slot = e.sb("step_slot", [1, N_STEPS], I32)
            t.need_steps = e.sb("need_steps", [1, N_GROUPS], I32)
            t.e_all = e.sb("e_all", [128, HG, ET_PAD])
            t.e_flat = t.e_all[:, :, :].rearrange("p h t -> p (h t)")
            with Memory(nc) as q:
                t.q3 = q.sb("q3", [TP, NT, 3 * F], BF16)
                stage_project(nc, a, t)
                stage_scores(nc, a, t)
            stage_edge_softmax(nc, a, t)
            stage_mix(nc, a, t)
            t.acc = e.sb("acc", [TP, NT, F + HG])
            stage_aggregate(nc, a, t)
            stage_graph_ffn(nc, a, t)
        stage_experts(nc, a, t, out)


_INS = ["x", "src", "dst", "L0_gnn_Wq", "L0_gnn_Wk", "L0_gnn_Wv", "L0_gnn_ln_g", "L0_gnn_ln_b", "L0_gnn_W1", "L0_gnn_b1",
        "L0_gnn_alpha", "L0_gnn_W2", "L0_gnn_b2", "L0_mix_Wqkv", "L0_mix_bqkv", "L0_mix_Wproj", "L0_mix_bproj",
        "L0_mix_temperature", "L0_ffn_Wr", "L0_ffn_br", "L0_ffn_ln_g", "L0_ffn_ln_b", "L0_ffn_W1", "L0_ffn_b1",
        "L0_ffn_W2", "L0_ffn_b2"]


def constants():
    f32 = np.float32
    i, j = np.triu_indices(DM, 1)
    pair = np.zeros((DM, NPAIR), f32)
    pair[i, np.arange(NPAIR)] = 1
    pair[j, np.arange(NPAIR)] = 1
    low = pair.astype(mybir.dt.np(BF16))
    tail = np.zeros((2, E_PAD + 1 - EDGES), np.int32)
    tail[0] = PAD_DST
    tail[0, -1] = -2
    keep = np.ones((NEX, NT), f32)
    keep[:, 0] = 0
    return {
        "c_ident": np.eye(128, dtype=f32), "c_identb": np.eye(128).astype(low.dtype),
        "c_iota": np.arange(N, dtype=f32)[None, :],
        "c_win_node": (np.arange(NT)[None, :] * TP + np.arange(TP)[:, None]).astype(f32),
        "c_win_end": ((np.arange(NT)[:, None] + 1) * TP).astype(f32), "c_win_id": np.arange(NT, dtype=f32)[:, None],
        "c_count": np.arange(N_STEPS, dtype=f32)[None, :],
        "c_head": np.array([[-1], [0]], np.int32), "c_tail": tail,
        "c_pair3": np.concatenate([low] * 3), "c_pair4": np.concatenate([pair] * 4),
        "c_pairT": np.ascontiguousarray(pair.T.reshape(NPB, PB, DM).transpose(1, 0, 2)),
        "c_before": np.tri(NEX, k=-1, dtype=f32).reshape(1, -1), "c_keep": keep.reshape(1, -1),
        "c_tri": np.triu(np.ones((TP, TP), f32), 1), "c_tile_at": (np.arange(NMT) * MT).astype(f32)[None, :],
    }


def kernel(**inputs):
    import concourse.bacc as bacc
    from concourse.bass_utils import run_bass_kernel_spmd

    nc = bacc.Bacc("TRN2", target_bir_lowering=False, num_devices=1)
    arrays = {name: np.ascontiguousarray(inputs[name]) for name in _INS}
    arrays.update(constants())
    aps = {name: nc.dram_tensor(name, x.shape, mybir.dt.from_np(x.dtype), kind="ExternalInput").ap() for name, x in arrays.items()}
    out = nc.dram_tensor("out", (N, F), F32, kind="ExternalOutput").ap()
    build(nc, aps, out)
    result = run_bass_kernel_spmd(nc, [arrays], core_ids=[0])
    return result.results[0]["out"]
```

```python
from contextlib import ExitStack

import numpy as np

import concourse.bass as bass
from concourse import mybir

F32 = mybir.dt.float32
BF16 = mybir.dt.bfloat16
I32 = mybir.dt.int32
ALU = mybir.AluOpType
ACT = mybir.ActivationFunctionType
AX = mybir.AxisListType
ds = bass.ds

N = 3125
F = 256
FC = F // 128
TP = 125
NT = N // TP
U = 5
HG = 4
DG = F // HG
HM = 8
DM = F // HM
NPAIR = DM * (DM - 1) // 2
PB = 124
NPB = NPAIR // PB
V1 = DM + 1
EDGES = 2 * 50000 + N
EJ = 4
GE = EJ * 128
N_GROUPS = -(-EDGES // GE)
G_PAD = 208
E_PAD = G_PAD * GE
ET_PAD = G_PAD * EJ
N_STEPS = N_GROUPS + NT - 1
KR = 4
CHUNKS = 32
CE = E_PAD // CHUNKS
SLOTS = N_STEPS // NT
HW = HM // 2 * V1
NEX = 8
HID = 4 * F
HB = HID // 128
MT = 256
NMT = (2 * N + NEX * (MT - 1)) // MT
ROWS = NMT * MT
BIG = 1e30
EPS = 1e-5
SCALE = float(DM) ** 0.25
PAD_DST = 4000


class Shared:
    pass


class Order:

    def __init__(self, eng, sem, base=0):
        self.eng, self.sem, self.base, self.n = eng, sem, base, 0

    def __call__(self, ins):
        ins.then_inc(self.sem, 1)
        self.n += 1
        self.eng.wait_ge(self.sem, self.base + self.n)


def bcast(ap, *shape):
    return ap.broadcast_to(list(shape))


def over_tiles(eng, body, n=NT, unroll=U):
    rounds = n // unroll
    for j in range(unroll):
        body(j, j, 0, False)
    with eng.Fori(1, rounds - 1) as i:
        for j in range(unroll):
            body(i * unroll + j, j, i, False)
    for j in range(unroll):
        body((rounds - 1) * unroll + j, j, rounds - 1, j == unroll - 1)


def wait(eng, sem, value):
    if not isinstance(value, int) or value > 0:
        eng.wait_ge(sem, value)


def psum_turn(u, j):
    return u if j == 0 else u - 1


class Memory:

    def __init__(self, nc):
        self.nc, self.stack, self.held = nc, ExitStack(), []

    def __enter__(self):
        self.stack.__enter__()
        return self

    def __exit__(self, *e):
        self.stack.__exit__(*e)
        for sem in self.held:
            self.nc.gpsimd.sem_clear(sem)
            self.nc.release_semaphore(sem)

    def sb(self, name, shape, dt=F32):
        return self.stack.enter_context(self.nc.sbuf_tensor(name, list(shape), dt))

    def ps(self, name, shape, dt=F32):
        return self.stack.enter_context(self.nc.psum_tensor(name, list(shape), dt))

    def sem(self, name):
        self.held.append(self.nc.alloc_semaphore(name))
        return self.held[-1]

    def gather_sems(self, name, n):
        return [self.nc.alloc_semaphore(f"{name}{i}") for i in range(n)]

    def sems(self, name, n):
        return [self.sem(f"{name}{i}") for i in range(n)]

    def block(self):
        return self.stack.enter_context(self.nc.Block())


def finish_stats(dve, order, st, mean, var, tmp):
    m_even, m_odd, q_even, q_odd = (st[:, :, i] for i in (1, 4, 2, 5))
    order(dve.tensor_tensor(tmp[:, 0, :], m_even, m_odd, ALU.add))
    order(dve.tensor_scalar(mean[:, :], tmp[:, 0, :], 0.5, None, ALU.mult))
    order(dve.tensor_tensor(tmp[:, 1, :], m_even, m_odd, ALU.subtract))
    order(dve.tensor_tensor(tmp[:, 2, :], tmp[:, 1, :], tmp[:, 1, :], ALU.mult))
    order(dve.tensor_tensor(tmp[:, 3, :], q_even, q_odd, ALU.add))
    order(dve.tensor_scalar(tmp[:, 4, :], tmp[:, 3, :], 1.0 / F, EPS, ALU.mult, ALU.add))
    return dve.scalar_tensor_tensor(var[:, :], tmp[:, 2, :], 0.25, tmp[:, 4, :], ALU.mult, ALU.add)


def stage_project(nc, a, t):
    with Memory(nc) as m:
        wall = m.sb("wall", [128, FC, 6 * F])
        mix_bias = m.sb("mix_bias", [TP, 3 * F])
        mean, rstd = m.sb("mean", [TP, NT]), m.sb("rstd", [TP, NT])

        with Memory(nc) as s:
            wst = s.sb("wst", [128, 6, F])
            wpst = s.sb("wpst", [128, FC, F])
            edge_i = s.sb("edge_i", [G_PAD // 2, 2, 2, GE], I32)
            edge_f = s.sb("edge_f", [G_PAD // 2, 2, 2, GE])
            zeros = s.sb("zeros", [128, 4096])
            st, var = s.sb("st", [TP, NT, 6]), s.sb("var", [TP, NT])
            std, tmp = s.sb("std", [TP, NT]), s.sb("tmp", [TP, 5, NT])
            first_dst = s.sb("first_dst", [1, N_GROUPS])
            win_end = s.sb("win_end", [NT, 1])
            win_id = s.sb("win_id", [NT, 1])
            count = s.sb("count", [1, N_STEPS])
            before = s.sb("before", [NT, N_GROUPS])
            last_group = s.sb("last_group", [NT, 3])
            passed = s.sb("passed", [NT, N_STEPS])
            count_w = s.sb("count_w", [NT, N_STEPS])
            row = s.sb("row", [1, 3, N_STEPS])
            tp = [s.ps(f"tp{i}", [128, 512]) for i in range(4)]
            first_ps = s.ps("first_ps", [NT, N_GROUPS])
            step_ps = s.ps("step_ps", [1, N_STEPS])
            group_ps = s.ps("group_ps", [1, N_GROUPS])
            x_in, w_in, c_in, pad_in, zero_out = s.sem("x_in"), s.sem("w_in"), s.sem("c_in"), s.sem("pad_in"), s.sem("zero_out")
            edge_in = s.sem("edge_in")
            memsets, edge_float, turned, drained = s.sem("memsets"), s.sem("edge_float"), s.sem("turned"), s.sem("drained")
            stats_done = s.sem("stats_done0")
            dve_order, var_ready, std_ready = s.sem("dve_order"), s.sem("var_ready"), s.sem("std_ready")
            first_row, firsts, before_ready, passed_ready, steps_ready = (
                s.sem(x) for x in ("first_row", "firsts", "before_ready", "passed_ready", "steps_ready"))
            banks = []
            for kind in range(2):
                for half in range(2):
                    banks.append(("edge", kind, half))
            for k in range(FC):
                for third in range(2):
                    banks.append(("mix", k, third))
            for k in range(FC):
                banks.append(("proj", k, 0))
            block = s.block()

            @block.sync
            def _(sp):
                for kind, (pad, given) in enumerate(((t.dst_pad, a["dst"]), (t.src_pad, a["src"]))):
                    sp.dma_start(pad[1:1 + EDGES].rearrange("(p c) -> p c", p=TP),
                                 given.rearrange("(p c) -> p c", p=TP)).then_inc(pad_in, 16)
                    sp.dma_start(pad[0:1].rearrange("(p c) -> p c", p=1),
                                 a["c_head"][kind:kind + 1, :]).then_inc(pad_in, 16)
                    sp.dma_start(pad[1 + EDGES:].rearrange("(p c) -> p c", p=1),
                                 a["c_tail"][kind:kind + 1, :]).then_inc(pad_in, 16)
                sp.dma_start(t.x_all[:, :, :], a["x"].rearrange("(t p) f -> p t f", p=TP)).then_inc(x_in, 16)
                for name, ap in (("c_ident", t.ident), ("c_identb", t.identb), ("c_win_node", t.win_node),
                                 ("c_win_end", win_end), ("c_win_id", win_id), ("c_count", count)):
                    sp.dma_start(ap[:, :], a[name]).then_inc(c_in, 16)
                sp.dma_start(count_w[:, :], a["c_count"][0, :].partition_broadcast(NT)).then_inc(c_in, 16)
                sp.dma_start(t.iota_n[:, :], a["c_iota"][0, :].partition_broadcast(128)).then_inc(c_in, 16)
                sp.wait_ge(pad_in, 6 * 16)
                for kind, pad in enumerate((t.dst_pad, t.src_pad)):
                    sp.dma_start(edge_i[:, kind, :, :],
                                 pad[1:1 + E_PAD].rearrange("(h g c) -> g h c", h=2, c=GE)).then_inc(edge_in, 16)
                sp.wait_ge(memsets, 2)
                for i in range(ROWS * F // (128 * 4096)):
                    sp.dma_start(t.x_rows.rearrange("(i p r) f -> i p (r f)", p=128, r=4096 // F)[i],
                                 zeros[:, :]).then_inc(zero_out, 16)
                sp.wait_ge(zero_out, ROWS * F // (128 * 4096) * 16)

            @block.gpsimd
            def _(pool):
                pool.memset(t.ones[:, :], 1.0).then_inc(memsets, 1)
                pool.memset(zeros[:, :], 0.0).then_inc(memsets, 1)

            @block.scalar
            def _(act):
                act.dma_start(wst[:, :, :], a["L0_mix_Wqkv"].rearrange("(o p) f -> p o f", p=128)).then_inc(w_in, 16)
                act.dma_start(wpst[:, :, :], a["L0_mix_Wproj"].rearrange("(o p) f -> p o f", p=128)).then_inc(w_in, 16)
                for i, name in enumerate(("L0_gnn_Wq", "L0_gnn_Wk", "L0_gnn_Wv")):
                    act.dma_start(wall[:, :, i * F:(i + 1) * F],
                                  a[name].rearrange("(k p) n -> p k n", p=128)).then_inc(w_in, 16)
                act.dma_start(mix_bias[:, :], a["L0_mix_bqkv"].partition_broadcast(TP)).then_inc(w_in, 16)
                act.wait_ge(var_ready, 1)
                act.activation(std[:, :], var[:, :], ACT.Sqrt).then_inc(std_ready, 1)
                act.wait_ge(w_in, 6 * 16)

            @block.tensor
            def _(pe):
                pe.wait_ge(c_in, 8 * 16)
                for i, (what, b, c) in enumerate(banks):
                    if i >= 4:
                        pe.wait_ge(drained, i - 3)
                    if what == "edge":
                        pe.wait_ge(edge_float, 1 + b)
                        for j in range(EJ):
                            last = pe.transpose(tp[i % 4][:, j * 104:(j + 1) * 104],
                                                edge_f[:, b, c, j * 128:(j + 1) * 128], t.ident[0:104, 0:104])
                    elif what == "mix":
                        pe.wait_ge(w_in, 6 * 16)
                        for j in range(3):
                            last = pe.transpose(tp[i % 4][:, j * 128:(j + 1) * 128],
                                                wst[:, 3 * c + j, b * 128:(b + 1) * 128], t.ident[:, :])
                    else:
                        for j in range(2):
                            last = pe.transpose(tp[i % 4][:, j * 128:(j + 1) * 128],
                                                wpst[:, j, b * 128:(b + 1) * 128], t.ident[:, :])
                    last.then_inc(turned, 1)
                pe.wait_ge(memsets, 1)
                pe.wait_ge(first_row, 1)
                pe.matmul(first_ps[:, :], t.ones[0:1, 0:NT], first_dst[:, :], start=True, stop=True).then_inc(firsts, 1)
                pe.wait_ge(before_ready, 1)
                pe.matmul(group_ps[:, :], t.ones[0:NT, 0:1], before[:, :], start=True, stop=True)
                pe.wait_ge(passed_ready, 1)
                pe.matmul(step_ps[:, :], t.ones[0:NT, 0:1], passed[:, :], start=True, stop=True).then_inc(steps_ready, 1)

            @block.vector
            def _(dve):
                order = Order(dve, dve_order)
                dve.wait_ge(edge_in, 32)
                for kind in range(2):
                    dve.tensor_copy(edge_f[:, kind, :, :], edge_i[:, kind, :, :]).then_inc(edge_float, 1)
                dve.wait_ge(x_in, 16)
                with dve.Fori(0, NT) as u:
                    dve.bn_stats(st[:, u, :], t.x_all[:, u, :]).then_inc(stats_done, 1)
                for i, (what, b, c) in enumerate(banks):
                    dve.wait_ge(turned, i + 1)
                    if what == "edge":
                        to = (t.dst_all, t.src_all)[b][:, c * 104:(c + 1) * 104, :]
                        src = tp[i % 4][:, 0:EJ * 104].rearrange("p (j g) -> p g j", j=EJ)
                    elif what == "mix":
                        at = 3 * F + 3 * c * 128
                        to, src = wall[:, b, at:at + 384], tp[i % 4][:, 0:384]
                    else:
                        to, src = t.wproj[:, b, :], tp[i % 4][:, 0:F]
                    dve.tensor_copy(to, src).then_inc(drained, 1)
                dve.wait_ge(drained, len(banks))
                dve.wait_ge(stats_done, NT)
                finish_stats(dve, order, st, mean, var, tmp).then_inc(var_ready, 1)
                dve.tensor_copy(first_dst[:, :], t.dst_all[0:1, 0:N_GROUPS, 0]).then_inc(first_row, 1)
                dve.wait_ge(firsts, 1)
                order(dve.tensor_scalar(before[:, :], first_ps[:, :], win_end[:, :], None, ALU.is_lt))
                dve.sem_inc(before_ready, 1)
                order(dve.tensor_reduce(last_group[:, 0:1], before[:, :], AX.X, ALU.add))
                order(dve.tensor_scalar(last_group[:, 1:2], last_group[:, 0:1], -1.0, 0.0, ALU.add, ALU.max))
                order(dve.tensor_tensor(last_group[:, 2:3], last_group[:, 1:2], win_id[:, :], ALU.add))
                order(dve.tensor_scalar(passed[:, :], count_w[:, :], last_group[:, 2:3], None, ALU.is_gt))
                dve.sem_inc(passed_ready, 1)
                dve.wait_ge(steps_ready, 1)
                order(dve.tensor_copy(row[:, 0, :], step_ps[:, :]))
                order(dve.tensor_tensor(row[:, 1, :], count[:, :], row[:, 0, :], ALU.subtract))
                order(dve.tensor_copy(t.step_w[:, :], row[:, 0, :]))
                order(dve.tensor_copy(t.step_g[:, :], row[:, 1, :]))
                order(dve.tensor_scalar(t.step_slot[:, :], t.step_g[:, :], KR - 1, None, ALU.bitwise_and))
                order(dve.tensor_scalar(row[:, 2, 0:N_GROUPS], group_ps[:, :], -1.0, float(NT + 1),
                                        ALU.mult, ALU.add))
                order(dve.tensor_tensor(row[:, 2, 0:N_GROUPS], row[:, 2, 0:N_GROUPS], count[:, 0:N_GROUPS], ALU.add))
                order(dve.memset(t.need_steps[:, 0:KR], 0))
                order(dve.tensor_copy(t.need_steps[:, KR:], row[:, 2, 1:N_GROUPS - KR + 1]))
                dve.wait_ge(std_ready, 1)
                order(dve.reciprocal(rstd[:, :], std[:, :]))

        with Memory(nc) as s:
            xn_t = [s.sb(f"xn_t{j}", [TP, F]) for j in range(U)]
            xnT = [s.sb(f"xnT{j}", [128, FC, TP]) for j in range(U)]
            kv_t = [s.sb(f"kv_t{j}", [TP, 2 * F]) for j in range(U)]
            mix_t = [s.sb(f"mix_t{j}", [TP, 3 * F]) for j in range(U)]
            q3_t = [s.sb(f"q3_t{j}", [TP, 3, F], BF16) for j in range(U)]
            rest = [s.sb(f"rest{j}", [TP, F]) for j in range(U)]
            turn_ps = [s.ps(f"turn_ps{i}", [128, FC, TP]) for i in range(2)]
            proj_ps = [s.ps(f"proj_ps{i}", [128, 6 * F]) for i in range(2)]
            xn_ready, turned, xnT_ready, proj_ready = (
                s.sem(x) for x in ("xn_ready", "turned", "xnT_ready", "proj_ready"))
            kv_ready, hi_ready, rest_ready, mid_ready, q3_ready, mix_ready = (
                s.sem(x) for x in ("kv_ready", "hi_ready", "rest_ready", "mid_ready", "q3_ready", "mix_ready"))
            xn_out, kv_out, q3_out, mix_out = (s.sems(x, U) for x in ("xn_out", "kv_out", "q3_out", "mix_out"))
            block = s.block()

            @block.sync
            def _(sp):
                def body(u, j, i, last):
                    sp.wait_ge(xn_ready, u + 1)
                    sp.dma_start(t.xn_all[:, u, :], xn_t[j][:, :]).then_inc(xn_out[j], 16)
                    sp.wait_ge(kv_ready, u + 1)
                    sp.dma_start(t.k_tab[ds(u * TP, TP), :], kv_t[j][:, 0:F]).then_inc(kv_out[j], 16)
                    sp.dma_start(t.v_tab[ds(u * TP, TP), :], kv_t[j][:, F:2 * F]).then_inc(kv_out[j], 16)
                    sp.wait_ge(mix_ready, u + 1)
                    sp.dma_start(t.mix_qkv[ds(u * TP, TP), :], mix_t[j][:, :]).then_inc(mix_out[j], 16)
                    sp.wait_ge(q3_ready, u + 1)
                    sp.dma_start(t.q3[:, u, :], q3_t[j][:, :, :].rearrange("p a f -> p (a f)")).then_inc(q3_out[j], 16)
                over_tiles(sp, body)
                for j in range(U):
                    for s_, per in ((xn_out, 16), (kv_out, 32), (q3_out, 16), (mix_out, 16)):
                        sp.wait_ge(s_[j], per * (NT // U))

            @block.vector
            def _(dve):
                def normalise(u, j, i):
                    wait(dve, xn_out[j], i * 16)
                    dve.tensor_scalar(xn_t[j][:, :], t.x_all[:, u, :], mean[:, ds(u, 1)], rstd[:, ds(u, 1)],
                                      ALU.subtract, ALU.mult).then_inc(xn_ready, 1)

                def body(u, j, i, last):
                    if not last:
                        normalise(u + 1, (j + 1) % U, i + (j + 1) // U)
                    dve.wait_ge(hi_ready, u + 1)
                    dve.tensor_tensor(rest[j][:, :], proj_ps[j % 2][0:TP, 0:F], q3_t[j][:, 0, :],
                                      ALU.subtract).then_inc(rest_ready, 1)
                    wait(dve, mix_out[j], i * 16)
                    dve.tensor_tensor(mix_t[j][:, :], proj_ps[j % 2][0:TP, 3 * F:6 * F], mix_bias[:, :],
                                      ALU.add).then_inc(mix_ready, 1)
                    dve.wait_ge(mid_ready, u + 1)
                    dve.tensor_tensor(q3_t[j][:, 2, :], rest[j][:, :], q3_t[j][:, 1, :],
                                      ALU.subtract).then_inc(q3_ready, 1)
                normalise(0, 0, 0)
                over_tiles(dve, body)

            @block.scalar
            def _(act):
                def turn_out(u, j):
                    act.wait_ge(turned, u + 1)
                    act.activation(xnT[j][:, :, :], turn_ps[j % 2][:, :, :], ACT.Copy).then_inc(xnT_ready, 1)

                def body(u, j, i, last):
                    if not last:
                        turn_out(u + 1, (j + 1) % U)
                    wait(act, kv_out[j], i * 32)
                    act.wait_ge(proj_ready, u + 1)
                    act.activation(kv_t[j][:, :], proj_ps[j % 2][0:TP, F:3 * F], ACT.Copy).then_inc(kv_ready, 1)
                    wait(act, q3_out[j], i * 16)
                    act.activation(q3_t[j][:, 0, :], proj_ps[j % 2][0:TP, 0:F], ACT.Copy).then_inc(hi_ready, 1)
                    act.wait_ge(rest_ready, u + 1)
                    act.activation(q3_t[j][:, 1, :], rest[j][:, :], ACT.Copy).then_inc(mid_ready, 1)
                turn_out(0, 0)
                over_tiles(act, body)

            @block.tensor
            def _(pe):
                def turn(u, j):
                    pe.wait_ge(xn_ready, u + 1)
                    wait(pe, xnT_ready, psum_turn(u, j))
                    for k in range(FC):
                        last = pe.transpose(turn_ps[j % 2][:, k, :], xn_t[j][:, k * 128:(k + 1) * 128],
                                            t.ident[0:TP, 0:TP])
                    last.then_inc(turned, 1)

                def body(u, j, i, last):
                    if not last:
                        turn(u + 1, (j + 1) % U)
                    pe.wait_ge(xnT_ready, u + 1)
                    wait(pe, mix_ready, psum_turn(u, j))
                    for k in range(FC):
                        for b in range(3):
                            mm = pe.matmul(proj_ps[j % 2][0:TP, b * 512:(b + 1) * 512], xnT[j][:, k, :],
                                           wall[:, k, b * 512:(b + 1) * 512], start=(k == 0), stop=(k == FC - 1))
                    mm.then_inc(proj_ready, 1)
                turn(0, 0)
                over_tiles(pe, body)


class Unit:

    def __init__(self, s, name, loaded, src, grow, factor):
        self.loaded, self.src, self.grow, self.factor = loaded, src, grow, factor
        self.sq = [s.sb(f"{name}_sq{j}", [TP, F]) for j in range(2)]
        self.nrm = [s.sb(f"{name}_nrm{j}", [TP, 5, HM]) for j in range(2)]
        self.unit = [s.sb(f"{name}_unit{j}", [TP, F]) for j in range(2)]
        self.rest = [s.sb(f"{name}_rest{j}", [TP, F]) for j in range(2)]
        self.parts = [s.sb(f"{name}_parts{j}", [TP, HM, 3, DM], BF16) for j in range(2)]
        self.turned_parts = [s.sb(f"{name}_T{j}", [3 * DM, HM, 128], BF16) for j in range(2)]
        self.turn_ps = s.ps(f"{name}_turn_ps", [3 * DM, HM, 128], BF16)
        (self.order, self.squared, self.rooted, self.scaled, self.rounded, self.rest_ready, self.middle, self.split,
         self.turned, self.ready) = (s.sem(f"{name}_{x}") for x in (
             "order", "squared", "rooted", "scaled", "rounded", "rest_ready", "middle", "split", "turned", "ready"))

    def heads(self, ap):
        return ap.rearrange("p (h d) -> p h d", h=HM)

    def dve_squares(self, dve, u, j, i):
        order = Order(dve, self.order, u * 4)
        dve.wait_ge(self.loaded[j], i * 16 + 16)
        order(dve.tensor_tensor(self.sq[j][:, :], self.src(j), self.src(j), ALU.mult))
        order(dve.tensor_reduce(self.nrm[j][:, 0, :], self.heads(self.sq[j][:, :]), AX.X, ALU.add))
        dve.tensor_scalar(self.nrm[j][:, 1, :], self.nrm[j][:, 0, :], self.grow, 1e-24, ALU.mult, ALU.max
                          ).then_inc(self.squared, 1)

    def act_root(self, act, u, j):
        act.wait_ge(self.squared, u + 1)
        act.activation(self.nrm[j][:, 2, :], self.nrm[j][:, 1, :], ACT.Sqrt).then_inc(self.rooted, 1)

    def dve_scale(self, dve, u, j):
        order = Order(dve, self.order, u * 4 + 2)
        dve.wait_ge(self.rooted, u + 1)
        order(dve.reciprocal(self.nrm[j][:, 3, :], self.nrm[j][:, 2, :]))
        order(dve.tensor_tensor(self.nrm[j][:, 4, :], self.nrm[j][:, 3, :], self.factor, ALU.mult))
        dve.tensor_tensor(self.heads(self.unit[j][:, :]), self.heads(self.src(j)),
                          bcast(self.nrm[j][:, 4, :].unsqueeze(2), TP, HM, DM), ALU.mult).then_inc(self.scaled, 1)

    def act_round(self, act, u, j):
        act.wait_ge(self.scaled, u + 1)
        act.activation(self.parts[j][:, :, 0, :], self.heads(self.unit[j][:, :]), ACT.Copy).then_inc(self.rounded, 1)

    def dve_rest(self, dve, u, j):
        dve.wait_ge(self.rounded, u + 3)
        dve.tensor_tensor(self.heads(self.rest[j][:, :]), self.heads(self.unit[j][:, :]), self.parts[j][:, :, 0, :],
                          ALU.subtract).then_inc(self.rest_ready, 1)

    def act_middle(self, act, u, j):
        act.wait_ge(self.rest_ready, u + 1)
        act.activation(self.parts[j][:, :, 1, :], self.heads(self.rest[j][:, :]), ACT.Copy).then_inc(self.middle, 1)

    def dve_last(self, dve, u, j):
        dve.wait_ge(self.middle, u + 1)
        dve.tensor_tensor(self.parts[j][:, :, 2, :], self.heads(self.rest[j][:, :]), self.parts[j][:, :, 1, :],
                          ALU.subtract).then_inc(self.split, 1)

    def pe_turn(self, pe, u, j, identb):
        pe.wait_ge(self.split, u + 1)
        wait(pe, self.ready, u)
        for h in range(HM):
            mm = pe.transpose(self.turn_ps[:, h, 0:TP], self.parts[j][:, h, :, :].rearrange("p a d -> p (a d)"),
                              identb[0:TP, 0:TP])
        return mm

    def act_turn_out(self, act, u, j):
        act.wait_ge(self.turned, u + 1)
        act.activation(self.turned_parts[j][:, :, 0:TP], self.turn_ps[:, :, 0:TP], ACT.Copy).then_inc(self.ready, 1)


def over_slots(eng, body):
    def round_(i, count):
        for c in range(count):
            body(i * 2 + c // SLOTS, c // SLOTS % 2, c % SLOTS, i * 2 * SLOTS + c, c, i)
    round_(0, 2 * SLOTS)
    with eng.Fori(1, NT // 2) as i:
        round_(i, 2 * SLOTS)
    round_(NT // 2, SLOTS + 1)


def within(x, count):
    return not isinstance(x, int) or x < count


def load_step(eng, table, s, most):
    return eng.value_load(table[0:1, ds(s, 1)], min_val=0, max_val=most)


def gather_program(pool, t, table, ring, idx, carrier, idx_ready, landed_slot, landed, steps_done):
    def place(g, slot, i):
        wait(pool, landed_slot[slot], i * 16 * EJ)
        pool.sem_inc(carrier, 1)
        pool.tensor_copy(idx[slot][:, :], t.src_all[:, g, :]).then_inc(idx_ready, 1)

    def fetch(g, slot, i):
        if within(g, N_GROUPS - 1):
            place(g + 1, (slot + 1) % KR, i + (slot + 1) // KR)
        need = pool.value_load(t.need_steps[0:1, ds(g, 1)], min_val=0, max_val=N_STEPS)
        pool.wait_ge(idx_ready, g + 1)
        pool.wait_ge(steps_done, need)
        pool.sem_inc(carrier, 1)
        for j in range(EJ):
            pool.indirect_dma_start(out=ring[:, slot, j, :], out_offset=None, in_=table,
                                    in_offset=bass.IndirectOffsetOnAxis(ap=idx[slot][:, j:j + 1], axis=0)
                                    ).then_inc(landed_slot[slot], 16)
        former = (slot - 1) % KR
        wait(pool, landed_slot[former], (i if slot == 0 else i + 1) * 16 * EJ)
        pool.sem_inc(landed, 1)

    place(0, 0, 0)
    for slot in range(KR):
        fetch(slot, slot, 0)
    with pool.Fori(1, N_GROUPS // KR) as i:
        for slot in range(KR):
            fetch(i * KR + slot, slot, i)
    for g in range(N_GROUPS // KR * KR, N_GROUPS):
        fetch(g, g % KR, g // KR)
    end = N_GROUPS - 1
    pool.wait_ge(landed_slot[end % KR], (end // KR + 1) * 16 * EJ)
    pool.sem_inc(landed, 1)
    pool.wait_ge(steps_done, N_STEPS + 1)


def stage_scores_and_sums(nc, a, t):
    x = t.mix
    with Memory(nc) as s:
        ring = s.sb("k_ring", [128, KR, EJ, F])
        idx = [s.sb(f"k_idx{i}", [128, EJ], I32) for i in range(KR)]
        dst_row = [s.sb(f"dst_row{i}", [TP, GE], I32) for i in range(2)]
        spread = [s.sb(f"spread{i}", [TP, GE], BF16) for i in range(2)]
        prod = s.sb("prod", [128, EJ * F])
        score = s.sb("score", [128, EJ, HG])
        q_ps = [s.ps(f"q_ps{i}", [128, EJ * F]) for i in range(2)]
        kv = [s.sb(f"kv{j}", [TP, 2 * F]) for j in range(2)]
        ksq = [s.sb(f"ksq{j}", [TP, F]) for j in range(2)]
        v1 = [s.sb(f"v1{j}", [TP, HM, V1]) for j in range(2)]
        phi = s.sb("phi", [TP, NPAIR])
        f_ps = s.ps("kf_ps", [TP, NPAIR])
        g_ps = s.ps("g_ps", [PB, NPB, V1])
        slv_ps = s.ps("slv_ps", [128, 2, HW])
        idx_ready, landed, steps_done, k_carrier = (s.sem(n) for n in ("k_idx_ready", "k_landed", "k_steps_done", "k_carrier"))
        landed_slot = s.gather_sems("k_landed_slot", KR)
        row_in = s.sems("dst_row_in", 2)
        spread_ready, q_ready, dve_order = s.sem("spread_ready"), s.sem("q_ready"), s.sem("k_dve_order")
        c_in, kv_in = s.sem("mixc_in"), s.sems("mkv_in", 2)
        ksq_ready, v1_ready, f_ready, phi_ready, g_ready, g_read, slv_ready, slv_read, cleared, start = (
            s.sem("k_" + n) for n in ("sq", "v1", "f", "phi", "g", "g_read", "slv", "slv_read", "cleared", "start"))
        k_ = Unit(s, "mk", kv_in, lambda j: kv[j][:, 0:F], 1.0, x.k_factor[:, :])
        block = s.block()

        @block.gpsimd
        def _(pool):
            gather_program(pool, t, t.k_tab, ring, idx, k_carrier, idx_ready, landed_slot, landed, steps_done)

        @block.sync
        def _(sp):
            for ap, src in ((x.pair3, a["c_pair3"]), (x.pair4, a["c_pair4"]),
                            (x.q_factor, a["L0_mix_temperature"][0, :, 0, 0].partition_broadcast(TP)),
                            (x.proj_bias, a["L0_mix_bproj"].partition_broadcast(TP))):
                sp.dma_start(ap[:, :], src).then_inc(c_in, 16)
            sp.dma_start(x.pairT[:, :, :], a["c_pairT"]).then_inc(c_in, 16)

            def load(u, j):
                sp.wait_ge(k_.rounded, u + 1)
                sp.dma_start(kv[j][:, :], t.mix_qkv[ds(u * TP, TP), F:3 * F]).then_inc(kv_in[j], 16)

            def body(u, j, k, n, c, i):
                g = load_step(sp, t.step_g, n, N_GROUPS - 1)
                wait(sp, spread_ready, n - 1)
                sp.dma_start(dst_row[c % 2][:, :], t.dst_pad[ds(g * GE + 1, GE)].partition_broadcast(TP)
                             ).then_inc(row_in[c % 2], 16)
                if k == 0 and within(u + 1, NT):
                    load(u + 1, 1 - j)
            load(0, 0)
            over_slots(sp, body)

        @block.vector
        def _(dve):
            def spread_rows(n, c, i):
                w = load_step(dve, t.step_w, n, NT - 1)
                dve.wait_ge(row_in[c % 2], (i * SLOTS + c // 2 + 1) * 16)
                dve.tensor_scalar(spread[c % 2][:, :], dst_row[c % 2][:, :], t.win_node[:, ds(w, 1)], None,
                                  ALU.is_equal).then_inc(spread_ready, 1)

            def body(u, j, k, n, c, i):
                order = Order(dve, dve_order, n * 2 + 1)
                g = load_step(dve, t.step_g, n, N_GROUPS - 1)
                slot = g & (KR - 1)
                dve.wait_ge(q_ready, n + 1)
                dve.wait_ge(landed, g + 2)
                dve.tensor_tensor(prod[:, :], ring[:, slot, :, :].rearrange("p j f -> p (j f)"), q_ps[c % 2][:, :],
                                  ALU.mult).then_inc(steps_done, 1)
                if within(n + 2, N_STEPS):
                    spread_rows(n + 2, c + 2, i)
                dve.wait_ge(steps_done, n + 2)
                dve.tensor_reduce(score[:, :, :], prod[:, :].rearrange("p (j h d) -> p j h d", j=EJ, h=HG),
                                  AX.X, ALU.add).then_inc(dve_order, 1)
                if k > 0:
                    h = k - 1
                    dve.wait_ge(g_ready, u * HM + h + 1)
                    wait(dve, g_read, u * HM + h)
                    dve.tensor_tensor(x.g_acc[:, h, :, :], x.g_acc[:, h, :, :], g_ps[:, :, :], ALU.add).then_inc(g_read, 1)
                if k % 3 == 1:
                    kind, rows = k // 3, 1 if k // 3 == 2 else 128
                    dve.wait_ge(slv_ready, u * 3 + kind + 1)
                    wait(dve, slv_read, u * 3 + kind)
                    at = x.slv_acc[0:rows, kind, :, :]
                    dve.tensor_tensor(at, at, slv_ps[0:rows, :, :], ALU.add).then_inc(slv_read, 1)
                dve.wait_ge(dve_order, n * 2 + 2)
                at = t.e_all[:, :, ds(g * EJ, EJ)]
                dve.tensor_tensor(at, at, score[:, :, :].rearrange("p j h -> p h j"), ALU.add).then_inc(dve_order, 1)
                dve.wait_ge(dve_order, n * 2 + 3)
                if within(u + 1, NT):
                    nxt = (u + 1, 1 - j)
                    if k == 0:
                        k_.dve_squares(dve, *nxt, i + j)
                    elif k == 2:
                        k_.dve_scale(dve, *nxt)
                    elif k == 4:
                        k_.dve_rest(dve, *nxt)
                    elif k == 6:
                        k_.dve_last(dve, *nxt)
            dve.memset(x.g_acc[:, :, :, :], 0.0)
            dve.memset(x.slv_acc[:, :, :, :], 0.0)
            dve.memset(x.coef[:, :, :, :], 0.0)
            dve.memset(x.k_factor[:, :], SCALE)
            for j in range(2):
                dve.memset(v1[j][:, :, 0:1], 1.0 / N)
            dve.wait_ge(c_in, 5 * 16)
            dve.tensor_scalar(x.q_factor[:, :], x.q_factor[:, :], SCALE * SCALE, None, ALU.mult).then_inc(cleared, 1)
            dve.memset(t.e_all[:, :, :], 0.0).then_inc(dve_order, 1)
            dve.sem_inc(steps_done, 1)
            spread_rows(0, 0, 0)
            spread_rows(1, 1, 0)
            dve.wait_ge(cleared, 1)
            k_.dve_squares(dve, 0, 0, 0)
            k_.dve_scale(dve, 0, 0)
            k_.dve_rest(dve, 0, 0)
            k_.dve_last(dve, 0, 0)
            dve.wait_ge(dve_order, 1)
            over_slots(dve, body)

        @block.scalar
        def _(act):
            act.preload_act_table(ACT.Sqrt)
            act.sem_inc(k_.rounded, 2)

            def round_(u, j, i):
                act.wait_ge(kv_in[j], i * 16 + 16)
                act.activation(v1[j][:, :, 1:V1], kv[j][:, F:2 * F].rearrange("p (h d) -> p h d", h=HM), ACT.Copy,
                               scale=1.0 / N).then_inc(v1_ready, 1)
                k_.act_round(act, u, j)
                act.activation(ksq[j][:, :], k_.unit[j][:, :], ACT.Square).then_inc(ksq_ready, 1)

            def body(u, j, k, n, c, i):
                if within(u, NT) and k < HM:
                    act.wait_ge(f_ready, u * HM + k + 1)
                    act.activation(phi[:, :], f_ps[:, :], ACT.Square).then_inc(phi_ready, 1)
                if within(u + 1, NT):
                    nxt = (u + 1, 1 - j)
                    if k == 1:
                        k_.act_root(act, *nxt)
                    elif k == 3:
                        round_(*nxt, i + j)
                    elif k == 5:
                        k_.act_middle(act, *nxt)
                    elif k == 8:
                        k_.act_turn_out(act, *nxt)
            act.wait_ge(cleared, 1)
            k_.act_root(act, 0, 0)
            round_(0, 0, 0)
            k_.act_middle(act, 0, 0)
            k_.act_turn_out(act, 0, 0)
            over_slots(act, body)

        @block.tensor
        def _(pe):
            def q_of_edges(n, c):
                w = load_step(pe, t.step_w, n, NT - 1)
                pe.wait_ge(spread_ready, n + 1)
                wait(pe, steps_done, n)
                for e in range(EJ):
                    for part in range(3):
                        mm = pe.matmul(q_ps[c % 2][:, e * F:(e + 1) * F], spread[c % 2][:, e * 128:(e + 1) * 128],
                                       t.q3[:, w, part * F:(part + 1) * F], start=(part == 0), stop=(part == 2))
                mm.then_inc(q_ready, 1)

            def sums(u, j, kind):
                wait(pe, slv_read, u * 3 + kind)
                rows = 1 if kind == 2 else 128
                for half in range(2):
                    lhsT = (t.ones[0:TP, 0:1] if kind == 2 else
                            (ksq[j] if kind == 0 else k_.unit[j])[:, half * 128:(half + 1) * 128])
                    mm = pe.matmul(slv_ps[0:rows, half, :], lhsT, v1[j][:, 4 * half:4 * half + 4, :].rearrange("p h e -> p (h e)"),
                                   start=True, stop=True)
                mm.then_inc(slv_ready, 1)

            def body(u, j, k, n, c, i):
                tile = within(u, NT)
                if tile and k == 0:
                    pe.wait_ge(k_.ready, u + 1)
                    pe.wait_ge(ksq_ready, u + 1)
                    pe.wait_ge(v1_ready, u + 1)
                    pe.sem_inc(start, 1)
                if tile and k < HM:
                    pe.matmul(f_ps[:, :], k_.turned_parts[j][:, k, 0:TP], x.pair3[:, :], start=True, stop=True).then_inc(f_ready, 1)
                if within(n + 1, N_STEPS):
                    q_of_edges(n + 1, c + 1)
                if tile and k % 3 == 0:
                    sums(u, j, k // 3)
                if tile and k < HM:
                    pe.wait_ge(phi_ready, u * HM + k + 1)
                    wait(pe, g_read, u * HM + k)
                    for b in range(NPB):
                        mm = pe.matmul(g_ps[:, b, :], phi[:, b * PB:(b + 1) * PB], v1[j][:, k, :], start=True, stop=True)
                    mm.then_inc(g_ready, 1)
                if k == 7 and within(u + 1, NT):
                    k_.pe_turn(pe, u + 1, 1 - j, t.identb).then_inc(k_.turned, 1)
            k_.pe_turn(pe, 0, 0, t.identb).then_inc(k_.turned, 1)
            q_of_edges(0, 0)
            over_slots(pe, body)


def stage_edge_softmax(nc, a, t):
    NB = HG * ET_PAD // 104
    NR = NB // 4
    with Memory(nc) as s:
        eT = s.sb("eT", [104, NB, 128])
        dst = s.sb("es_dst", [128, CE + 2], I32)
        pen = s.sb("pen", [128, CE + 1])
        e = s.sb("es_e", [128, CE])
        fwd, bwd = s.sb("es_fwd", [128, CE]), s.sb("es_bwd", [128, CE])
        ends = s.sb("ends", [128, 6])
        rows = s.sb("es_rows", [1, 4, 128])
        carry = s.sb("carry", [1, 2, 129])
        start = s.sb("es_start", [128, 2])
        tp = [s.ps(f"es_tp{i}", [128, 512]) for i in range(4)]
        row_ps, start_ps = s.ps("row_ps", [1, 4, 128]), s.ps("start_ps", [128, 2])
        turned, drained, e_out, e_in, dst_in = (s.sem(x) for x in ("es_turned", "es_drained", "e_out", "e_in", "es_dst_in"))
        dve_order, ends_ready, rows_ready, carry_ready, start_ready = (
            s.sem(x) for x in ("es_order", "ends_ready", "es_rows_ready", "carry_ready", "es_start_ready"))
        less_max, exp_ready, ex_out, ex_in = (s.sem(x) for x in ("less_max", "exp_ready", "ex_out", "ex_in"))
        block = s.block()

        @block.sync
        def _(sp):
            for h in range(HG):
                at = slice(h * CHUNKS, (h + 1) * CHUNKS)
                for first, col, width in ((1, 1, CE), (0, 0, 1), (CE + 1, CE + 1, 1)):
                    src = t.dst_pad[0:E_PAD] if first == 0 else t.dst_pad[1:1 + E_PAD] if first == 1 else t.dst_pad[2:2 + E_PAD]
                    src = src.rearrange("(k c) -> k c", c=CE)
                    src = src if first == 1 else src[:, 0:1] if first == 0 else src[:, CE - 1:CE]
                    sp.dma_start(dst[at, col:col + width], src, allow_slow_non_contiguous=True).then_inc(dst_in, 16)
            sp.wait_ge(drained, NR)
            sp.dma_start(t.e_dram.rearrange("h (b t p) -> t (h b) p", t=104, p=128), eT[:, :, :]).then_inc(e_out, 16)
            sp.wait_ge(e_out, 16)
            sp.dma_start(e[:, :], t.e_dram.rearrange("h (k c) -> (h k) c", c=CE)).then_inc(e_in, 16)
            sp.wait_ge(exp_ready, 1)
            sp.dma_start(t.ex_dram.rearrange("h (k c) -> (h k) c", c=CE), fwd[:, :]).then_inc(ex_out, 16)
            sp.wait_ge(ex_out, 16)
            sp.dma_start(eT[:, :, :], t.ex_dram.rearrange("h (b t p) -> t (h b) p", t=104, p=128)).then_inc(ex_in, 16)

        @block.tensor
        def _(pe):
            for r in range(NR):
                if r >= 4:
                    pe.wait_ge(drained, r - 3)
                for i in range(4):
                    b = 4 * r + i
                    mm = pe.transpose(tp[r % 4][0:104, i * 128:(i + 1) * 128], t.e_flat[:, b * 104:(b + 1) * 104], t.ident[:, :])
                mm.then_inc(turned, 1)
            pe.wait_ge(ends_ready, 1)
            for i in range(4):
                mm = pe.transpose(row_ps[:, i, :], ends[:, i:i + 1], t.ident[:, :])
            mm.then_inc(rows_ready, 1)
            pe.wait_ge(carry_ready, 1)
            pe.transpose(start_ps[:, 0:1], carry[:, 0, 0:128], t.ident[0:1, 0:1])
            pe.transpose(start_ps[:, 1:2], carry[:, 1, 1:129], t.ident[0:1, 0:1]).then_inc(start_ready, 1)
            pe.wait_ge(ex_in, 16)
            for r in range(NR):
                pe.wait_ge(drained, NR + r - 3)
                for i in range(4):
                    mm = pe.transpose(tp[r % 4][:, i * 104:(i + 1) * 104], eT[:, 4 * r + i, :], t.ident[0:104, 0:104])
                mm.then_inc(turned, 1)

        @block.scalar
        def _(act):
            act.preload_act_table(ACT.Exp)
            for r in range(NR):
                act.wait_ge(turned, r + 1)
                act.activation(eT[:, 4 * r:4 * r + 4, :], tp[r % 4][0:104, :].rearrange("t (b p) -> t b p", b=4),
                               ACT.Copy).then_inc(drained, 1)
            act.wait_ge(less_max, 1)
            act.activation(fwd[:, :], bwd[:, :], ACT.Exp, scale=1.0 / float(F) ** 0.5).then_inc(exp_ready, 1)
            for r in range(NR):
                act.wait_ge(turned, NR + r + 1)
                act.activation(t.e_flat[:, 4 * r * 104:(4 * r + 4) * 104], tp[r % 4][:, 0:416], ACT.Copy).then_inc(drained, 1)

        @block.vector
        def _(dve):
            order = Order(dve, dve_order)
            dve.wait_ge(dst_in, 3 * HG * 16)
            order(dve.tensor_tensor(pen[:, :], dst[:, 1:CE + 2], dst[:, 0:CE + 1], ALU.is_equal))
            order(dve.tensor_scalar(pen[:, :], pen[:, :], -1.0, BIG, ALU.add, ALU.mult))
            order(dve.tensor_tensor(ends[:, 4:5], dst[:, 1:2], dst[:, CE:CE + 1], ALU.is_equal))
            order(dve.tensor_scalar(ends[:, 5:6], ends[:, 4:5], -1.0, BIG, ALU.add, ALU.mult))
            order(dve.tensor_tensor(ends[:, 2:3], ends[:, 5:6], pen[:, 0:1], ALU.add))
            order(dve.tensor_tensor(ends[:, 3:4], ends[:, 5:6], pen[:, CE:CE + 1], ALU.add))
            order(dve.memset(carry[:, :, :], -BIG))
            dve.wait_ge(e_in, 16)
            scan = dve.tensor_tensor_scan
            order(scan(fwd[:, :], pen[:, 0:CE], e[:, :], -BIG, ALU.add, ALU.max))
            order(scan(bwd[:, ::-1], pen[:, CE:0:-1], e[:, ::-1], -BIG, ALU.add, ALU.max))
            order(dve.tensor_copy(ends[:, 0:1], fwd[:, CE - 1:CE]))
            order(dve.tensor_copy(ends[:, 1:2], bwd[:, 0:1]))
            dve.sem_inc(ends_ready, 1)
            dve.wait_ge(rows_ready, 1)
            order(dve.tensor_copy(rows[:, :, :], row_ps[:, :, :]))
            order(scan(carry[:, 0, 1:129], rows[:, 2, :], rows[:, 0, :], -BIG, ALU.add, ALU.max))
            order(scan(carry[:, 1, 127::-1], rows[:, 3, ::-1], rows[:, 1, ::-1], -BIG, ALU.add, ALU.max))
            dve.sem_inc(carry_ready, 1)
            dve.wait_ge(start_ready, 1)
            order(dve.tensor_copy(start[:, :], start_ps[:, :]))
            order(scan(fwd[:, :], pen[:, 0:CE], e[:, :], start[:, 0:1], ALU.add, ALU.max))
            order(scan(bwd[:, ::-1], pen[:, CE:0:-1], e[:, ::-1], start[:, 1:2], ALU.add, ALU.max))
            order(dve.tensor_tensor(fwd[:, :], fwd[:, :], bwd[:, :], ALU.max))
            dve.tensor_tensor(bwd[:, :], e[:, :], fwd[:, :], ALU.subtract).then_inc(less_max, 1)


def stage_coefficients(nc, a, t):
    x = t.mix
    with Memory(nc) as s:
        rs_ps = [s.ps(f"rs_ps{i}", [PB, NPB, V1]) for i in range(2)]
        m_ps = s.ps("m_ps", [128, 2, V1])
        rs_ready, m_half, m_ready, dve_order = s.sem("rs_ready"), s.sem("m_half"), s.sem("m_ready"), s.sem("coef_order")
        block = s.block()

        @block.tensor
        def _(pe):
            for h in range(HM):
                at, cols = slice(32 * (h % 4), 32 * (h % 4) + 32), slice((h % 4) * V1, (h % 4 + 1) * V1)
                if h >= 2:
                    pe.wait_ge(m_half, h - 1)
                for b in range(NPB):
                    mm = pe.matmul(rs_ps[h % 2][:, b, :], x.pair4[at, b * PB:(b + 1) * PB], x.slv_acc[at, 0, h // 4, cols],
                                   start=True, stop=True)
                mm.then_inc(rs_ready, 1)
            for h in range(HM):
                pe.wait_ge(m_half, h + 1)
                at = slice(32 * (h % 4), 32 * (h % 4) + 32)
                for b in range(NPB):
                    mm = pe.matmul(m_ps[at, h // 4, :], x.pairT[:, b, :], x.g_acc[:, h, b, :], start=(b == 0), stop=(b == NPB - 1))
                mm.then_inc(m_ready, 1)

        @block.vector
        def _(dve):
            order = Order(dve, dve_order)
            for h in range(HM):
                dve.wait_ge(rs_ready, h + 1)
                order(dve.tensor_tensor(x.g_acc[:, h, :, :], x.g_acc[:, h, :, :], rs_ps[h % 2][:, :, :], ALU.subtract))
                dve.tensor_scalar(x.g_acc[:, h, :, :], x.g_acc[:, h, :, :], 0.25, None, ALU.mult).then_inc(m_half, 1)
            dve.wait_ge(m_ready, HM)
            for h in range(HM):
                at, cols = slice(32 * (h % 4), 32 * (h % 4) + 32), slice((h % 4) * V1, (h % 4 + 1) * V1)
                dve.scalar_tensor_tensor(x.coef[at, 0, h // 4, cols], x.slv_acc[at, 0, h // 4, cols], 0.5,
                                         m_ps[at, h // 4, :], ALU.mult, ALU.subtract)
                dve.tensor_scalar(x.coef[at, 1, h // 4, cols], x.slv_acc[at, 1, h // 4, cols], SCALE ** 2, None, ALU.mult)
            order(dve.tensor_scalar(x.slv_acc[0:1, 2, :, :], x.slv_acc[0:1, 2, :, :], SCALE ** 4, None, ALU.mult))


def stage_aggregate_and_mix(nc, a, t):
    FD = F + HG
    x = t.mix
    with Memory(nc) as s:
        ring = s.sb("v_ring", [128, KR, EJ, F])
        idx = [s.sb(f"v_idx{i}", [128, EJ], I32) for i in range(KR)]
        hot = [s.sb(f"hot{i}", [128, EJ, TP]) for i in range(2)]
        val = [s.sb(f"val{i}", [128, EJ, FD]) for i in range(2)]
        sum_ps = [s.ps(f"sum_ps{i}", [TP, FD]) for i in range(2)]
        idx_ready, landed, v_carrier = (s.sem(n) for n in ("v_idx_ready", "v_landed", "v_carrier"))
        landed_slot = s.gather_sems("v_landed_slot", KR)
        val_ready, sum_ready, sum_read, cleared = s.sem("val_ready"), s.sem("sum_ready"), s.sem("sum_read"), s.sem("cleared")
        mq = [s.sb(f"mq{j}", [TP, F]) for j in range(2)]
        qT = [s.sb(f"qT{j}", [128, 2, FC, TP]) for j in range(2)]
        phi = s.sb("qphi", [PB, NPB, TP])
        inv = [s.sb(f"y_inv{j}", [TP, HM]) for j in range(2)]
        y = [s.sb(f"y{j}", [TP, F]) for j in range(2)]
        yT = [s.sb(f"yT{j}", [128, FC, TP]) for j in range(2)]
        biased = [s.sb(f"biased{j}", [TP, F]) for j in range(2)]
        qT_ps = s.ps("qT_ps", [128, FC, TP])
        f_ps = s.ps("qf_ps", [PB, NPB, TP])
        y_ps = s.ps("y_ps", [TP, HM, V1])
        yT_ps = s.ps("yT_ps", [128, FC, TP])
        out_ps = s.ps("out_ps", [TP, F])
        mq_in = s.sems("mq_in", 2)
        qT_ready, f_ready, phi_ready, y_summed, inv_ready, y_ready, yT_turned, yT_ready, out_ready, biased_ready, added, start = (
            s.sem("q_" + n) for n in ("T2", "f", "phi", "sum", "inv", "y", "yT_turned", "yT", "out", "biased", "added", "start"))
        q = Unit(s, "mq", mq_in, lambda j: mq[j][:, :], SCALE * SCALE, x.q_factor[:, :])
        block = s.block()

        @block.gpsimd
        def _(pool):
            gather_program(pool, t, t.v_tab, ring, idx, v_carrier, idx_ready, landed_slot, landed, val_ready)

        @block.sync
        def _(sp):
            def load(u, j):
                sp.wait_ge(q.rounded, u + 1)
                sp.dma_start(mq[j][:, :], t.mix_qkv[ds(u * TP, TP), 0:F]).then_inc(mq_in[j], 16)
            for u in range(2):
                load(u, u % 2)
            with sp.Fori(1, NT // 2) as i:
                for j in range(2):
                    load(i * 2 + j, j)
            load(NT - 1, 0)

        @block.vector
        def _(dve):
            def weigh(n, c):
                w = load_step(dve, t.step_w, n, NT - 1)
                g = load_step(dve, t.step_g, n, N_GROUPS - 1)
                slot = g & (KR - 1)
                ex = t.e_all[:, :, ds(g * EJ, EJ)].rearrange("p h j -> p j h")
                dve.tensor_tensor(hot[c % 2][:, :, :], bcast(t.iota_n[:, ds(w * TP, TP)].unsqueeze(1), 128, EJ, TP),
                                  bcast(t.dst_all[:, g, :].unsqueeze(2), 128, EJ, TP), ALU.is_equal)
                dve.tensor_scalar(val[c % 2][:, :, F:FD], ex, 1.0, None, ALU.mult)
                dve.wait_ge(landed, g + 2)
                dve.tensor_tensor(val[c % 2][:, :, 0:F].rearrange("p j (h d) -> p j h d", h=HG),
                                  ring[:, slot, :, :].rearrange("p j (h d) -> p j h d", h=HG),
                                  bcast(ex.unsqueeze(3), 128, EJ, HG, DG), ALU.mult).then_inc(val_ready, 1)

            def onto_x(u, j):
                dve.wait_ge(out_ready, u + 1)
                dve.tensor_tensor(biased[j][:, :], out_ps[:, :], x.proj_bias[:, :], ALU.add).then_inc(biased_ready, 1)
                dve.wait_ge(biased_ready, u + 1)
                dve.tensor_tensor(t.x_all[:, u, :], t.x_all[:, u, :], biased[j][:, :], ALU.add)

            def body(u, j, k, n, c, i):
                if within(n + 1, N_STEPS):
                    weigh(n + 1, c + 1)
                w = load_step(dve, t.step_w, n, NT - 1)
                dve.wait_ge(sum_ready, n + 1)
                wait(dve, sum_read, n)
                at = t.acc[:, w, :]
                dve.tensor_tensor(at, at, sum_ps[c % 2][:, :], ALU.add).then_inc(sum_read, 1)
                if k == 8:
                    dve.wait_ge(y_summed, u + 1)
                    dve.reciprocal(inv[j][:, :], y_ps[:, :, 0]).then_inc(inv_ready, 1)
                    dve.wait_ge(inv_ready, u + 1)
                    dve.tensor_tensor(y[j][:, :].rearrange("p (h d) -> p h d", h=HM), y_ps[:, :, 1:V1],
                                      bcast(inv[j][:, :].unsqueeze(2), TP, HM, DM), ALU.mult).then_inc(y_ready, 1)
                elif k == 3 and within(1, u + 1 if isinstance(u, int) else 2):
                    onto_x(u - 1, 1 - j)
                if within(u + 1, NT):
                    nxt = (u + 1, 1 - j)
                    if k == 0:
                        q.dve_squares(dve, *nxt, i + j)
                    elif k == 2:
                        q.dve_scale(dve, *nxt)
                    elif k == 4:
                        q.dve_rest(dve, *nxt)
                    elif k == 6:
                        q.dve_last(dve, *nxt)
            dve.memset(t.acc[:, :, :], 0.0).then_inc(cleared, 1)
            q.dve_squares(dve, 0, 0, 0)
            q.dve_scale(dve, 0, 0)
            q.dve_rest(dve, 0, 0)
            q.dve_last(dve, 0, 0)
            dve.wait_ge(cleared, 1)
            dve.sem_inc(val_ready, 1)
            weigh(0, 0)
            over_slots(dve, body)
            onto_x(NT - 1, 0)

        @block.scalar
        def _(act):
            act.preload_act_table(ACT.Sqrt)
            act.sem_inc(q.rounded, 2)

            def turn_out(u, j):
                q.act_turn_out(act, u, j)
                act.activation(qT[j][:, 0, :, :], qT_ps[:, :, :], ACT.Square)
                act.activation(qT[j][:, 1, :, :], qT_ps[:, :, :], ACT.Copy).then_inc(qT_ready, 1)

            def body(u, j, k, n, c, i):
                if within(u, NT) and k < HM:
                    act.wait_ge(f_ready, u * HM + k + 1)
                    act.activation(phi[:, :, :], f_ps[:, :, :], ACT.Square).then_inc(phi_ready, 1)
                nxt = (u + 1, 1 - j)
                if within(u + 1, NT):
                    if k == 1:
                        q.act_root(act, *nxt)
                    elif k == 3:
                        q.act_round(act, *nxt)
                    elif k == 5:
                        q.act_middle(act, *nxt)
                    elif k == 8:
                        turn_out(*nxt)
                if k == 8:
                    act.wait_ge(yT_turned, u + 1)
                    act.activation(yT[j][:, :, :], yT_ps[:, :, :], ACT.Copy).then_inc(yT_ready, 1)
            q.act_root(act, 0, 0)
            q.act_round(act, 0, 0)
            q.act_middle(act, 0, 0)
            turn_out(0, 0)
            over_slots(act, body)

        @block.tensor
        def _(pe):
            flat = y_ps[:, :, :].rearrange("p h e -> p (h e)")

            def turn(u, j):
                mm = q.pe_turn(pe, u, j, t.identb)
                wait(pe, qT_ready, u)
                for b in range(FC):
                    mm = pe.transpose(qT_ps[:, b, :], q.unit[j][:, b * 128:(b + 1) * 128], t.ident[0:TP, 0:TP])
                mm.then_inc(q.turned, 1)

            def project(u, j):
                pe.wait_ge(yT_ready, u + 1)
                wait(pe, biased_ready, u)
                for b in range(FC):
                    mm = pe.matmul(out_ps[:, :], yT[j][:, b, :], t.wproj[:, b, :], start=(b == 0), stop=(b == FC - 1))
                mm.then_inc(out_ready, 1)

            def body(u, j, k, n, c, i):
                tile = within(u, NT)
                if tile and k == 0:
                    pe.wait_ge(qT_ready, u + 1)
                    wait(pe, y_ready, u)
                    pe.sem_inc(start, 1)
                    pe.matmul(flat, t.ones[0:1, 0:TP], x.slv_acc[0:1, 2, :, :].rearrange("p a e -> p (a e)"), start=True, stop=False,
                              skip_group_check=True)
                    for kind in range(2):
                        for half in range(2):
                            pe.matmul(flat[:, half * HW:(half + 1) * HW], qT[j][:, kind, half, :], x.coef[:, kind, half, :],
                                      start=False, stop=False, skip_group_check=True)
                if tile and k < HM:
                    for b in range(NPB):
                        mm = pe.matmul(f_ps[:, b, :], x.pair3[:, b * PB:(b + 1) * PB], q.turned_parts[j][:, k, 0:TP],
                                       start=True, stop=True)
                    mm.then_inc(f_ready, 1)
                pe.wait_ge(val_ready, n + 2)
                wait(pe, sum_read, n - 1)
                for e in range(EJ):
                    mm = pe.matmul(sum_ps[c % 2][:, :], hot[c % 2][:, e, :], val[c % 2][:, e, :], start=(e == 0), stop=(e == EJ - 1))
                mm.then_inc(sum_ready, 1)
                if tile and k < HM:
                    pe.wait_ge(phi_ready, u * HM + k + 1)
                    for b in range(NPB):
                        mm = pe.matmul(y_ps[:, k, :], phi[:, b, :], x.g_acc[:, k, b, :], start=False,
                                       stop=(b == NPB - 1), skip_group_check=True)
                    if k == HM - 1:
                        mm.then_inc(y_summed, 1)
                if k == 1 and within(1, u + 1 if isinstance(u, int) else 2):
                    project(u - 1, 1 - j)
                if k == 7 and within(u + 1, NT):
                    turn(u + 1, 1 - j)
                if k == 8:
                    pe.wait_ge(y_ready, u + 1)
                    for b in range(FC):
                        mm = pe.transpose(yT_ps[:, b, :], y[j][:, b * 128:(b + 1) * 128], t.ident[0:TP, 0:TP])
                    mm.then_inc(yT_turned, 1)
            turn(0, 0)
            over_slots(pe, body)
            project(NT - 1, 0)


def stage_graph_ffn(nc, a, t):
    with Memory(nc) as s:
        w1, w2 = s.sb("g_w1", [128, FC, HID]), s.sb("g_w2", [128, HB, F])
        cols = s.sb("g_cols", [128, 2, HB])
        cols_in = s.sb("g_cols_in", [2 * HB, 128])
        gamma, beta, b2 = s.sb("gamma", [TP, F]), s.sb("beta", [TP, F]), s.sb("g_b2", [TP, F])
        wr, br = s.sb("wr", [128, FC, NEX]), s.sb("br", [TP, NEX])
        den = [s.sb(f"den{j}", [TP, 2, HG]) for j in range(U)]
        buf = [s.sb(f"g_buf{j}", [TP, F]) for j in range(U)]
        buf2 = [s.sb(f"g_buf2{j}", [TP, F]) for j in range(U)]
        plus_b2 = [s.sb(f"plus_b2{j}", [TP, F]) for j in range(U)]
        r1 = [s.sb(f"r1{j}", [TP, F]) for j in range(U)]
        r1T = [s.sb(f"r1T{j}", [128, FC, TP]) for j in range(U)]
        hid = [s.sb(f"hid{i}", [128, HB, TP]) for i in range(U)]
        low = [s.sb(f"low{i}", [128, HB, TP]) for i in range(2)]
        st, tmp = s.sb("g_st", [TP, NT, 6]), s.sb("g_tmp", [TP, 5, NT])
        var, std = s.sb("g_var", [TP, NT]), s.sb("g_std", [TP, NT])
        mean, rstd = s.sb("g_mean", [TP, NT]), s.sb("g_rstd", [TP, NT])
        turn_ps = [s.ps(f"r1_ps{i}", [128, FC, TP]) for i in range(2)]
        hid_ps = [s.ps(f"hid_ps{i}", [128, 2, 512]) for i in range(2)]
        y_ps = [s.ps(f"gy_ps{i}", [TP, F]) for i in range(2)]
        w_in, cols_turned, cols_ready = s.sem("g_w_in"), s.sem("g_cols_turned"), s.sem("g_cols_ready")
        stat_order, stats_done, var_ready, std_ready = s.sem("stat_order"), s.sem("stats_done"), s.sem("g_var_ready"), s.sem("g_std_ready")
        res_order, norm_order, end_order, carrier = s.sem("res_order"), s.sem("norm_order"), s.sem("end_order"), s.sem("g_carrier")
        r1_ready, turned, r1T_ready, h_ready, biased, low_ready, act_ready, y_ready, y_read, sum_ready = (
            s.sem("g_" + x) for x in ("r1", "turned", "r1T", "h", "biased", "low", "act", "y", "y_read", "sum"))
        z_ready, z_turned, zT_ready, logit_ready, logit_read = (s.sem("g_" + x) for x in ("z", "z_turned", "zT", "logit", "logit_read"))
        block = s.block()
        RESIDUAL, END = 4, 4
        STAT = 7

        @block.sync
        def _(sp):
            for ap, src in ((w1, a["L0_gnn_W1"].rearrange("(k p) n -> p k n", p=128)),
                            (w2, a["L0_gnn_W2"].rearrange("(k p) n -> p k n", p=128)),
                            (wr, a["L0_ffn_Wr"].rearrange("(k p) n -> p k n", p=128))):
                sp.dma_start(ap[:, :, :], src).then_inc(w_in, 16)
            for ap, name in ((gamma, "L0_gnn_ln_g"), (beta, "L0_gnn_ln_b"), (b2, "L0_gnn_b2"), (br, "L0_ffn_br")):
                sp.dma_start(ap[:, :], a[name].partition_broadcast(TP)).then_inc(w_in, 16)
            sp.dma_start(cols_in[0:HB, :], a["L0_gnn_b1"].rearrange("(b p) -> b p", p=128)).then_inc(w_in, 16)
            sp.dma_start(cols_in[HB:2 * HB, :], a["L0_gnn_alpha"].rearrange("(b p) -> b p", p=128)).then_inc(w_in, 16)

        @block.vector
        def _(dve):
            def batched(n, mean, rstd):
                order = Order(dve, stat_order, n * STAT)
                dve.wait_ge(stats_done, (n + 1) * NT)
                finish_stats(dve, order, st, mean, var, tmp).then_inc(var_ready, 1)
                dve.wait_ge(std_ready, n + 1)
                order(dve.reciprocal(rstd[:, :], std[:, :]))

            def stats(u, src):
                dve.sem_inc(carrier, 1)
                dve.bn_stats(st[:, u, :], src).then_inc(stats_done, 1)

            dve.wait_ge(w_in, 9 * 16)
            dve.wait_ge(cols_turned, 1)
            dve.tensor_copy(cols[:, :, :], turn_ps[0][:, 0, 0:2 * HB].rearrange("p (c b) -> p c b", c=2)).then_inc(cols_ready, 1)
            dve.wait_ge(cols_ready, 1)

            def residual(u, j, i, last):
                order = Order(dve, res_order, u * RESIDUAL)
                order(dve.tensor_scalar(den[j][:, 0, :], t.acc[:, u, F:F + HG], 1e-30, None, ALU.max))
                order(dve.reciprocal(den[j][:, 1, :], den[j][:, 0, :]))
                order(dve.tensor_tensor(buf[j][:, :].rearrange("p (h d) -> p h d", h=HG),
                                        t.acc[:, u, 0:F].rearrange("p (h d) -> p h d", h=HG),
                                        bcast(den[j][:, 1, :].unsqueeze(2), TP, HG, DG), ALU.mult))
                order(dve.tensor_tensor(t.xn_all[:, u, :], buf[j][:, :], t.xn_all[:, u, :], ALU.add))
                stats(u, t.xn_all[:, u, :])
            over_tiles(dve, residual)
            batched(0, mean, rstd)

            def normal(u, j):
                order = Order(dve, norm_order, u * 2)
                order(dve.tensor_scalar(buf[j][:, :], t.xn_all[:, u, :], mean[:, ds(u, 1)], rstd[:, ds(u, 1)],
                                        ALU.subtract, ALU.mult))
                order(dve.tensor_tensor(buf2[j][:, :], buf[j][:, :], gamma[:, :], ALU.mult))
                dve.tensor_tensor(r1[j][:, :], buf2[j][:, :], beta[:, :], ALU.add).then_inc(r1_ready, 1)

            def ffn(u, j, i, last):
                dve.wait_ge(biased, u + 1)
                dve.scalar_tensor_tensor(low[j % 2][:, :, :], hid[j][:, :, :], 0.0,
                                         bcast(cols[:, 1, :].unsqueeze(2), 128, HB, TP), ALU.min, ALU.mult).then_inc(low_ready, 1)
                dve.wait_ge(low_ready, u + 1)
                dve.scalar_tensor_tensor(hid[j][:, :, :], hid[j][:, :, :], 0.0, low[j % 2][:, :, :],
                                         ALU.max, ALU.add).then_inc(act_ready, 1)
                if not (isinstance(u, int) and u + 2 >= NT):
                    normal(u + 2, (j + 2) % U)
                dve.wait_ge(y_ready, u + 1)
                dve.tensor_tensor(plus_b2[j][:, :], y_ps[j % 2][:, :], b2[:, :], ALU.add).then_inc(y_read, 1)
                dve.wait_ge(y_read, u + 1)
                dve.tensor_tensor(t.xn_all[:, u, :], plus_b2[j][:, :], r1[j][:, :], ALU.add).then_inc(sum_ready, 1)
                dve.wait_ge(sum_ready, u + 1)
                stats(u, t.xn_all[:, u, :])
            normal(0, 0)
            normal(1, 1)
            over_tiles(dve, ffn)
            batched(1, mean, rstd)

            def onto_x(u, j, i, last):
                order = Order(dve, end_order, u * END)
                order(dve.tensor_scalar(buf[j][:, :], t.xn_all[:, u, :], mean[:, ds(u, 1)], rstd[:, ds(u, 1)],
                                        ALU.subtract, ALU.mult))
                order(dve.tensor_tensor(buf2[j][:, :], buf[j][:, :], gamma[:, :], ALU.mult))
                order(dve.tensor_tensor(plus_b2[j][:, :], buf2[j][:, :], beta[:, :], ALU.add))
                order(dve.tensor_tensor(t.x_all[:, u, :], t.x_all[:, u, :], plus_b2[j][:, :], ALU.add))
                stats(u, t.x_all[:, u, :])
            over_tiles(dve, onto_x)
            batched(2, t.x_mean, t.x_rstd)

            def make_z(u, j):
                dve.tensor_scalar(r1[j][:, :], t.x_all[:, u, :], t.x_mean[:, ds(u, 1)], t.x_rstd[:, ds(u, 1)],
                                  ALU.subtract, ALU.mult).then_inc(z_ready, 1)
                dve.wait_ge(z_ready, u + 1)
                stats(u, r1[j][:, :])

            def route(u, j, i, last):
                if not last:
                    make_z(u + 1, (j + 1) % U)
                dve.wait_ge(logit_ready, u + 1)
                dve.tensor_tensor(t.logits[:, u, :], y_ps[j % 2][:, 0:NEX], br[:, :], ALU.add).then_inc(logit_read, 1)
            make_z(0, 0)
            over_tiles(dve, route)
            batched(3, t.z_mean, t.z_rstd)

        @block.scalar
        def _(act):
            act.preload_act_table(ACT.Sqrt)

            def root(n):
                act.wait_ge(var_ready, n + 1)
                act.activation(std[:, :], var[:, :], ACT.Sqrt).then_inc(std_ready, 1)

            def turn_out(u, j):
                act.wait_ge(turned, u + 1)
                act.activation(r1T[j][:, :, :], turn_ps[j % 2][:, :, :], ACT.Copy).then_inc(r1T_ready, 1)

            def bias(u, j):
                act.wait_ge(h_ready, u + 1)
                for b in range(HB):
                    one = act.activation(hid[j][:, b, :], hid_ps[j % 2][:, b // 4, (b % 4) * TP:(b % 4 + 1) * TP],
                                         ACT.Identity, bias=cols[:, 0, b:b + 1])
                one.then_inc(biased, 1)

            def body(u, j, i, last):
                if not last:
                    turn_out(u + 1, (j + 1) % U)
                    bias(u + 1, (j + 1) % U)
            root(0)
            turn_out(0, 0)
            bias(0, 0)
            over_tiles(act, body)
            root(1)
            root(2)

            def z_turn_out(u, j, i, last):
                act.wait_ge(z_turned, u + 1)
                act.activation(r1T[j][:, :, :], turn_ps[j % 2][:, :, :], ACT.Copy).then_inc(zT_ready, 1)
            over_tiles(act, z_turn_out)
            root(3)

        @block.tensor
        def _(pe):
            pe.wait_ge(w_in, 9 * 16)
            pe.transpose(turn_ps[0][:, 0, 0:2 * HB], cols_in[:, :], t.ident[0:2 * HB, 0:2 * HB]).then_inc(cols_turned, 1)
            pe.wait_ge(cols_ready, 1)

            def turn(u, j, ready, out, done):
                pe.wait_ge(ready, u + 1)
                wait(pe, out, psum_turn(u, j))
                for k in range(FC):
                    mm = pe.transpose(turn_ps[j % 2][:, k, :], r1[j][:, k * 128:(k + 1) * 128], t.ident[0:TP, 0:TP])
                mm.then_inc(done, 1)

            def hidden(u, j):
                pe.wait_ge(r1T_ready, u + 1)
                wait(pe, biased, psum_turn(u, j))
                for b in range(HB):
                    for k in range(FC):
                        mm = pe.matmul(hid_ps[j % 2][:, b // 4, (b % 4) * TP:(b % 4 + 1) * TP], w1[:, k, b * 128:(b + 1) * 128],
                                       r1T[j][:, k, :], start=(k == 0), stop=(k == FC - 1))
                mm.then_inc(h_ready, 1)

            def body(u, j, i, last):
                if not last:
                    turn(u + 1, (j + 1) % U, r1_ready, r1T_ready, turned)
                    hidden(u + 1, (j + 1) % U)
                pe.wait_ge(act_ready, u + 1)
                wait(pe, y_read, psum_turn(u, j))
                for b in range(HB):
                    mm = pe.matmul(y_ps[j % 2][:, :], hid[j][:, b, :], w2[:, b, :], start=(b == 0), stop=(b == HB - 1))
                mm.then_inc(y_ready, 1)
            turn(0, 0, r1_ready, r1T_ready, turned)
            hidden(0, 0)
            over_tiles(pe, body)

            def logits(u, j, i, last):
                if not last:
                    turn(u + 1, (j + 1) % U, z_ready, zT_ready, z_turned)
                pe.wait_ge(zT_ready, u + 1)
                wait(pe, logit_read, psum_turn(u, j))
                for k in range(FC):
                    mm = pe.matmul(y_ps[j % 2][:, 0:NEX], r1T[j][:, k, :], wr[:, k, :], start=(k == 0), stop=(k == FC - 1))
                mm.then_inc(logit_ready, 1)
            turn(0, 0, z_ready, zT_ready, z_turned)
            over_tiles(pe, logits)


def stage_experts(nc, a, t, out):
    with Memory(nc) as m:
        weight = m.sb("weight", [TP, 2, NT])
        pos = m.sb("pos", [TP, NT, 2], I32)
        tile_ex = m.sb("tile_ex", [1, NMT], I32)
        table = m.sb("ex_table", [128, NEX, HB + 2 * FC])

        with Memory(nc) as s:
            before = s.sb("e_before", [TP, NEX * NEX])
            keep = s.sb("keep", [TP, NEX * NT])
            tri = s.sb("tri", [TP, TP])
            tile_at = s.sb("tile_at", [1, NMT])
            tab_in = s.sb("tab_in", [NEX * HB + 2 * NEX * FC, 128])
            more, same = s.sb("more", [TP, NT, NEX, NEX]), s.sb("same", [TP, NT, NEX, NEX])
            rank = s.sb("rank", [TP, NT, NEX])
            pick = s.sb("pick", [TP, 3, NT, NEX])
            prod = s.sb("r_prod", [TP, 2, NT, NEX])
            best = s.sb("best", [TP, 2, NT])
            diff, p2, den = s.sb("diff", [TP, NT]), s.sb("p2", [TP, NT]), s.sb("r_den", [TP, NT])
            tot, upto, at = s.sb("tot", [TP, NEX, NT]), s.sb("upto", [TP, NEX, NT]), s.sb("at", [TP, NEX, NT])
            size, size_i = s.sb("size", [TP, 4, NEX]), s.sb("size_i", [TP, 2, NEX], I32)
            pos_f = s.sb("pos_f", [TP, 2, NT])
            past = s.sb("past", [1, NMT, NEX])
            tile_f = s.sb("tile_f", [1, 2, NMT])
            zb = [s.sb(f"zb{j}", [TP, F]) for j in range(U)]
            rows = [s.sb(f"rows{j}", [TP, F]) for j in range(U)]
            idx = [s.sb(f"s_idx{j}", [TP, 2], I32) for j in range(U)]
            pre_ps, tot_ps = s.ps("pre_ps", [TP, NT, NEX]), s.ps("tot_ps", [TP, NT, NEX])
            tab_ps = s.ps("tab_ps", [128, 128])
            c_in, dve_order, picked, counted, diff_ready, p2_ready, tab_turned = (
                s.sem("r_" + x) for x in ("c_in", "order", "picked", "counted", "diff", "p2", "tab"))
            z_again, rows_ready, idx_ready, carrier = s.sem("z_again"), s.sem("rows_ready"), s.sem("s_idx_ready"), s.sem("s_carrier")
            row_out = s.gather_sems("row_out", U)
            block = s.block()

            @block.sync
            def _(sp):
                for ap, name in ((before, "c_before"), (keep, "c_keep")):
                    sp.dma_start(ap[:, :], a[name][0, :].partition_broadcast(TP)).then_inc(c_in, 16)
                sp.dma_start(tri[:, :], a["c_tri"]).then_inc(c_in, 16)
                sp.dma_start(tile_at[:, :], a["c_tile_at"]).then_inc(c_in, 16)
                lo = NEX * HB
                sp.dma_start(tab_in[0:lo, :], a["L0_ffn_b1"].rearrange("e (b p) -> (e b) p", p=128)).then_inc(c_in, 16)
                sp.dma_start(tab_in[lo:lo + NEX * FC, :], a["L0_ffn_ln_g"].rearrange("e (k p) -> (e k) p", p=128)).then_inc(c_in, 16)
                sp.dma_start(tab_in[lo + NEX * FC:, :], a["L0_ffn_ln_b"].rearrange("e (k p) -> (e k) p", p=128)).then_inc(c_in, 16)

            @block.tensor
            def _(pe):
                pe.wait_ge(c_in, 7 * 16)
                rows_ = NEX * HB + 2 * NEX * FC
                pe.transpose(tab_ps[:, 0:rows_], tab_in[:, :], t.ident[0:rows_, 0:rows_]).then_inc(tab_turned, 1)
                pe.wait_ge(picked, 1)
                flat = pick[:, 2, :, :].rearrange("p t e -> p (t e)")
                pe.matmul(pre_ps[:, :, :].rearrange("p t e -> p (t e)"), tri[:, :], flat, start=True, stop=True)
                pe.matmul(tot_ps[:, :, :].rearrange("p t e -> p (t e)"), t.ones[0:TP, 0:TP], flat, start=True, stop=True
                          ).then_inc(counted, 1)

            @block.scalar
            def _(act):
                act.preload_act_table(ACT.Exp)
                act.wait_ge(diff_ready, 1)
                act.activation(p2[:, :], diff[:, :], ACT.Exp).then_inc(p2_ready, 1)

            @block.vector
            def _(dve):
                order = Order(dve, dve_order)
                L = t.logits
                full = (TP, NT, NEX, NEX)
                mine, other = bcast(L[:, :, :].unsqueeze(3), *full), bcast(L[:, :, :].unsqueeze(2), *full)
                dve.wait_ge(c_in, 7 * 16)
                order(dve.tensor_tensor(more[:, :, :, :], other, mine, ALU.is_gt))
                order(dve.tensor_tensor(same[:, :, :, :], other, mine, ALU.is_equal))
                flat = lambda x: x[:, :, :, :].rearrange("p t i j -> p t (i j)")
                order(dve.tensor_tensor(flat(same), flat(same), bcast(before[:, :].unsqueeze(1), TP, NT, NEX * NEX), ALU.mult))
                order(dve.tensor_tensor(flat(more), flat(more), flat(same), ALU.add))
                order(dve.tensor_reduce(rank[:, :, :], more[:, :, :, :], AX.X, ALU.add))
                order(dve.tensor_scalar(pick[:, 0, :, :], rank[:, :, :], 0.0, None, ALU.is_equal))
                order(dve.tensor_scalar(pick[:, 1, :, :], rank[:, :, :], 1.0, None, ALU.is_equal))
                order(dve.tensor_tensor(pick[:, 2, :, :], pick[:, 0, :, :], pick[:, 1, :, :], ALU.add))
                dve.sem_inc(picked, 1)
                for c in range(2):
                    order(dve.tensor_tensor(prod[:, c, :, :], L[:, :, :], pick[:, c, :, :], ALU.mult))
                order(dve.tensor_reduce(best[:, :, :], prod[:, :, :, :], AX.X, ALU.add))
                order(dve.tensor_tensor(diff[:, :], best[:, 1, :], best[:, 0, :], ALU.subtract))
                dve.sem_inc(diff_ready, 1)
                dve.wait_ge(p2_ready, 1)
                order(dve.tensor_scalar(den[:, :], p2[:, :], 1.0, None, ALU.add))
                order(dve.reciprocal(weight[:, 0, :], den[:, :]))
                order(dve.tensor_tensor(weight[:, 1, :], p2[:, :], weight[:, 0, :], ALU.mult))
                dve.wait_ge(counted, 1)
                order(dve.tensor_copy(tot[:, :, :], tot_ps[:, :, :].rearrange("p t e -> p e t")))
                order(dve.tensor_tensor_scan(upto[:, :, :].rearrange("p e t -> p (e t)"), keep[:, :],
                                             tot[:, :, :].rearrange("p e t -> p (e t)"), 0.0, ALU.mult, ALU.add))
                order(dve.tensor_scalar(size[:, 0, :], upto[:, :, NT - 1], float(MT - 1), None, ALU.add))
                order(dve.tensor_copy(size_i[:, 0, :], size[:, 0, :]))
                bits = MT.bit_length() - 1
                order(dve.tensor_scalar(size_i[:, 1, :], size_i[:, 0, :], bits, bits, ALU.logical_shift_right, ALU.logical_shift_left))
                order(dve.tensor_copy(size[:, 1, :], size_i[:, 1, :]))
                order(dve.tensor_tensor_scan(size[:, 2, :], t.ones[0:TP, 0:NEX], size[:, 1, :], 0.0, ALU.mult, ALU.add))
                order(dve.tensor_tensor(size[:, 3, :], size[:, 2, :], size[:, 1, :], ALU.subtract))
                order(dve.tensor_tensor(at[:, :, :], upto[:, :, :], tot[:, :, :], ALU.subtract))
                order(dve.tensor_tensor(at[:, :, :], at[:, :, :], bcast(size[:, 3, :].unsqueeze(2), TP, NEX, NT), ALU.add))
                order(dve.tensor_tensor(at[:, :, :], at[:, :, :], pre_ps[:, :, :].rearrange("p t e -> p e t"), ALU.add))
                for c in range(2):
                    order(dve.tensor_tensor(prod[:, c, :, :], at[:, :, :].rearrange("p e t -> p t e"), pick[:, c, :, :], ALU.mult))
                order(dve.tensor_reduce(pos_f[:, :, :], prod[:, :, :, :], AX.X, ALU.add))
                order(dve.tensor_copy(pos[:, :, :], pos_f[:, :, :].rearrange("p c t -> p t c")))
                order(dve.tensor_tensor(past[:, :, :], bcast(size[0:1, 2, :].unsqueeze(1), 1, NMT, NEX),
                                        bcast(tile_at[:, :].unsqueeze(2), 1, NMT, NEX), ALU.is_le))
                order(dve.tensor_reduce(tile_f[:, 0, :], past[:, :, :], AX.X, ALU.add))
                order(dve.tensor_scalar(tile_f[:, 1, :], tile_f[:, 0, :], float(NEX - 1), None, ALU.min))
                order(dve.tensor_copy(tile_ex[:, :], tile_f[:, 1, :]))
                dve.wait_ge(tab_turned, 1)
                lo = NEX * HB
                dve.tensor_copy(table[:, :, 0:HB], tab_ps[:, 0:lo].rearrange("p (e b) -> p e b", b=HB))
                for c in range(2):
                    dve.tensor_copy(table[:, :, HB + c * FC:HB + (c + 1) * FC],
                                    tab_ps[:, lo + c * NEX * FC:lo + (c + 1) * NEX * FC].rearrange("p (e k) -> p e k", k=FC))

                def make_rows(u, j, i, last):
                    wait(dve, row_out[j], i * 32)
                    dve.tensor_scalar(idx[j][:, :], pos[:, u, :], 0.0, None, ALU.add).then_inc(idx_ready, 1)
                    dve.tensor_scalar(zb[j][:, :], t.x_all[:, u, :], t.x_mean[:, ds(u, 1)], t.x_rstd[:, ds(u, 1)],
                                      ALU.subtract, ALU.mult).then_inc(z_again, 1)
                    dve.wait_ge(z_again, u + 1)
                    dve.tensor_scalar(rows[j][:, :], zb[j][:, :], t.z_mean[:, ds(u, 1)], t.z_rstd[:, ds(u, 1)],
                                      ALU.subtract, ALU.mult).then_inc(rows_ready, 1)
                over_tiles(dve, make_rows)

            @block.gpsimd
            def _(pool):
                def scatter(u, j, i, last):
                    pool.wait_ge(rows_ready, u + 1)
                    pool.sem_inc(carrier, 1)
                    for c in range(2):
                        pool.indirect_dma_start(out=t.x_rows, out_offset=bass.IndirectOffsetOnAxis(ap=idx[j][:, c:c + 1], axis=0),
                                                in_=rows[j][:, :], in_offset=None).then_inc(row_out[j], 16)
                over_tiles(pool, scatter)
                for j in range(U):
                    pool.wait_ge(row_out[j], NT // U * 32)

        with Memory(nc) as s:
            w1 = [s.sb(f"e_w1{i}", [128, FC, HID]) for i in range(2)]
            w2 = [s.sb(f"e_w2{i}", [128, HB, F]) for i in range(2)]
            b2 = [s.sb(f"e_b2{i}", [128, F]) for i in range(2)]
            xr = [s.sb(f"xr{i}", [128, 2, F]) for i in range(2)]
            small = [s.sb(f"small{i}", [128, HB + 2 * FC]) for i in range(2)]
            xT = [s.sb(f"e_xT{i}", [128, FC, MT]) for i in range(2)]
            hT = [s.sb(f"e_hT{i}", [128, HB, MT]) for i in range(2)]
            y = [s.sb(f"e_y{i}", [128, 2, F]) for i in range(2)]
            turn_ps = [s.ps(f"e_turn{i}", [128, FC, MT]) for i in range(2)]
            h_ps = s.ps("e_h", [128, HB, MT])
            y_ps = s.ps("e_yps", [128, 2, 512])
            w1_in, w2_in, b2_in, x_in, y_out = (s.sems("e_" + x, 2) for x in ("w1_in", "w2_in", "b2_in", "x_in", "y_out"))
            small_ready, turned, xT_ready, h_ready, h_read, y_ready, y_read = (
                s.sem("e_" + x) for x in ("small", "turned", "xT", "h", "h_read", "y", "y_read"))
            block = s.block()

            def over_experts(eng, body):
                for par in range(2):
                    body(par, par, 0, False)
                with eng.Fori(1, NMT // 2 - 1) as i:
                    for par in range(2):
                        body(i * 2 + par, par, i, False)
                for par in range(2):
                    body(NMT - 2 + par, par, NMT // 2 - 1, par == 1)

            @block.sync
            def _(sp):
                def body(n, par, i, last):
                    ex = sp.value_load(tile_ex[0:1, ds(n, 1)], min_val=0, max_val=NEX - 1)
                    wait(sp, y_read, n)
                    sp.dma_start(xr[par][:, :, :], t.x_rows[ds(n * MT, MT), :].rearrange("(s p) f -> p s f", p=128)
                                 ).then_inc(x_in[par], 16)
                    sp.dma_start(w1[par][:, :, :], a["L0_ffn_W1"].rearrange("e (k p) n -> e p k n", p=128)[ex]).then_inc(w1_in[par], 16)
                    sp.dma_start(w2[par][:, :, :], a["L0_ffn_W2"].rearrange("e (b p) n -> e p b n", p=128)[ex]).then_inc(w2_in[par], 16)
                    sp.dma_start(b2[par][:, :], a["L0_ffn_b2"][ex].partition_broadcast(128)).then_inc(b2_in[par], 16)
                over_experts(sp, body)

            @block.vector
            def _(dve):
                def prepare(n, par, i):
                    ex = dve.value_load(tile_ex[0:1, ds(n, 1)], min_val=0, max_val=NEX - 1)
                    dve.wait_ge(turned, n + 1)
                    dve.tensor_scalar(small[par][:, :], table[:, ex, :], 0.0, None, ALU.add).then_inc(small_ready, 1)
                    dve.wait_ge(small_ready, n + 1)
                    for k in range(FC):
                        one = dve.tensor_scalar(xT[par][:, k, :], turn_ps[par][:, k, :], small[par][:, HB + k:HB + k + 1],
                                                small[par][:, HB + FC + k:HB + FC + k + 1], ALU.mult, ALU.add)
                    one.then_inc(xT_ready, 1)

                def body(n, par, i, last):
                    if not last:
                        prepare(n + 1, 1 - par, i + par)
                    wait(dve, y_out[par], i * 16)
                    dve.wait_ge(b2_in[par], i * 16 + 16)
                    dve.wait_ge(y_ready, n + 1)
                    dve.tensor_tensor(y[par][:, :, :], y_ps[:, :, 0:F], bcast(b2[par][:, :].unsqueeze(1), 128, 2, F), ALU.add
                                      ).then_inc(y_read, 1)
                dve.sem_inc(y_read, 1)
                prepare(0, 0, 0)
                over_experts(dve, body)

            @block.scalar
            def _(act):
                act.preload_act_table(ACT.Gelu)
                act.sem_inc(h_read, HB // 2)

                def store(n, par):
                    act.wait_ge(y_read, n + 2)
                    act.dma_start(t.y_rows[ds(n * MT, MT), :].rearrange("(s p) f -> p s f", p=128), y[par][:, :, :]
                                  ).then_inc(y_out[par], 16)

                def gelus(n, par):
                    act.wait_ge(small_ready, n + 1)
                    for b in range(HB):
                        if b % 2 == 0:
                            act.wait_ge(h_ready, n * (HB // 2) + b // 2 + 1)
                        gelu = act.activation(hT[par][:, b, :], h_ps[:, b, :], ACT.Gelu, bias=small[par][:, b:b + 1])
                        if b % 2:
                            gelu.then_inc(h_read, 1)

                def body(n, par, i, last):
                    if not last:
                        gelus(n + 1, 1 - par)
                    store(n, par)
                gelus(0, 0)
                over_experts(act, body)
                for par in range(2):
                    act.wait_ge(y_out[par], NMT // 2 * 16)

            @block.tensor
            def _(pe):
                def turn(n, par, i):
                    pe.wait_ge(x_in[par], i * 16 + 16)
                    for half in range(2):
                        for k in range(FC):
                            mm = pe.transpose(turn_ps[par][:, k, half * 128:(half + 1) * 128], xr[par][:, half, k * 128:(k + 1) * 128],
                                              t.ident[:, :])
                    mm.then_inc(turned, 1)

                def body(n, par, i, last):
                    if not last:
                        turn(n + 1, 1 - par, i + par)
                    pe.wait_ge(w1_in[par], i * 16 + 16)
                    pe.wait_ge(xT_ready, n + 1)
                    for b in range(HB):
                        if b % 2 == 0:
                            pe.wait_ge(h_read, n * (HB // 2) + b // 2 + 1)
                        for k in range(FC):
                            mm = pe.matmul(h_ps[:, b, :], w1[par][:, k, b * 128:(b + 1) * 128], xT[par][:, k, :],
                                           start=(k == 0), stop=(k == FC - 1))
                        if b % 2:
                            mm.then_inc(h_ready, 1)
                    pe.wait_ge(w2_in[par], i * 16 + 16)
                    pe.wait_ge(y_read, n + 1)
                    for b in range(HB):
                        if b % 2 == 0:
                            pe.wait_ge(h_read, (n + 1) * (HB // 2) + b // 2 + 1)
                        for half in range(2):
                            mm = pe.matmul(y_ps[:, half, 0:F], hT[par][:, b, half * 128:(half + 1) * 128], w2[par][:, b, :],
                                           start=(b == 0), stop=(b == HB - 1))
                    mm.then_inc(y_ready, 1)
                turn(0, 0, 0)
                over_experts(pe, body)

        with Memory(nc) as s:
            idx = [s.sb(f"c_idx{j}", [TP, 2], I32) for j in range(U)]
            got = [[s.sb(f"got{c}{j}", [TP, F]) for c in range(2)] for j in range(U)]
            part = [[s.sb(f"part{c}{j}", [TP, F]) for c in range(2)] for j in range(U)]
            res = [s.sb(f"res{j}", [TP, F]) for j in range(U)]
            got_in, res_out = s.gather_sems("got_in", U), s.sems("res_out", U)
            idx_ready, used, part_order, carrier, a_carrier = (
                s.sem("c_" + x) for x in ("idx", "used", "order", "carrier", "a_carrier"))
            block = s.block()

            @block.scalar
            def _(act):
                def body(u, j, i, last):
                    act.wait_ge(used, u + 1)
                    act.sem_inc(a_carrier, 1)
                    act.activation(idx[j][:, :], pos[:, u, :], ACT.Copy).then_inc(idx_ready, 1)
                over_tiles(act, body)

            @block.gpsimd
            def _(pool):
                def body(u, j, i, last):
                    pool.wait_ge(idx_ready, u + 1)
                    pool.sem_inc(carrier, 1)
                    for c in range(2):
                        pool.indirect_dma_start(out=got[j][c][:, :], out_offset=None, in_=t.y_rows,
                                                in_offset=bass.IndirectOffsetOnAxis(ap=idx[j][:, c:c + 1], axis=0)
                                                ).then_inc(got_in[j], 16)
                over_tiles(pool, body)

            @block.vector
            def _(dve):
                dve.sem_inc(used, U)

                def body(u, j, i, last):
                    order = Order(dve, part_order, u * 2)
                    dve.wait_ge(got_in[j], i * 32 + 32)
                    order(dve.tensor_scalar(part[j][0][:, :], got[j][0][:, :], weight[:, 0, ds(u, 1)], None, ALU.mult))
                    order(dve.scalar_tensor_tensor(part[j][1][:, :], got[j][1][:, :], weight[:, 1, ds(u, 1)], part[j][0][:, :],
                                                   ALU.mult, ALU.add))
                    wait(dve, res_out[j], i * 16)
                    dve.tensor_tensor(res[j][:, :], part[j][1][:, :], t.x_all[:, u, :], ALU.add).then_inc(used, 1)
                over_tiles(dve, body)

            @block.sync
            def _(sp):
                def body(u, j, i, last):
                    sp.wait_ge(used, u + 1 + U)
                    sp.dma_start(out[ds(u * TP, TP), :], res[j][:, :]).then_inc(res_out[j], 16)
                over_tiles(sp, body)
                for j in range(U):
                    sp.wait_ge(res_out[j], NT // U * 16)


def mix_memory(m):
    x = Shared()
    x.pair3 = m.sb("pair3", [3 * DM, NPAIR], BF16)
    x.pair4 = m.sb("pair4", [128, NPAIR])
    x.pairT = m.sb("pairT", [PB, NPB, DM])
    x.g_acc = m.sb("g_acc", [PB, HM, NPB, V1])
    x.slv_acc = m.sb("slv_acc", [128, 3, 2, HW])
    x.coef = m.sb("coef", [128, 2, 2, HW])
    x.k_factor, x.q_factor = m.sb("k_factor", [TP, HM]), m.sb("q_factor", [TP, HM])
    x.proj_bias = m.sb("proj_bias", [TP, F])
    return x


def build(nc, a, out):
    def dram(name, shape, dt=F32):
        return nc.dram_tensor(name, shape, dt, kind="Internal").ap()

    t = Shared()
    t.k_tab, t.v_tab = dram("k_tab", (N, F)), dram("v_tab", (N, F))
    t.mix_qkv = dram("mix_qkv", (N, 3 * F))
    t.dst_pad, t.src_pad = dram("dst_pad", (E_PAD + 2,), I32), dram("src_pad", (E_PAD + 2,), I32)
    t.e_dram, t.ex_dram = dram("e_dram", (HG, E_PAD)), dram("ex_dram", (HG, E_PAD))
    t.x_rows, t.y_rows = dram("x_rows", (ROWS, F)), dram("y_rows", (ROWS, F))
    with Memory(nc) as m:
        t.x_all = m.sb("x_all", [TP, NT, F])
        t.xn_all = m.sb("xn_all", [TP, NT, F])
        t.ident, t.identb = m.sb("ident", [128, 128]), m.sb("identb", [128, 128], BF16)
        t.ones = m.sb("ones", [128, 128])
        t.wproj = m.sb("wproj", [128, FC, F])
        t.logits = m.sb("logits", [TP, NT, NEX])
        t.x_mean, t.x_rstd = m.sb("x_mean", [TP, NT]), m.sb("x_rstd", [TP, NT])
        t.z_mean, t.z_rstd = m.sb("z_mean", [TP, NT]), m.sb("z_rstd", [TP, NT])
        with Memory(nc) as e:
            t.iota_n = e.sb("iota_n", [128, N])
            t.win_node = e.sb("win_node", [TP, NT])
            t.dst_all = e.sb("dst_all", [128, G_PAD, EJ])
            t.src_all = e.sb("src_all", [128, G_PAD, EJ], I32)
            t.step_g = e.sb("step_g", [1, N_STEPS], I32)
            t.step_w = e.sb("step_w", [1, N_STEPS], I32)
            t.step_slot = e.sb("step_slot", [1, N_STEPS], I32)
            t.need_steps = e.sb("need_steps", [1, N_GROUPS], I32)
            t.e_all = e.sb("e_all", [128, HG, ET_PAD])
            t.e_flat = t.e_all[:, :, :].rearrange("p h t -> p (h t)")
            t.mix = mix_memory(e)
            with Memory(nc) as q:
                t.q3 = q.sb("q3", [TP, NT, 3 * F], BF16)
                stage_project(nc, a, t)
                stage_scores_and_sums(nc, a, t)
            stage_edge_softmax(nc, a, t)
            stage_coefficients(nc, a, t)
            t.acc = e.sb("acc", [TP, NT, F + HG])
            stage_aggregate_and_mix(nc, a, t)
            stage_graph_ffn(nc, a, t)
        stage_experts(nc, a, t, out)


_INS = ["x", "src", "dst", "L0_gnn_Wq", "L0_gnn_Wk", "L0_gnn_Wv", "L0_gnn_ln_g", "L0_gnn_ln_b", "L0_gnn_W1", "L0_gnn_b1",
        "L0_gnn_alpha", "L0_gnn_W2", "L0_gnn_b2", "L0_mix_Wqkv", "L0_mix_bqkv", "L0_mix_Wproj", "L0_mix_bproj",
        "L0_mix_temperature", "L0_ffn_Wr", "L0_ffn_br", "L0_ffn_ln_g", "L0_ffn_ln_b", "L0_ffn_W1", "L0_ffn_b1",
        "L0_ffn_W2", "L0_ffn_b2"]


def constants():
    f32 = np.float32
    i, j = np.triu_indices(DM, 1)
    pair = np.zeros((DM, NPAIR), f32)
    pair[i, np.arange(NPAIR)] = 1
    pair[j, np.arange(NPAIR)] = 1
    low = pair.astype(mybir.dt.np(BF16))
    tail = np.zeros((2, E_PAD + 1 - EDGES), np.int32)
    tail[0] = PAD_DST
    tail[0, -1] = -2
    keep = np.ones((NEX, NT), f32)
    keep[:, 0] = 0
    return {
        "c_ident": np.eye(128, dtype=f32), "c_identb": np.eye(128).astype(low.dtype),
        "c_iota": np.arange(N, dtype=f32)[None, :],
        "c_win_node": (np.arange(NT)[None, :] * TP + np.arange(TP)[:, None]).astype(f32),
        "c_win_end": ((np.arange(NT)[:, None] + 1) * TP).astype(f32), "c_win_id": np.arange(NT, dtype=f32)[:, None],
        "c_count": np.arange(N_STEPS, dtype=f32)[None, :],
        "c_head": np.array([[-1], [0]], np.int32), "c_tail": tail,
        "c_pair3": np.concatenate([low] * 3), "c_pair4": np.concatenate([pair] * 4),
        "c_pairT": np.ascontiguousarray(pair.T.reshape(NPB, PB, DM).transpose(1, 0, 2)),
        "c_before": np.tri(NEX, k=-1, dtype=f32).reshape(1, -1), "c_keep": keep.reshape(1, -1),
        "c_tri": np.triu(np.ones((TP, TP), f32), 1), "c_tile_at": (np.arange(NMT) * MT).astype(f32)[None, :],
    }


def kernel(**inputs):
    import concourse.bacc as bacc
    from concourse.bass_utils import run_bass_kernel_spmd

    nc = bacc.Bacc("TRN2", target_bir_lowering=False, num_devices=1)
    arrays = {name: np.ascontiguousarray(inputs[name]) for name in _INS}
    arrays.update(constants())
    aps = {name: nc.dram_tensor(name, x.shape, mybir.dt.from_np(x.dtype), kind="ExternalInput").ap() for name, x in arrays.items()}
    out = nc.dram_tensor("out", (N, F), F32, kind="ExternalOutput").ap()
    build(nc, aps, out)
    result = run_bass_kernel_spmd(nc, [arrays], core_ids=[0])
    return result.results[0]["out"]
```

```python
from contextlib import ExitStack

import numpy as np

import concourse.bass as bass
from concourse import mybir

F32 = mybir.dt.float32
BF16 = mybir.dt.bfloat16
I32 = mybir.dt.int32
ALU = mybir.AluOpType
ACT = mybir.ActivationFunctionType
AX = mybir.AxisListType
ds = bass.ds

N = 3125
F = 256
FC = F // 128
TP = 125
NT = N // TP
U = 5
HG = 4
DG = F // HG
HM = 8
DM = F // HM
NPAIR = DM * (DM - 1) // 2
PB = 124
NPB = NPAIR // PB
V1 = DM + 1
EDGES = 2 * 50000 + N
EJ = 4
GE = EJ * 128
N_GROUPS = -(-EDGES // GE)
G_PAD = 208
E_PAD = G_PAD * GE
HALF = G_PAD // 2
ET_PAD = G_PAD * EJ
N_STEPS = N_GROUPS + NT - 1
K_RING, V_RING = 8, 16
CHUNKS = 32
CE = E_PAD // CHUNKS
SLOTS = N_STEPS // NT
HW = HM // 2 * V1
NEX = 8
HID = 4 * F
HB = HID // 128
MT = 256
NMT = (2 * N + NEX * (MT - 1)) // MT
ROWS = NMT * MT
RW = F + 2
BIG = 1e30
EPS = 1e-5
SCALE = float(DM) ** 0.25
MIX_BLOCKS = ((2, 3, 4), (5, 0, 1))
PAD_DST = 4000


class Shared:
    pass


class Order:

    def __init__(self, eng, sem, base=0):
        self.eng, self.sem, self.base, self.n = eng, sem, base, 0

    def __call__(self, ins):
        ins.then_inc(self.sem, 1)
        self.n += 1
        self.eng.wait_ge(self.sem, self.base + self.n)


def bcast(ap, *shape):
    return ap.broadcast_to(list(shape))


def over_tiles(eng, body, n=NT, unroll=U):
    rounds = n // unroll
    for j in range(unroll):
        body(j, j, 0, False)
    with eng.Fori(1, rounds - 1) as i:
        for j in range(unroll):
            body(i * unroll + j, j, i, False)
    for j in range(unroll):
        body((rounds - 1) * unroll + j, j, rounds - 1, j == unroll - 1)


def within(x, count):
    return not isinstance(x, int) or x < count


def wait(eng, sem, value):
    if not isinstance(value, int) or value > 0:
        eng.wait_ge(sem, value)


def psum_turn(u, j):
    return u if j == 0 else u - 1


class Memory:

    def __init__(self, nc):
        self.nc, self.stack, self.held = nc, ExitStack(), []

    def __enter__(self):
        self.stack.__enter__()
        return self

    def __exit__(self, *e):
        self.stack.__exit__(*e)
        for sem in self.held:
            self.nc.gpsimd.sem_clear(sem)
            self.nc.release_semaphore(sem)

    def sb(self, name, shape, dt=F32):
        return self.stack.enter_context(self.nc.sbuf_tensor(name, list(shape), dt))

    def ps(self, name, shape, dt=F32):
        return self.stack.enter_context(self.nc.psum_tensor(name, list(shape), dt))

    def sem(self, name):
        self.held.append(self.nc.alloc_semaphore(name))
        return self.held[-1]

    def gather_sems(self, name, n):
        return [self.nc.alloc_semaphore(f"{name}{i}") for i in range(n)]

    def sems(self, name, n):
        return [self.sem(f"{name}{i}") for i in range(n)]

    def block(self):
        return self.stack.enter_context(self.nc.Block())


def finish_stats(dve, order, st, mean, var, tmp):
    m_even, m_odd, q_even, q_odd = (st[:, :, i] for i in (1, 4, 2, 5))
    order(dve.tensor_tensor(tmp[:, 0, :], m_even, m_odd, ALU.add))
    order(dve.tensor_scalar(mean[:, :], tmp[:, 0, :], 0.5, None, ALU.mult))
    order(dve.tensor_tensor(tmp[:, 1, :], m_even, m_odd, ALU.subtract))
    order(dve.tensor_tensor(tmp[:, 2, :], tmp[:, 1, :], tmp[:, 1, :], ALU.mult))
    order(dve.tensor_tensor(tmp[:, 3, :], q_even, q_odd, ALU.add))
    order(dve.tensor_scalar(tmp[:, 4, :], tmp[:, 3, :], 1.0 / F, EPS, ALU.mult, ALU.add))
    return dve.scalar_tensor_tensor(var[:, :], tmp[:, 2, :], 0.25, tmp[:, 4, :], ALU.mult, ALU.add)


def stage_project(nc, a, t, m):
    wqk = m.sb("wqk", [128, FC, 2 * F])
    mean, rstd = m.sb("mean", [TP, NT]), m.sb("rstd", [TP, NT])

    with Memory(nc) as s:
        wst = s.sb("wst", [128, 6, F])
        wpst = s.sb("wpst", [128, FC, F])
        edge_i = s.sb("edge_i", [G_PAD // 2, 2, 2, GE], I32)
        edge_f = s.sb("edge_f", [G_PAD // 2, 2, 2, GE])
        st, var = s.sb("st", [TP, NT, 6]), s.sb("var", [TP, NT])
        std, tmp = s.sb("std", [TP, NT]), s.sb("tmp", [TP, 5, NT])
        first_dst = s.sb("first_dst", [1, N_GROUPS])
        win_end = s.sb("win_end", [NT, 1])
        win_id = s.sb("win_id", [NT, 1])
        count = s.sb("count", [1, N_STEPS])
        before = s.sb("before", [NT, N_GROUPS])
        last_group = s.sb("last_group", [NT, 3])
        passed = s.sb("passed", [NT, N_STEPS])
        count_w = s.sb("count_w", [NT, N_STEPS])
        row = s.sb("row", [1, 3, N_STEPS])
        tp = [s.ps(f"tp{i}", [128, 512]) for i in range(4)]
        first_ps = s.ps("first_ps", [NT, N_GROUPS])
        step_ps = s.ps("step_ps", [1, N_STEPS])
        group_ps = s.ps("group_ps", [1, N_GROUPS])
        x_in, w_in, c_in, pad_in = s.sems("x_in", U), s.sem("w_in"), s.sem("c_in"), s.sem("pad_in")
        edge_in, small_in = s.sem("edge_in"), s.sem("small_in")
        memsets, edge_float, turned, drained = s.sem("memsets"), s.sem("edge_float"), s.sem("turned"), s.sem("drained")
        stats_done = s.sem("stats_done0")
        dve_order, var_ready, std_ready = s.sem("dve_order"), s.sem("var_ready"), s.sem("std_ready")
        first_row, firsts, before_ready, passed_ready, steps_ready = (
            s.sem(x) for x in ("first_row", "firsts", "before_ready", "passed_ready", "steps_ready"))
        banks = []
        for kind in range(2):
            for half in range(2):
                banks.append(("edge", kind, half))
        for k in range(FC):
            for third in range(2):
                banks.append(("mix", k, third))
        for k in range(FC):
            banks.append(("proj", k, 0))
        block = s.block()

        @block.sync
        def _(sp):
            full, part = divmod(EDGES - HALF * GE, GE)
            for kind, name in enumerate(("dst", "src")):
                for half, groups in ((0, HALF), (1, full)):
                    first = half * HALF * GE
                    sp.dma_start(edge_i[0:groups, kind, half, :], a[name][first:first + groups * GE].rearrange("(g c) -> g c", c=GE)
                                 ).then_inc(edge_in, 16)
                sp.dma_start(edge_i[full:full + 1, kind, 1, 0:part], a[name][EDGES - part:].rearrange("(p c) -> p c", p=1)
                             ).then_inc(edge_in, 16)
                if kind == 0:
                    sp.dma_start(t.ident[:, :], a["c_ident"]).then_inc(c_in, 16)
            rest = GE - part
            sp.dma_start(edge_i[full:full + 1, :, 1, part:], a["c_tail"][:, 0:rest].rearrange("k (g c) -> g k c", g=1)
                         ).then_inc(edge_in, 16)
            sp.dma_start(edge_i[full + 1:, :, 1, :], a["c_tail"][:, rest:-1].rearrange("k (g c) -> g k c", c=GE)).then_inc(edge_in, 16)
            for name, ap in (("c_identb", t.identb), ("c_win_node", t.win_node),
                             ("c_win_end", win_end), ("c_win_id", win_id), ("c_count", count)):
                sp.dma_start(ap[:, :], a[name]).then_inc(small_in, 16)
            sp.dma_start(count_w[:, :], a["c_count"][0, :].partition_broadcast(NT)).then_inc(small_in, 16)
            sp.dma_start(t.dst_pad[1:1 + EDGES].rearrange("(p c) -> p c", p=TP),
                         a["dst"].rearrange("(p c) -> p c", p=TP)).then_inc(pad_in, 16)
            sp.dma_start(t.dst_pad[0:1].rearrange("(p c) -> p c", p=1), a["c_head"][0:1, :]).then_inc(pad_in, 16)
            sp.dma_start(t.dst_pad[1 + EDGES:].rearrange("(p c) -> p c", p=1), a["c_tail"][0:1, :]).then_inc(pad_in, 16)
            sp.wait_ge(pad_in, 3 * 16)

        @block.gpsimd
        def _(pool):
            pool.memset(t.ones[:, :], 1.0).then_inc(memsets, 1)
            pool.memset(t.late_bias[:, 2 * F:3 * F], 0.0)

        @block.scalar
        def _(act):
            for part in range(U):
                if part == 1:
                    act.wait_ge(edge_in, 8 * 16)
                at = slice(part * U, (part + 1) * U)
                act.dma_start(t.x_all[:, at, :], a["x"].rearrange("(t p) f -> p t f", p=TP)[:, at, :]).then_inc(x_in[part], 16)
            act.dma_start(wst[:, :, :], a["L0_mix_Wqkv"].rearrange("(o p) f -> p o f", p=128)).then_inc(w_in, 16)
            act.dma_start(wpst[:, :, :], a["L0_mix_Wproj"].rearrange("(o p) f -> p o f", p=128)).then_inc(w_in, 16)
            for to, name in ((wqk[:, :, 0:F], "L0_gnn_Wq"), (wqk[:, :, F:2 * F], "L0_gnn_Wk"),
                             (t.w_late[:, :, 2 * F:3 * F], "L0_gnn_Wv")):
                act.dma_start(to, a[name].rearrange("(k p) n -> p k n", p=128)).then_inc(w_in, 16)
            act.dma_start(t.late_bias[:, 0:2 * F], a["L0_mix_bqkv"][F:3 * F].partition_broadcast(TP)).then_inc(w_in, 16)
            act.dma_start(t.late_bias[:, 3 * F:4 * F], a["L0_mix_bqkv"][0:F].partition_broadcast(TP)).then_inc(w_in, 16)
            act.wait_ge(var_ready, 1)
            act.activation(std[:, :], var[:, :], ACT.Sqrt).then_inc(std_ready, 1)
            act.wait_ge(w_in, 7 * 16)

        @block.tensor
        def _(pe):
            def places():
                pe.wait_ge(memsets, 1)
                pe.wait_ge(first_row, 1)
                pe.matmul(first_ps[:, :], t.ones[0:1, 0:NT], first_dst[:, :], start=True, stop=True).then_inc(firsts, 1)
                pe.wait_ge(before_ready, 1)
                pe.matmul(group_ps[:, :], t.ones[0:NT, 0:1], before[:, :], start=True, stop=True)
                pe.wait_ge(passed_ready, 1)
                pe.matmul(step_ps[:, :], t.ones[0:NT, 0:1], passed[:, :], start=True, stop=True).then_inc(steps_ready, 1)

            pe.wait_ge(c_in, 16)
            for i, (what, b, c) in enumerate(banks):
                if i == 4:
                    places()
                if i >= 4:
                    pe.wait_ge(drained, i - 3)
                if what == "edge":
                    pe.wait_ge(edge_float, 1 + b)
                    for j in range(EJ):
                        last = pe.transpose(tp[i % 4][:, j * 104:(j + 1) * 104],
                                            edge_f[:, b, c, j * 128:(j + 1) * 128], t.ident[0:104, 0:104])
                elif what == "mix":
                    pe.wait_ge(w_in, 7 * 16)
                    for j, o in enumerate(MIX_BLOCKS[c]):
                        last = pe.transpose(tp[i % 4][:, j * 128:(j + 1) * 128],
                                            wst[:, o, b * 128:(b + 1) * 128], t.ident[:, :])
                else:
                    for j in range(2):
                        last = pe.transpose(tp[i % 4][:, j * 128:(j + 1) * 128],
                                            wpst[:, j, b * 128:(b + 1) * 128], t.ident[:, :])
                last.then_inc(turned, 1)

        @block.vector
        def _(dve):
            order = Order(dve, dve_order)
            def stats(part):
                dve.wait_ge(x_in[part], 16)
                for u in range(part * U, (part + 1) * U):
                    dve.bn_stats(st[:, u, :], t.x_all[:, u, :]).then_inc(stats_done, 1)

            def drain(i):
                what, b, c = banks[i]
                dve.wait_ge(turned, i + 1)
                if what == "edge":
                    to = (t.dst_all, t.src_all)[b][:, c * 104:(c + 1) * 104, :]
                    src = tp[i % 4][:, 0:EJ * 104].rearrange("p (j g) -> p g j", j=EJ)
                elif what == "mix" and c == 0:
                    to, src = t.w_late[:, b, 0:384], tp[i % 4][:, 0:384]
                elif what == "mix":
                    dve.tensor_copy(t.w_late[:, b, 384:512], tp[i % 4][:, 0:128])
                    to, src = t.w_late[:, b, 3 * F:4 * F], tp[i % 4][:, 128:384]
                else:
                    to, src = t.wproj[:, b, :], tp[i % 4][:, 0:F]
                dve.tensor_copy(to, src).then_inc(drained, 1)

            dve.wait_ge(edge_in, 8 * 16)
            for kind in range(2):
                dve.tensor_copy(edge_f[:, kind, :, :], edge_i[:, kind, :, :]).then_inc(edge_float, 1)
            stats(0)
            for i in range(4):
                drain(i)
            dve.wait_ge(drained, 4)
            dve.tensor_copy(first_dst[:, :], t.dst_all[0:1, 0:N_GROUPS, 0]).then_inc(first_row, 1)
            stats(1)
            dve.wait_ge(small_in, 6 * 16)
            dve.wait_ge(firsts, 1)
            order(dve.tensor_scalar(before[:, :], first_ps[:, :], win_end[:, :], None, ALU.is_lt))
            dve.sem_inc(before_ready, 1)
            order(dve.tensor_reduce(last_group[:, 0:1], before[:, :], AX.X, ALU.add))
            order(dve.tensor_scalar(last_group[:, 1:2], last_group[:, 0:1], -1.0, 0.0, ALU.add, ALU.max))
            order(dve.tensor_tensor(last_group[:, 2:3], last_group[:, 1:2], win_id[:, :], ALU.add))
            order(dve.tensor_scalar(passed[:, :], count_w[:, :], last_group[:, 2:3], None, ALU.is_gt))
            dve.sem_inc(passed_ready, 1)
            stats(2)
            stats(3)
            dve.wait_ge(steps_ready, 1)
            order(dve.tensor_copy(row[:, 0, :], step_ps[:, :]))
            order(dve.tensor_tensor(row[:, 1, :], count[:, :], row[:, 0, :], ALU.subtract))
            order(dve.tensor_copy(t.step_w[:, :], row[:, 0, :]))
            order(dve.tensor_copy(t.step_g[:, :], row[:, 1, :]))
            order(dve.tensor_scalar(row[:, 2, 0:N_GROUPS], group_ps[:, :], -1.0, float(NT + 1),
                                    ALU.mult, ALU.add))
            order(dve.tensor_tensor(row[:, 2, 0:N_GROUPS], row[:, 2, 0:N_GROUPS], count[:, 0:N_GROUPS], ALU.add))
            for need, size in ((t.need_k, K_RING), (t.need_v, V_RING)):
                dve.memset(need[:, 0:size], 0)
                dve.tensor_copy(need[:, size:], row[:, 2, 1:N_GROUPS - size + 1])
            stats(4)
            dve.wait_ge(stats_done, NT)
            finish_stats(dve, order, st, mean, var, tmp).then_inc(var_ready, 1)
            for i in range(4, len(banks)):
                drain(i)
            dve.wait_ge(std_ready, 1)
            order(dve.reciprocal(rstd[:, :], std[:, :]))

    t.k_rows = Gather(m, "k", t.k_tab, K_RING)
    with Memory(nc) as s:
        xn_t = [s.sb(f"xn_t{j}", [TP, F]) for j in range(U)]
        xnT, again = ([s.sb(f"{name}{j}", [128, FC * TP]) for j in range(U)] for name in ("xnT", "xnT_again"))
        k_t = [s.sb(f"k_t{j}", [TP, F]) for j in range(U)]
        rest = [s.sb(f"rest{j}", [TP, F]) for j in range(U)]
        turn_ps = [s.ps(f"turn_ps{i}", [128, FC, TP]) for i in range(2)]
        proj_ps = [s.ps(f"proj_ps{j}", [TP, 512]) for j in range(U)]
        xn_ready, turned, xnT_ready, k_made, k_ready, q_made, hi_ready, rest_ready, mid_ready, q3_ready = (
            s.sem(x) for x in ("xn_ready", "turned", "xnT_ready", "k_made", "k_ready", "q_made", "hi_ready", "rest_ready",
                               "mid_ready", "q3_ready"))
        xnT_out, k_out, xnT_in = (s.sems(x, U) for x in ("xnT_out", "k_out", "xnT_again_in"))
        xn_out = s.gather_sems("xn_out", U)
        block = s.block()

        @block.sync
        def _(sp):
            def body(u, j, i, last):
                sp.wait_ge(k_ready, u + 1)
                sp.dma_start(t.k_tab[ds(u * TP, TP), :], k_t[j][:, :]).then_inc(k_out[j], 16)

            def reload(u, j, i, last):
                wait(sp, q_made, u - U + 1)
                sp.dma_start(again[j][:, :], t.xnT[:, u, :]).then_inc(xnT_in[j], 16)
            over_tiles(sp, body)
            for j in range(U):
                for out in (xnT_out, k_out):
                    sp.wait_ge(out[j], 16 * (NT // U))
            over_tiles(sp, reload)

        @block.gpsimd
        def _(pool):
            for sums in (t.mix.g_acc, t.mix.slv_acc, t.mix.coef):
                pool.memset(sums[:, :, :, :], 0.0)
            pool.memset(t.e_all[:, :, :], 0.0)

            def store_xn(u, j, i, last):
                pool.wait_ge(xn_ready, u + 1)
                pool.dma_start(t.xn_dram[ds(u * TP, TP), :], xn_t[j][:, :]).then_inc(xn_out[j], 16)
            over_tiles(pool, store_xn)
            for j in range(U):
                pool.wait_ge(xn_out[j], 16 * (NT // U))
            for j in range(U):
                pool.wait_ge(k_out[j], 16 * (NT // U))
            t.k_rows.first(pool, t)

        @block.vector
        def _(dve):
            def normalise(u, j, i):
                wait(dve, xn_out[j], i * 16)
                dve.tensor_scalar(xn_t[j][:, :], t.x_all[:, u, :], mean[:, ds(u, 1)], rstd[:, ds(u, 1)],
                                  ALU.subtract, ALU.mult).then_inc(xn_ready, 1)

            def ahead(u, j, i, last):
                if within(u + 2, NT):
                    normalise(u + 2, (j + 2) % U, i + (j + 2) // U)
                wait(dve, k_out[j], i * 16)
                dve.wait_ge(k_made, u + 1)
                dve.tensor_scalar(k_t[j][:, :], proj_ps[j][:, 0:F], 0.0, None, ALU.add).then_inc(k_ready, 1)

            def second(u, j):
                dve.wait_ge(hi_ready, u + 1)
                wait(dve, mid_ready, u - U + 1)
                dve.tensor_tensor(rest[j][:, :], proj_ps[j][:, 0:F], t.q3[:, u, 0:F], ALU.subtract).then_inc(rest_ready, 1)

            def split(u, j, i, last):
                if not last:
                    second(u + 1, (j + 1) % U)
                dve.wait_ge(mid_ready, u + 1)
                dve.tensor_tensor(t.q3[:, u, 2 * F:3 * F], rest[j][:, :], t.q3[:, u, F:2 * F], ALU.subtract).then_inc(q3_ready, 1)
            normalise(0, 0, 0)
            normalise(1, 1, 0)
            over_tiles(dve, ahead)
            second(0, 0)
            over_tiles(dve, split)

        @block.scalar
        def _(act):
            def turn_out(u, j, i, last):
                wait(act, xnT_out[j], i * 16)
                act.wait_ge(turned, u + 1)
                act.activation(xnT[j][:, :], turn_ps[j % 2][:, :, :].rearrange("p k n -> p (k n)"), ACT.Copy
                               ).then_inc(xnT_ready, 1)
                act.wait_ge(xnT_ready, u + 1)
                act.dma_start(t.xnT[:, u, :], xnT[j][:, :]).then_inc(xnT_out[j], 16)

            def first_part(u, j):
                act.wait_ge(q_made, u + 1)
                act.activation(t.q3[:, u, 0:F], proj_ps[j][:, 0:F], ACT.Copy).then_inc(hi_ready, 1)

            def body(u, j, i, last):
                if within(u + 2, NT):
                    first_part(u + 2, (j + 2) % U)
                act.wait_ge(rest_ready, u + 1)
                act.activation(t.q3[:, u, F:2 * F], rest[j][:, :], ACT.Copy).then_inc(mid_ready, 1)
            over_tiles(act, turn_out)
            for u in range(2):
                first_part(u, u)
            over_tiles(act, body)

        @block.tensor
        def _(pe):
            def turn(u, j):
                pe.wait_ge(xn_ready, u + 1)
                wait(pe, xnT_ready, psum_turn(u, j))
                for k in range(FC):
                    last = pe.transpose(turn_ps[j % 2][:, k, :], xn_t[j][:, k * 128:(k + 1) * 128],
                                        t.ident[0:TP, 0:TP])
                last.then_inc(turned, 1)

            def project(j, from_, cols):
                for k in range(FC):
                    mm = pe.matmul(proj_ps[j][:, 0:F], from_[j][:, k * TP:(k + 1) * TP], wqk[:, k, cols], start=(k == 0),
                                   stop=(k == FC - 1))
                return mm

            def make_k(u, j, i, last):
                if not last:
                    turn(u + 1, (j + 1) % U)
                pe.wait_ge(xnT_ready, u + 1)
                wait(pe, k_ready, u - U + 1)
                project(j, xnT, slice(F, 2 * F)).then_inc(k_made, 1)

            def make_q(u, j, i, last):
                wait(pe, rest_ready, u - U + 1)
                pe.wait_ge(xnT_in[j], i * 16 + 16)
                project(j, again, slice(0, F)).then_inc(q_made, 1)
            turn(0, 0)
            over_tiles(pe, make_k)
            pe.wait_ge(k_ready, NT)
            over_tiles(pe, make_q)


class Unit:

    def __init__(self, s, name, arrived, src, grow, factor):
        self.arrived, self.src, self.grow, self.factor = arrived, src, grow, factor
        self.sq = [s.sb(f"{name}_sq{j}", [TP, F]) for j in range(2)]
        self.nrm = [s.sb(f"{name}_nrm{j}", [TP, 5, HM]) for j in range(2)]
        self.unit = [s.sb(f"{name}_unit{j}", [TP, F]) for j in range(2)]
        self.rest = [s.sb(f"{name}_rest{j}", [TP, F]) for j in range(2)]
        self.parts = [s.sb(f"{name}_parts{j}", [TP, HM, 3, DM], BF16) for j in range(2)]
        self.turned_parts = [s.sb(f"{name}_T{j}", [3 * DM, HM, 128], BF16) for j in range(2)]
        self.turn_ps = s.ps(f"{name}_turn_ps", [3 * DM, HM, 128], BF16)
        (self.order, self.squared, self.rooted, self.scaled, self.rounded, self.rest_ready, self.middle, self.split,
         self.turned, self.ready) = (s.sem(f"{name}_{x}") for x in (
             "order", "squared", "rooted", "scaled", "rounded", "rest_ready", "middle", "split", "turned", "ready"))

    def heads(self, ap):
        return ap.rearrange("p (h d) -> p h d", h=HM)

    def dve_square(self, dve, u, j, i):
        self.arrived(dve, u, j, i)
        dve.tensor_tensor(self.sq[j][:, :], self.src(j), self.src(j), ALU.mult).then_inc(self.order, 1)

    def dve_sum(self, dve, u, j):
        dve.wait_ge(self.order, u * 4 + 1)
        dve.tensor_reduce(self.nrm[j][:, 0, :], self.heads(self.sq[j][:, :]), AX.X, ALU.add).then_inc(self.order, 1)

    def dve_floor(self, dve, u, j):
        dve.wait_ge(self.order, u * 4 + 2)
        dve.tensor_scalar(self.nrm[j][:, 1, :], self.nrm[j][:, 0, :], self.grow, 1e-24, ALU.mult, ALU.max
                          ).then_inc(self.squared, 1)

    def act_root(self, act, u, j):
        act.wait_ge(self.squared, u + 1)
        act.activation(self.nrm[j][:, 2, :], self.nrm[j][:, 1, :], ACT.Sqrt).then_inc(self.rooted, 1)

    def dve_invert(self, dve, u, j):
        dve.wait_ge(self.rooted, u + 1)
        dve.reciprocal(self.nrm[j][:, 3, :], self.nrm[j][:, 2, :]).then_inc(self.order, 1)

    def dve_grow(self, dve, u, j):
        dve.wait_ge(self.order, u * 4 + 3)
        dve.tensor_tensor(self.nrm[j][:, 4, :], self.nrm[j][:, 3, :], self.factor, ALU.mult).then_inc(self.order, 1)

    def dve_scale(self, dve, u, j):
        dve.wait_ge(self.order, u * 4 + 4)
        dve.tensor_tensor(self.heads(self.unit[j][:, :]), self.heads(self.src(j)),
                          bcast(self.nrm[j][:, 4, :].unsqueeze(2), TP, HM, DM), ALU.mult).then_inc(self.scaled, 1)

    def act_round(self, act, u, j):
        act.wait_ge(self.scaled, u + 1)
        act.activation(self.parts[j][:, :, 0, :], self.heads(self.unit[j][:, :]), ACT.Copy).then_inc(self.rounded, 1)

    def dve_rest(self, dve, u, j):
        dve.wait_ge(self.rounded, u + 3)
        dve.tensor_tensor(self.heads(self.rest[j][:, :]), self.heads(self.unit[j][:, :]), self.parts[j][:, :, 0, :],
                          ALU.subtract).then_inc(self.rest_ready, 1)

    def act_middle(self, act, u, j):
        act.wait_ge(self.rest_ready, u + 1)
        act.activation(self.parts[j][:, :, 1, :], self.heads(self.rest[j][:, :]), ACT.Copy).then_inc(self.middle, 1)

    def dve_last(self, dve, u, j):
        dve.wait_ge(self.middle, u + 1)
        dve.tensor_tensor(self.parts[j][:, :, 2, :], self.heads(self.rest[j][:, :]), self.parts[j][:, :, 1, :],
                          ALU.subtract).then_inc(self.split, 1)

    def pe_turn(self, pe, u, j, identb):
        pe.wait_ge(self.split, u + 1)
        wait(pe, self.ready, u)
        for h in range(HM):
            mm = pe.transpose(self.turn_ps[:, h, 0:TP], self.parts[j][:, h, :, :].rearrange("p a d -> p (a d)"),
                              identb[0:TP, 0:TP])
        return mm

    def act_turn_out(self, act, u, j):
        act.wait_ge(self.turned, u + 1)
        act.activation(self.turned_parts[j][:, :, 0:TP], self.turn_ps[:, :, 0:TP], ACT.Copy).then_inc(self.ready, 1)


def over_slots(eng, body):
    def round_(i, count):
        for c in range(count):
            body(i * 2 + c // SLOTS, c // SLOTS % 2, c % SLOTS, i * 2 * SLOTS + c, c, i)
    round_(0, 2 * SLOTS)
    with eng.Fori(1, NT // 2 - 1) as i:
        round_(i, 2 * SLOTS)
    round_(NT // 2 - 1, 2 * SLOTS)
    round_(NT // 2, SLOTS + 1)


def load_step(eng, table, s, most):
    return eng.value_load(table[0:1, ds(s, 1)], min_val=0, max_val=most)


class Gather:

    def __init__(self, m, name, table, size):
        self.table, self.size = table, size
        self.ring = m.sb(f"{name}_ring", [128, size, EJ, F])
        self.idx = [m.sb(f"{name}_idx{i}", [128, size // 2, EJ], I32) for i in range(2)]
        self.idx_ready, self.landed, self.carrier = (m.sem(f"{name}_{x}") for x in ("idx_ready", "landed", "g_carrier"))
        self.landed_slot = m.gather_sems(f"{name}_landed_slot", size)

    def place(self, pool, t, half, i):
        size = self.size // 2
        for slot in range(half * size, (half + 1) * size):
            wait(pool, self.landed_slot[slot], i * 16 * EJ)
        pool.sem_inc(self.carrier, 1)
        pool.tensor_copy(self.idx[half][:, :, :], t.src_all[:, ds(i * self.size + half * size, size), :]).then_inc(self.idx_ready, 1)

    def fetch(self, pool, slot, i):
        half, at = divmod(slot, self.size // 2)
        pool.wait_ge(self.idx_ready, i * 2 + half + 1)
        pool.sem_inc(self.carrier, 1)
        for j in range(EJ):
            pool.indirect_dma_start(out=self.ring[:, slot, j, :], out_offset=None, in_=self.table,
                                    in_offset=bass.IndirectOffsetOnAxis(ap=self.idx[half][:, at, j:j + 1], axis=0)
                                    ).then_inc(self.landed_slot[slot], 16)

    def land(self, pool, slot, i):
        pool.wait_ge(self.landed_slot[slot], (i + 1) * 16 * EJ)
        pool.sem_inc(self.landed, 1)

    def first(self, pool, t):
        for half in range(2):
            self.place(pool, t, half, 0)
        for slot in range(self.size):
            self.fetch(pool, slot, 0)
            if slot > 0:
                self.land(pool, slot - 1, 0)
            if slot == self.size // 2 + 1:
                self.place(pool, t, 0, 1)

    def rest(self, pool, t, needed, steps_done):
        size = self.size
        rounds, left = divmod(N_GROUPS, size)

        def body(slot, i):
            need = pool.value_load(needed[0:1, ds(i * size + slot, 1)], min_val=0, max_val=N_STEPS)
            pool.wait_ge(steps_done, need)
            self.fetch(pool, slot, i)
            self.land(pool, (slot - 1) % size, i if slot else i - 1)
            if slot == 1 and within(i * size + size // 2, N_GROUPS):
                self.place(pool, t, 1, i)
            if slot == size // 2 + 1 and within(i * size + size, N_GROUPS):
                self.place(pool, t, 0, i + 1)

        with pool.Fori(1, rounds) as i:
            for slot in range(size):
                body(slot, i)
        for slot in range(left):
            body(slot, rounds)
        self.land(pool, (left - 1) % size, rounds if left else rounds - 1)
        pool.wait_ge(steps_done, N_STEPS + 1)


def stage_scores_and_sums(nc, a, t):
    x = t.mix
    with Memory(nc) as s:
        rows = t.k_rows
        dst_row = [s.sb(f"dst_row{i}", [TP, GE], I32) for i in range(2)]
        spread = [s.sb(f"spread{i}", [TP, GE], BF16) for i in range(2)]
        away = s.sb("away", [TP, GE])
        prod = [s.sb(f"prod{i}", [128, EJ * F]) for i in range(2)]
        score = [s.sb(f"score{i}", [128, EJ, HG]) for i in range(2)]
        q_ps = [s.ps(f"q_ps{i}", [128, EJ * F]) for i in range(2)]
        xnT = [t.late[:, j, 0:FC * TP].rearrange("p (k n) -> p k n", k=FC) for j in range(2)]
        kv, vq = ([t.late[0:TP, 2 * j + b:2 * j + b + 2, :].rearrange("p b f -> p (b f)") for j in range(2)] for b in (2, 6))
        ksq = [s.sb(f"ksq{j}", [TP, F]) for j in range(2)]
        v1 = [s.sb(f"v1{j}", [TP, HM, V1]) for j in range(2)]
        phi = s.sb("phi", [TP, NPAIR])
        f_ps = s.ps("kf_ps", [TP, NPAIR])
        sums_ps = s.ps("sums_ps", [128, 512])
        g_ps = sums_ps[0:PB, 0:NPB * V1].rearrange("p (b e) -> p b e", b=NPB)
        slv_ps = sums_ps[:, NPB * V1:NPB * V1 + 2 * HW].rearrange("p (a e) -> p a e", a=2)
        late_ps = s.ps("late_ps", [TP, 2 * F])
        steps_done = s.sem("k_steps_done")
        row_in = s.sems("dst_row_in", 2)
        away_ready, spread_ready, q_ready, dve_order, a_carrier = (
            s.sem(n) for n in ("away_ready", "spread_ready", "q_ready", "k_dve_order", "k_a_carrier"))
        c_in, xnT_in, vq_out = s.sem("mixc_in"), s.sems("late_xnT_in", 2), s.sems("late_vq_out", 2)
        late_ready, late_read = s.sem("late_ready"), s.sem("late_read")
        ksq_ready, v1_ready, f_ready, phi_ready, g_ready, g_read, slv_ready, slv_read, cleared, start = (
            s.sem("k_" + n) for n in ("sq", "v1", "f", "phi", "g", "g_read", "slv", "slv_read", "cleared", "start"))
        k_ = Unit(s, "mk", lambda eng, u, j, i: eng.wait_ge(late_read, u * 2 + 1), lambda j: kv[j][:, 0:F], 1.0, x.k_factor[:, :])
        block = s.block()

        @block.gpsimd
        def _(pool):
            rows.rest(pool, t, t.need_k, steps_done)

        @block.sync
        def _(sp):
            def load(u, j):
                wait(sp, late_ready, u * 2 - 2)
                sp.dma_start(xnT[j], t.xnT[:, u, :].rearrange("p (k n) -> p k n", k=FC)).then_inc(xnT_in[j], 16)
            for u in range(2):
                load(u, u)
            for ap, src in ((x.pair3, a["c_pair3"]), (x.pair4, a["c_pair4"]),
                            (x.q_factor, a["L0_mix_temperature"][0, :, 0, 0].partition_broadcast(TP)),
                            (x.proj_bias, a["L0_mix_bproj"].partition_broadcast(TP))):
                sp.dma_start(ap[:, :], src).then_inc(c_in, 16)
            sp.dma_start(x.pairT[:, :, :], a["c_pairT"]).then_inc(c_in, 16)


            def store(u, j):
                sp.wait_ge(late_read, u * 2 + 2)
                sp.dma_start(t.v_tab[ds(u * TP, TP), :], vq[j][:, 0:F]).then_inc(vq_out[j], 16)
                sp.dma_start(t.mix_q[ds(u * TP, TP), :], vq[j][:, F:2 * F]).then_inc(vq_out[j], 16)

            def body(u, j, k, n, c, i):
                g = load_step(sp, t.step_g, n, N_GROUPS - 1)
                wait(sp, spread_ready, n - 1)
                sp.dma_start(dst_row[c % 2][:, :], t.dst_pad[ds(g * GE + 1, GE)].partition_broadcast(TP)
                             ).then_inc(row_in[c % 2], 16)
                if isinstance(n, int) and n == 1:
                    store(0, 0)
                if k == 1 and within(u + 2, NT):
                    load(u + 2, j)
                if k == 1 and within(u + 1, NT):
                    store(u + 1, 1 - j)
            over_slots(sp, body)
            for j in range(2):
                sp.wait_ge(vq_out[j], (NT + 1 - j) // 2 * 32)

        @block.vector
        def _(dve):
            def late(u, j, i, kind):
                dve.wait_ge(late_ready, u * 2 + kind + 1)
                if kind == 0:
                    dve.wait_ge(k_.rounded, u + 1)
                else:
                    wait(dve, vq_out[j], i * 32)
                dve.tensor_tensor((kv, vq)[kind][j], late_ps[:, :], t.late_bias[:, kind * 2 * F:(kind + 1) * 2 * F],
                                  ALU.add).then_inc(late_read, 1)

            held = Shared()

            def add_scores(n, c, g):
                dve.wait_ge(dve_order, n * 2 + 2)
                at = t.e_all[:, :, ds(g * EJ, EJ)]
                dve.tensor_tensor(at, at, score[c % 2][:, :, :].rearrange("p j h -> p h j"), ALU.add).then_inc(dve_order, 1)

            def body(u, j, k, n, c, i):
                more, nxt = within(u + 1, NT), (u + 1, 1 - j)
                if more and k == 0:
                    k_.dve_square(dve, *nxt, i + j)
                elif more and k == 2:
                    k_.dve_invert(dve, *nxt)
                g = load_step(dve, t.step_g, n, N_GROUPS - 1)
                slot = g & (K_RING - 1)
                dve.wait_ge(q_ready, n + 1)
                dve.wait_ge(rows.landed, g + 1)
                dve.tensor_tensor(prod[c % 2][:, :], rows.ring[:, slot, :, :].rearrange("p j f -> p (j f)"), q_ps[c % 2][:, :],
                                  ALU.mult).then_inc(steps_done, 1)
                if more and k == 0:
                    k_.dve_sum(dve, *nxt)
                elif more and k == 2:
                    k_.dve_grow(dve, *nxt)
                if c == 0 and not (isinstance(n, int) and n == 0):
                    held.g = load_step(dve, t.step_g, n - 1, N_GROUPS - 1)
                if not (isinstance(n, int) and n == 0):
                    add_scores(n - 1, c + 1, held.g)
                held.g = g
                if k > 0:
                    h = k - 1
                    dve.wait_ge(g_ready, u * HM + h + 1)
                    wait(dve, g_read, u * HM + h)
                    dve.tensor_tensor(x.g_acc[:, h, :, :], x.g_acc[:, h, :, :], g_ps[:, :, :], ALU.add).then_inc(g_read, 1)
                if k % 3 == 1:
                    kind, parts = k // 3, 1 if k // 3 == 2 else 128
                    dve.wait_ge(slv_ready, u * 3 + kind + 1)
                    wait(dve, slv_read, u * 3 + kind)
                    at = x.slv_acc[0:parts, kind, :, :]
                    dve.tensor_tensor(at, at, slv_ps[0:parts, :, :], ALU.add).then_inc(slv_read, 1)
                if k in (3, 6) and within(u + 2, NT):
                    late(u + 2, j, i + 1, k // 3 - 1)
                if more and k == 0:
                    k_.dve_floor(dve, *nxt)
                elif more and k == 2:
                    k_.dve_scale(dve, *nxt)
                elif more and k == 4:
                    k_.dve_rest(dve, *nxt)
                elif more and k == 6:
                    k_.dve_last(dve, *nxt)
                dve.wait_ge(steps_done, n + 2)
                dve.tensor_reduce(score[c % 2][:, :, :], prod[c % 2][:, :].rearrange("p (j h d) -> p j h d", j=EJ, h=HG),
                                  AX.X, ALU.add).then_inc(dve_order, 1)
            dve.memset(x.k_factor[:, :], SCALE)
            for j in range(2):
                dve.memset(v1[j][:, :, 0:1], 1.0 / N)
            dve.wait_ge(c_in, 5 * 16)
            dve.tensor_scalar(x.q_factor[:, :], x.q_factor[:, :], SCALE * SCALE, None, ALU.mult).then_inc(cleared, 1)
            dve.sem_inc(dve_order, 1)
            dve.sem_inc(steps_done, 1)
            dve.wait_ge(cleared, 1)
            late(0, 0, 0, 0)
            k_.dve_square(dve, 0, 0, 0)
            k_.dve_sum(dve, 0, 0)
            k_.dve_floor(dve, 0, 0)
            late(0, 0, 0, 1)
            k_.dve_invert(dve, 0, 0)
            k_.dve_grow(dve, 0, 0)
            k_.dve_scale(dve, 0, 0)
            late(1, 1, 0, 0)
            k_.dve_rest(dve, 0, 0)
            late(1, 1, 0, 1)
            k_.dve_last(dve, 0, 0)
            over_slots(dve, body)
            add_scores(N_STEPS - 1, N_STEPS - 1, held.g)

        @block.scalar
        def _(act):
            act.preload_act_table(ACT.Sqrt)
            act.sem_inc(k_.rounded, 2)

            def round_(u, j, i):
                act.wait_ge(late_read, u * 2 + 1)
                act.activation(v1[j][:, :, 1:V1], kv[j][:, F:2 * F].rearrange("p (h d) -> p h d", h=HM), ACT.Copy,
                               scale=1.0 / N).then_inc(v1_ready, 1)
                k_.act_round(act, u, j)
                act.activation(ksq[j][:, :], k_.unit[j][:, :], ACT.Square).then_inc(ksq_ready, 1)

            def spread_rows(n, c, i):
                w = load_step(act, t.step_w, n, NT - 1)
                act.wait_ge(row_in[c % 2], (i * SLOTS + c // 2 + 1) * 16)
                wait(act, spread_ready, n)
                act.sem_inc(a_carrier, 1)
                act.activation(away[:, :], dst_row[c % 2][:, :], ACT.Square, bias=t.win_node[:, ds(w, 1)]).then_inc(away_ready, 1)
                wait(act, q_ready, n - 1)
                act.wait_ge(away_ready, n + 1)
                act.activation(spread[c % 2][:, :], away[:, :], ACT.Relu, bias=1.0, scale=-1.0).then_inc(spread_ready, 1)

            def body(u, j, k, n, c, i):
                if within(u, NT) and k < HM:
                    act.wait_ge(f_ready, u * HM + k + 1)
                    act.activation(phi[:, :], f_ps[:, :], ACT.Square).then_inc(phi_ready, 1)
                if within(n + 2, N_STEPS):
                    spread_rows(n + 2, c + 2, i)
                if within(u + 1, NT):
                    nxt = (u + 1, 1 - j)
                    if k == 1:
                        k_.act_root(act, *nxt)
                    elif k == 3:
                        round_(*nxt, i + j)
                    elif k == 5:
                        k_.act_middle(act, *nxt)
                    elif k == 8:
                        k_.act_turn_out(act, *nxt)
            spread_rows(0, 0, 0)
            spread_rows(1, 1, 0)
            act.wait_ge(cleared, 1)
            k_.act_root(act, 0, 0)
            round_(0, 0, 0)
            k_.act_middle(act, 0, 0)
            k_.act_turn_out(act, 0, 0)
            over_slots(act, body)

        @block.tensor
        def _(pe):
            def q_of_edges(n, c):
                w = load_step(pe, t.step_w, n, NT - 1)
                pe.wait_ge(spread_ready, n + 1)
                wait(pe, steps_done, n)
                for e in range(EJ):
                    for part in range(3):
                        mm = pe.matmul(q_ps[c % 2][:, e * F:(e + 1) * F], spread[c % 2][:, e * 128:(e + 1) * 128],
                                       t.q3[:, w, part * F:(part + 1) * F], start=(part == 0), stop=(part == 2))
                mm.then_inc(q_ready, 1)

            def late(u, j, i, kind):
                pe.wait_ge(xnT_in[j], i * 16 + 16)
                wait(pe, late_read, u * 2 + kind)
                for b in range(FC):
                    mm = pe.matmul(late_ps[:, :], xnT[j][:, b, :], t.w_late[:, b, kind * 2 * F:(kind + 1) * 2 * F],
                                   start=(b == 0), stop=(b == FC - 1))
                mm.then_inc(late_ready, 1)

            def sums(u, j, kind):
                wait(pe, slv_read, u * 3 + kind)
                wait(pe, g_read, u * HM + 3 * kind)
                parts = 1 if kind == 2 else 128
                for half in range(2):
                    lhsT = (t.ones[0:TP, 0:1] if kind == 2 else
                            (ksq[j] if kind == 0 else k_.unit[j])[:, half * 128:(half + 1) * 128])
                    mm = pe.matmul(slv_ps[0:parts, half, :], lhsT, v1[j][:, 4 * half:4 * half + 4, :].rearrange("p h e -> p (h e)"),
                                   start=True, stop=True)
                mm.then_inc(slv_ready, 1)

            def body(u, j, k, n, c, i):
                tile = within(u, NT)
                if tile and k == 0:
                    pe.wait_ge(k_.ready, u + 1)
                    pe.wait_ge(ksq_ready, u + 1)
                    pe.wait_ge(v1_ready, u + 1)
                    pe.sem_inc(start, 1)
                if tile and k < HM:
                    pe.matmul(f_ps[:, :], k_.turned_parts[j][:, k, 0:TP], x.pair3[:, :], start=True, stop=True).then_inc(f_ready, 1)
                if within(n + 1, N_STEPS):
                    q_of_edges(n + 1, c + 1)
                if tile and k % 3 == 0:
                    sums(u, j, k // 3)
                if tile and k < HM:
                    pe.wait_ge(phi_ready, u * HM + k + 1)
                    wait(pe, g_read, u * HM + k)
                    if k % 3 == 1:
                        pe.wait_ge(slv_read, u * 3 + k // 3 + 1)
                    for b in range(NPB):
                        mm = pe.matmul(g_ps[:, b, :], phi[:, b * PB:(b + 1) * PB], v1[j][:, k, :], start=True, stop=True)
                    mm.then_inc(g_ready, 1)
                if k in (2, 5) and within(u + 2, NT):
                    late(u + 2, j, i + 1, k // 3)
                if k == 7 and within(u + 1, NT):
                    k_.pe_turn(pe, u + 1, 1 - j, t.identb).then_inc(k_.turned, 1)
            for u in range(2):
                for kind in range(2):
                    late(u, u, 0, kind)
            q_of_edges(0, 0)
            k_.pe_turn(pe, 0, 0, t.identb).then_inc(k_.turned, 1)
            over_slots(pe, body)


def stage_edge_softmax(nc, a, t):
    NB = HG * ET_PAD // 104
    NR = NB // 4
    NTP = 3
    x = t.mix
    with Memory(nc) as s:
        x_flat, xn_flat = (buf[:, :, :].rearrange("p t f -> p (t f)") for buf in (t.x_buf, t.xn_buf))
        eT = x_flat[0:104, 0:NB * 128].rearrange("p (b e) -> p b e", b=NB)
        dst = s.sb("es_dst", [128, CE + 2], I32)
        pen = xn_flat[:, 0:CE + 1]
        e = s.sb("es_e", [128, CE])
        run = s.sb("es_run", [128, CE])
        ends = s.sb("ends", [128, 6])
        rows = xn_flat[0:1, CE + 1:CE + 1 + 4 * 128].rearrange("p (a b) -> p a b", a=4)
        carry = xn_flat[0:1, CE + 1 + 4 * 128:CE + 1 + 4 * 128 + 2 * 129].rearrange("p (a b) -> p a b", a=2)
        start = s.sb("es_start", [128, 2])
        tp = [s.ps(f"es_tp{i}", [128, 512]) for i in range(NTP)]
        rs_ps = [s.ps(f"rs_ps{i}", [PB, NPB, V1]) for i in range(2)]
        m_ps = s.ps("m_ps", [128, 2, V1])
        rs_ready, m_half, m_ready, c_order = s.sem("rs_ready"), s.sem("m_half"), s.sem("m_ready"), s.sem("coef_order")
        row_ps, start_ps = s.ps("row_ps", [1, 4, 128]), s.ps("start_ps", [128, 2])
        turned, drained, e_in, dst_in = (s.sem(x) for x in ("es_turned", "es_drained", "e_in", "es_dst_in"))
        e_out = s.sems("e_out", HG)
        dve_order, ends_ready, rows_ready, carry_ready, start_ready = (
            s.sem(x) for x in ("es_order", "ends_ready", "es_rows_ready", "carry_ready", "es_start_ready"))
        less_max, exp_ready, late_in = s.sem("less_max"), s.sem("exp_ready"), s.sem("late_in")
        ex_out, ex_in = s.sems("ex_out", HG), s.sems("ex_in", HG)
        block = s.block()

        @block.gpsimd
        def _(pool):
            t.v_rows.first(pool, t)

        @block.sync
        def _(sp):
            for h in range(HG):
                at = slice(h * CHUNKS, (h + 1) * CHUNKS)
                for first, col, width in ((1, 1, CE), (0, 0, 1), (CE + 1, CE + 1, 1)):
                    src = t.dst_pad[0:E_PAD] if first == 0 else t.dst_pad[1:1 + E_PAD] if first == 1 else t.dst_pad[2:2 + E_PAD]
                    src = src.rearrange("(k c) -> k c", c=CE)
                    src = src if first == 1 else src[:, 0:1] if first == 0 else src[:, CE - 1:CE]
                    sp.dma_start(dst[at, col:col + width], src, allow_slow_non_contiguous=True).then_inc(dst_in, 16)
            per = NB // HG
            at = [slice(h * CHUNKS, (h + 1) * CHUNKS) for h in range(HG)]
            for h in range(HG):
                sp.wait_ge(drained, (h + 1) * NR // HG)
                sp.dma_start(t.e_dram[h].rearrange("(b t p) -> t b p", t=104, p=128), eT[:, h * per:(h + 1) * per, :]).then_inc(e_out[h], 16)
            for h in range(HG):
                sp.wait_ge(e_out[h], 16)
                sp.dma_start(e[at[h], :], t.e_dram[h].rearrange("(k c) -> k c", c=CE)).then_inc(e_in, 16)
            sp.wait_ge(e_in, HG * 16)
            sp.dma_start(t.iota_n[:, :], a["c_iota"][0, :].partition_broadcast(128)).then_inc(late_in, 16)
            sp.wait_ge(exp_ready, 1)
            for h in range(HG):
                sp.dma_start(t.ex_dram[h].rearrange("(k c) -> k c", c=CE), run[at[h], :]).then_inc(ex_out[h], 16)
            for h in range(HG):
                sp.wait_ge(ex_out[h], 16)
                sp.dma_start(eT[:, h * per:(h + 1) * per, :], t.ex_dram[h].rearrange("(b t p) -> t b p", t=104, p=128)).then_inc(ex_in[h], 16)
            sp.wait_ge(late_in, 16)

        @block.tensor
        def _(pe):
            for r in range(NR):
                if r >= NTP:
                    pe.wait_ge(drained, r - NTP + 1)
                for i in range(4):
                    b = 4 * r + i
                    mm = pe.transpose(tp[r % NTP][0:104, i * 128:(i + 1) * 128], t.e_flat[:, b * 104:(b + 1) * 104], t.ident[:, :])
                mm.then_inc(turned, 1)
            for h in range(HM):
                at, cols = slice(32 * (h % 4), 32 * (h % 4) + 32), slice((h % 4) * V1, (h % 4 + 1) * V1)
                if h >= 2:
                    pe.wait_ge(m_half, h - 1)
                for b in range(NPB):
                    mm = pe.matmul(rs_ps[h % 2][:, b, :], x.pair4[at, b * PB:(b + 1) * PB], x.slv_acc[at, 0, h // 4, cols],
                                   start=True, stop=True)
                mm.then_inc(rs_ready, 1)
            for h in range(HM):
                pe.wait_ge(m_half, h + 1)
                at = slice(32 * (h % 4), 32 * (h % 4) + 32)
                for b in range(NPB):
                    mm = pe.matmul(m_ps[at, h // 4, :], x.pairT[:, b, :], x.g_acc[:, h, b, :], start=(b == 0), stop=(b == NPB - 1))
                mm.then_inc(m_ready, 1)
            pe.wait_ge(ends_ready, 1)
            for i in range(4):
                mm = pe.transpose(row_ps[:, i, :], ends[:, i:i + 1], t.ident[:, :])
            mm.then_inc(rows_ready, 1)
            pe.wait_ge(carry_ready, 1)
            pe.transpose(start_ps[:, 0:1], carry[:, 0, 0:128], t.ident[0:1, 0:1])
            pe.transpose(start_ps[:, 1:2], carry[:, 1, 1:129], t.ident[0:1, 0:1]).then_inc(start_ready, 1)
            for r in range(NR):
                pe.wait_ge(ex_in[r * HG // NR], 16)
                pe.wait_ge(drained, NR + r - NTP + 1)
                for i in range(4):
                    mm = pe.transpose(tp[r % NTP][:, i * 104:(i + 1) * 104], eT[:, 4 * r + i, :], t.ident[0:104, 0:104])
                mm.then_inc(turned, 1)

        @block.scalar
        def _(act):
            act.preload_act_table(ACT.Exp)
            for r in range(NR):
                act.wait_ge(turned, r + 1)
                act.activation(eT[:, 4 * r:4 * r + 4, :], tp[r % NTP][0:104, :].rearrange("t (b p) -> t b p", b=4),
                               ACT.Copy).then_inc(drained, 1)
            act.wait_ge(less_max, 1)
            act.activation(run[:, :], run[:, :], ACT.Exp, scale=1.0 / float(F) ** 0.5).then_inc(exp_ready, 1)
            for r in range(NR):
                act.wait_ge(turned, NR + r + 1)
                act.activation(t.e_flat[:, 4 * r * 104:(4 * r + 4) * 104], tp[r % NTP][:, 0:416], ACT.Copy).then_inc(drained, 1)

        @block.vector
        def _(dve):
            order = Order(dve, dve_order)
            dve.wait_ge(dst_in, 3 * HG * 16)
            order(dve.tensor_tensor(pen[:, :], dst[:, 1:CE + 2], dst[:, 0:CE + 1], ALU.is_equal))
            order(dve.tensor_scalar(pen[:, :], pen[:, :], -1.0, BIG, ALU.add, ALU.mult))
            order(dve.tensor_tensor(ends[:, 4:5], dst[:, 1:2], dst[:, CE:CE + 1], ALU.is_equal))
            order(dve.tensor_scalar(ends[:, 5:6], ends[:, 4:5], -1.0, BIG, ALU.add, ALU.mult))
            order(dve.tensor_tensor(ends[:, 2:3], ends[:, 5:6], pen[:, 0:1], ALU.add))
            order(dve.tensor_tensor(ends[:, 3:4], ends[:, 5:6], pen[:, CE:CE + 1], ALU.add))
            order(dve.memset(carry[:, :, :], -BIG))
            coef_order = Order(dve, c_order)
            for h in range(HM):
                dve.wait_ge(rs_ready, h + 1)
                coef_order(dve.tensor_tensor(x.g_acc[:, h, :, :], x.g_acc[:, h, :, :], rs_ps[h % 2][:, :, :], ALU.subtract))
                dve.tensor_scalar(x.g_acc[:, h, :, :], x.g_acc[:, h, :, :], 0.25, None, ALU.mult).then_inc(m_half, 1)
            dve.wait_ge(m_ready, HM)
            for h in range(HM):
                at, cols = slice(32 * (h % 4), 32 * (h % 4) + 32), slice((h % 4) * V1, (h % 4 + 1) * V1)
                dve.scalar_tensor_tensor(x.coef[at, 0, h // 4, cols], x.slv_acc[at, 0, h // 4, cols], 0.5,
                                         m_ps[at, h // 4, :], ALU.mult, ALU.subtract)
                dve.tensor_scalar(x.coef[at, 1, h // 4, cols], x.slv_acc[at, 1, h // 4, cols], SCALE ** 2, None, ALU.mult)
            coef_order(dve.tensor_scalar(x.slv_acc[0:1, 2, :, :], x.slv_acc[0:1, 2, :, :], SCALE ** 4, None, ALU.mult))
            dve.wait_ge(e_in, HG * 16)
            scan = dve.tensor_tensor_scan
            order(scan(run[:, :], pen[:, 0:CE], e[:, :], -BIG, ALU.add, ALU.max))
            order(dve.tensor_copy(ends[:, 0:1], run[:, CE - 1:CE]))
            order(scan(run[:, ::-1], pen[:, CE:0:-1], e[:, ::-1], -BIG, ALU.add, ALU.max))
            order(dve.tensor_copy(ends[:, 1:2], run[:, 0:1]))
            dve.sem_inc(ends_ready, 1)
            dve.wait_ge(rows_ready, 1)
            order(dve.tensor_copy(rows[:, :, :], row_ps[:, :, :]))
            order(scan(carry[:, 0, 1:129], rows[:, 2, :], rows[:, 0, :], -BIG, ALU.add, ALU.max))
            order(scan(carry[:, 1, 127::-1], rows[:, 3, ::-1], rows[:, 1, ::-1], -BIG, ALU.add, ALU.max))
            dve.sem_inc(carry_ready, 1)
            dve.wait_ge(start_ready, 1)
            order(dve.tensor_copy(start[:, :], start_ps[:, :]))
            order(scan(run[:, :], pen[:, 0:CE], e[:, :], start[:, 0:1], ALU.add, ALU.max))
            order(scan(run[:, ::-1], pen[:, CE:0:-1], run[:, ::-1], start[:, 1:2], ALU.add, ALU.max))
            dve.tensor_tensor(run[:, :], e[:, :], run[:, :], ALU.subtract).then_inc(less_max, 1)


def stage_aggregate_and_mix(nc, a, t):
    FD = F + HG
    x = t.mix
    with Memory(nc) as s:
        xn_flat, taken = t.xn_buf[:, :, :].rearrange("p t f -> p (t f)"), [0]

        def spare(parts, *shape):
            at, size = taken[0], int(np.prod(shape))
            taken[0] += size
            flat = xn_flat[0:parts, at:at + size]
            names = "abc"[:len(shape)]
            return flat if len(shape) == 1 else flat.rearrange(f"p ({' '.join(names)}) -> p {' '.join(names)}", **dict(zip(names[1:], shape[1:])))
        hot = [spare(128, EJ, TP) for i in range(2)]
        val = [spare(128, EJ, FD) for i in range(2)]
        sum_ps = [s.ps(f"sum_ps{i}", [TP, FD]) for i in range(2)]
        val_ready, sum_ready, sum_read, cleared = s.sem("val_ready"), s.sem("sum_ready"), s.sem("sum_read"), s.sem("cleared")
        mq = [spare(TP, F) for j in range(2)]
        qT = [spare(128, 2, FC, TP) for j in range(2)]
        phi = spare(PB, NPB, TP)
        inv = [s.sb(f"y_inv{j}", [TP, HM]) for j in range(2)]
        y = [spare(TP, F) for j in range(2)]
        yT = [spare(128, FC, TP) for j in range(2)]
        biased = spare(TP, F)
        qT_ps = s.ps("qT_ps", [128, FC, TP])
        f_ps = s.ps("qf_ps", [PB, NPB, TP])
        y_ps = s.ps("y_ps", [TP, HM, V1])
        yT_ps = s.ps("yT_ps", [128, FC, TP])
        out_ps = s.ps("out_ps", [TP, F])
        mq_in, x_in = s.sems("mq_in", 2), s.sem("q_x_in")
        qT_ready, f_ready, phi_ready, y_summed, inv_ready, y_ready, yT_turned, yT_ready, out_ready, biased_ready, start = (
            s.sem("q_" + n) for n in ("T2", "f", "phi", "sum", "inv", "y", "yT_turned", "yT", "out", "biased", "start"))
        q = Unit(s, "mq", lambda eng, u, j, i: eng.wait_ge(mq_in[j], i * 16 + 16), lambda j: mq[j][:, :], SCALE * SCALE, x.q_factor[:, :])
        block = s.block()

        @block.gpsimd
        def _(pool):
            pool.memset(t.acc[:, :, :], 0.0).then_inc(cleared, 1)
            t.v_rows.rest(pool, t, t.need_v, val_ready)

        @block.sync
        def _(sp):
            def load(u, j):
                sp.wait_ge(q.rounded, u + 1)
                sp.dma_start(mq[j][:, :], t.mix_q[ds(u * TP, TP), :]).then_inc(mq_in[j], 16)
            for u in range(2):
                load(u, u % 2)
            sp.dma_start(t.x_all[:, :, :], a["x"].rearrange("(t p) f -> p t f", p=TP)).then_inc(x_in, 16)
            with sp.Fori(1, NT // 2) as i:
                for j in range(2):
                    load(i * 2 + j, j)
            load(NT - 1, 0)

        @block.vector
        def _(dve):
            def weigh(n, c):
                w = load_step(dve, t.step_w, n, NT - 1)
                g = load_step(dve, t.step_g, n, N_GROUPS - 1)
                slot = g & (V_RING - 1)
                ex = t.e_all[:, :, ds(g * EJ, EJ)].rearrange("p h j -> p j h")
                dve.tensor_tensor(hot[c % 2][:, :, :], bcast(t.iota_n[:, ds(w * TP, TP)].unsqueeze(1), 128, EJ, TP),
                                  bcast(t.dst_all[:, g, :].unsqueeze(2), 128, EJ, TP), ALU.is_equal)
                dve.tensor_scalar(val[c % 2][:, :, F:FD], ex, 1.0, None, ALU.mult)
                dve.wait_ge(t.v_rows.landed, g + 1)
                dve.tensor_tensor(val[c % 2][:, :, 0:F].rearrange("p j (h d) -> p j h d", h=HG),
                                  t.v_rows.ring[:, slot, :, :].rearrange("p j (h d) -> p j h d", h=HG),
                                  bcast(ex.unsqueeze(3), 128, EJ, HG, DG), ALU.mult).then_inc(val_ready, 1)
                return w

            def add_bias(u):
                dve.wait_ge(out_ready, u + 1)
                dve.tensor_tensor(biased[:, :], out_ps[:, :], x.proj_bias[:, :], ALU.add).then_inc(biased_ready, 1)

            def onto_x(u):
                dve.wait_ge(x_in, 16)
                dve.wait_ge(biased_ready, u + 1)
                dve.tensor_tensor(t.x_all[:, u, :], t.x_all[:, u, :], biased[:, :], ALU.add)

            held = Shared()

            def body(u, j, k, n, c, i):
                more, nxt = within(u + 1, NT), (u + 1, 1 - j)
                former = k == 3 and within(1, u + 1 if isinstance(u, int) else 2)
                if more and k == 0:
                    q.dve_square(dve, *nxt, i + j)
                elif more and k == 2:
                    q.dve_invert(dve, *nxt)
                if former:
                    add_bias(u - 1)
                w = held.w if c or isinstance(n, int) and n == 0 else load_step(dve, t.step_w, n, NT - 1)
                if within(n + 1, N_STEPS):
                    held.w = weigh(n + 1, c + 1)
                if k == 8:
                    dve.wait_ge(y_summed, u + 1)
                    dve.reciprocal(inv[j][:, :], y_ps[:, :, 0]).then_inc(inv_ready, 1)
                if more and k == 0:
                    q.dve_sum(dve, *nxt)
                elif more and k == 2:
                    q.dve_grow(dve, *nxt)
                elif more and k == 4:
                    q.dve_rest(dve, *nxt)
                elif more and k == 6:
                    q.dve_last(dve, *nxt)
                dve.wait_ge(sum_ready, n + 1)
                wait(dve, sum_read, n)
                at = t.acc[:, w, :]
                dve.tensor_tensor(at, at, sum_ps[c % 2][:, :], ALU.add).then_inc(sum_read, 1)
                if k == 8:
                    dve.wait_ge(inv_ready, u + 1)
                    dve.tensor_tensor(y[j][:, :].rearrange("p (h d) -> p h d", h=HM), y_ps[:, :, 1:V1],
                                      bcast(inv[j][:, :].unsqueeze(2), TP, HM, DM), ALU.mult).then_inc(y_ready, 1)
                if more and k == 0:
                    q.dve_floor(dve, *nxt)
                elif more and k == 2:
                    q.dve_scale(dve, *nxt)
                if former:
                    onto_x(u - 1)
            dve.sem_inc(val_ready, 1)
            held.w = weigh(0, 0)
            q.dve_square(dve, 0, 0, 0)
            for step in (q.dve_sum, q.dve_floor, q.dve_invert, q.dve_grow, q.dve_scale):
                step(dve, 0, 0)
            q.dve_rest(dve, 0, 0)
            q.dve_last(dve, 0, 0)
            dve.wait_ge(cleared, 1)
            over_slots(dve, body)
            add_bias(NT - 1)
            onto_x(NT - 1)

        @block.scalar
        def _(act):
            act.preload_act_table(ACT.Sqrt)
            act.sem_inc(q.rounded, 2)

            def turn_out(u, j):
                q.act_turn_out(act, u, j)
                act.activation(qT[j][:, 0, :, :], qT_ps[:, :, :], ACT.Square)
                act.activation(qT[j][:, 1, :, :], qT_ps[:, :, :], ACT.Copy).then_inc(qT_ready, 1)

            def body(u, j, k, n, c, i):
                if within(u, NT) and k < HM:
                    act.wait_ge(f_ready, u * HM + k + 1)
                    act.activation(phi[:, :, :], f_ps[:, :, :], ACT.Square).then_inc(phi_ready, 1)
                nxt = (u + 1, 1 - j)
                if within(u + 1, NT):
                    if k == 1:
                        q.act_root(act, *nxt)
                    elif k == 3:
                        q.act_round(act, *nxt)
                    elif k == 5:
                        q.act_middle(act, *nxt)
                    elif k == 8:
                        turn_out(*nxt)
                if k == 8:
                    act.wait_ge(yT_turned, u + 1)
                    act.activation(yT[j][:, :, :], yT_ps[:, :, :], ACT.Copy).then_inc(yT_ready, 1)
            q.act_root(act, 0, 0)
            q.act_round(act, 0, 0)
            q.act_middle(act, 0, 0)
            turn_out(0, 0)
            over_slots(act, body)

        @block.tensor
        def _(pe):
            flat = y_ps[:, :, :].rearrange("p h e -> p (h e)")

            def turn(u, j):
                mm = q.pe_turn(pe, u, j, t.identb)
                wait(pe, qT_ready, u)
                for b in range(FC):
                    mm = pe.transpose(qT_ps[:, b, :], q.unit[j][:, b * 128:(b + 1) * 128], t.ident[0:TP, 0:TP])
                mm.then_inc(q.turned, 1)

            def project(u, j):
                pe.wait_ge(yT_ready, u + 1)
                wait(pe, biased_ready, u)
                for b in range(FC):
                    mm = pe.matmul(out_ps[:, :], yT[j][:, b, :], t.wproj[:, b, :], start=(b == 0), stop=(b == FC - 1))
                mm.then_inc(out_ready, 1)

            def body(u, j, k, n, c, i):
                tile = within(u, NT)
                if tile and k == 0:
                    pe.wait_ge(qT_ready, u + 1)
                    wait(pe, y_ready, u)
                    pe.sem_inc(start, 1)
                    pe.matmul(flat, t.ones[0:1, 0:TP], x.slv_acc[0:1, 2, :, :].rearrange("p a e -> p (a e)"), start=True, stop=False,
                              skip_group_check=True)
                    for kind in range(2):
                        for half in range(2):
                            pe.matmul(flat[:, half * HW:(half + 1) * HW], qT[j][:, kind, half, :], x.coef[:, kind, half, :],
                                      start=False, stop=False, skip_group_check=True)
                if tile and k < HM:
                    for b in range(NPB):
                        mm = pe.matmul(f_ps[:, b, :], x.pair3[:, b * PB:(b + 1) * PB], q.turned_parts[j][:, k, 0:TP],
                                       start=True, stop=True)
                    mm.then_inc(f_ready, 1)
                pe.wait_ge(val_ready, n + 2)
                wait(pe, sum_read, n - 1)
                for e in range(EJ):
                    mm = pe.matmul(sum_ps[c % 2][:, :], hot[c % 2][:, e, :], val[c % 2][:, e, :], start=(e == 0), stop=(e == EJ - 1))
                mm.then_inc(sum_ready, 1)
                if tile and k < HM:
                    pe.wait_ge(phi_ready, u * HM + k + 1)
                    for b in range(NPB):
                        mm = pe.matmul(y_ps[:, k, :], phi[:, b, :], x.g_acc[:, k, b, :], start=False,
                                       stop=(b == NPB - 1), skip_group_check=True)
                    if k == HM - 1:
                        mm.then_inc(y_summed, 1)
                if k == 1 and within(1, u + 1 if isinstance(u, int) else 2):
                    project(u - 1, 1 - j)
                if k == 7 and within(u + 1, NT):
                    turn(u + 1, 1 - j)
                if k == 8:
                    pe.wait_ge(y_ready, u + 1)
                    for b in range(FC):
                        mm = pe.transpose(yT_ps[:, b, :], y[j][:, b * 128:(b + 1) * 128], t.ident[0:TP, 0:TP])
                    mm.then_inc(yT_turned, 1)
            turn(0, 0)
            over_slots(pe, body)
            project(NT - 1, 0)


def over_pipeline(eng, body):
    def rounds(i):
        for j in range(U):
            def at(d, i=i, j=j):
                k = j + d
                tile = i * U + k
                return (tile, k % U, i + k // U) if not isinstance(tile, int) or 0 <= tile < NT else None
            body(at)
    rounds(-1)
    rounds(0)
    with eng.Fori(1, NT // U - 1) as i:
        rounds(i)
    rounds(NT // U - 1)
    rounds(NT // U)


def stage_graph_ffn(nc, a, t):
    with Memory(nc) as s:
        spare = t.v_rows.ring
        w1 = spare[:, 8:10, :, :].rearrange("p s j f -> p (s j f)").rearrange("p (k n) -> p k n", k=FC)
        w2 = spare[:, 10:12, :, :].rearrange("p s j f -> p (s j) f")
        cols = s.sb("g_cols", [128, 2, HB])
        cols_in = s.sb("g_cols_in", [2 * HB, 128])
        gamma, beta, b2 = s.sb("gamma", [TP, F]), s.sb("beta", [TP, F]), s.sb("g_b2", [TP, F])
        wr, br = s.sb("wr", [128, FC, NEX]), s.sb("br", [TP, NEX])
        eps = s.sb("eps", [TP, 1])
        zeros = spare[:, 12:14, :, :].rearrange("p s j f -> p (s j f)")[:, 0:4 * RW]

        def slots(name, shape):
            return [s.sb(f"{name}{j}", shape) for j in range(U)]
        z = slots("z", [TP, F])
        s1 = [t.iota_n[0:TP, HB * TP + j * F:HB * TP + (j + 1) * F] for j in range(U)]
        s0 = [spare[0:TP, 14, i, :] for i in range(4)] + [spare[0:TP, 13, 2, :]]
        r1 = [spare[0:TP, 15, i, :] for i in range(4)] + [spare[0:TP, 13, 3, :]]
        hid = [spare[:, i, :, :].rearrange("p j f -> p (j f)")[:, 0:HB * TP].rearrange("p (b n) -> p b n", b=HB) for i in range(U)]
        branch = [spare[0:TP, U + i // 4, i % 4, :] for i in range(U)]
        scaled1, plus, scaled2 = (spare[0:TP, U + 1, i, :] for i in (1, 2, 3))
        fin = spare[0:TP, U + 2, 0, :]
        r1T, zT = (spare[:, U + 2, i, 0:FC * TP].rearrange("p (k n) -> p k n", k=FC) for i in (1, 2))
        low = t.iota_n[:, 0:HB * TP].rearrange("p (b n) -> p b n", b=HB)
        den = slots("den", [TP, 2, HG])
        STATS = range(4)
        st, mv, std, rstd = ([slots(f"{n}{b}", [TP, w]) for b in STATS] for n, w in (("st", 6), ("mv", 2), ("std", 1), ("rstd", 1)))
        r1_ps, z_ps = s.ps("r1_ps", [128, FC, TP]), s.ps("z_ps", [128, FC, TP])
        hid_ps = [s.ps(f"hid_ps{i}", [128, 2, 512]) for i in range(2)]
        y_ps, logit_ps = s.ps("gy_ps", [TP, F]), s.ps("logit_ps", [TP, NEX])
        w_in, cols_turned, cols_ready, carrier = s.sem("g_w_in"), s.sem("g_cols_turned"), s.sem("g_cols_ready"), s.sem("g_carrier")
        den_max, den_inv, weighted, s0_ready, scaled1_ready, r1_ready, low_ready, act_ready, plus_ready, s1_ready = (
            s.sem("g_" + n) for n in ("den_max", "den_inv", "weighted", "s0", "scaled1", "r1", "low", "act", "plus", "s1"))
        scaled2_ready, fin_ready, x_ready, z_ready, xn_ready, logit_read = (
            s.sem("g_" + n) for n in ("scaled2", "fin", "x", "z", "xn", "logit_read"))
        xn_first, xn_rest, small_in = s.sem("g_xn_first"), s.sem("g_xn_rest"), s.sem("g_small_in")
        zeros_ready, zero_out = s.sem("zeros_ready"), s.sem("zero_out")
        counted, var_ready, std_ready, rstd_ready = (s.sems("g_" + n, 4) for n in ("counted", "var", "std", "rstd"))
        r1_turned, r1T_ready, h_ready, biased, y_ready, z_turned, zT_ready, logit_ready = (
            s.sem("g_" + n) for n in ("r1_turned", "r1T", "h", "biased", "y", "z_turned", "zT", "logit"))
        block = s.block()

        @block.sync
        def _(sp):
            def load_xn(sem, at):
                sp.dma_start(t.xn_all[:, at, :], t.xn_dram.rearrange("(t p) f -> p t f", p=TP)[:, at, :]).then_inc(sem, 16)
            sp.dma_start(cols_in[0:HB, :], a["L0_gnn_b1"].rearrange("(b p) -> b p", p=128)).then_inc(small_in, 16)
            sp.dma_start(cols_in[HB:2 * HB, :], a["L0_gnn_alpha"].rearrange("(b p) -> b p", p=128)).then_inc(small_in, 16)
            load_xn(xn_first, slice(0, U))
            for ap, name in ((gamma, "L0_gnn_ln_g"), (beta, "L0_gnn_ln_b"), (b2, "L0_gnn_b2"), (br, "L0_ffn_br")):
                sp.dma_start(ap[:, :], a[name].partition_broadcast(TP)).then_inc(small_in, 16)
            for ap, src in ((w1, a["L0_gnn_W1"].rearrange("(k p) n -> p k n", p=128)),
                            (w2, a["L0_gnn_W2"].rearrange("(k p) n -> p k n", p=128)),
                            (wr, a["L0_ffn_Wr"].rearrange("(k p) n -> p k n", p=128))):
                sp.dma_start(ap[:, :, :], src).then_inc(w_in, 16)
            load_xn(xn_rest, slice(U, NT))
            sp.wait_ge(zeros_ready, 1)
            fills = ROWS // (128 * 4)
            for i in range(fills):
                sp.dma_start(t.x_rows.rearrange("(i p r) f -> i p (r f)", p=128, r=4)[i], zeros[:, :]).then_inc(zero_out, 16)
            sp.dma_start(t.x_sum[1 + N:, :], zeros[:, 0:F]).then_inc(zero_out, 16)
            sp.wait_ge(zero_out, (fills + 1) * 16)

        @block.gpsimd
        def _(pool):
            pool.memset(zeros[:, :], 0.0).then_inc(zeros_ready, 1)

        @block.vector
        def _(dve):
            def count(b, tile, src, ready):
                u, j, _ = tile
                dve.wait_ge(ready, u + 1)
                dve.bn_stats(st[b][j][:, :], src).then_inc(counted[b], 1)

            def join(b, tile):
                u, j, _ = tile
                dve.wait_ge(counted[b], u + 1)
                dve.sem_inc(carrier, 1)
                dve.bn_aggr(mv[b][j][:, :], st[b][j][:, :]).then_inc(var_ready[b], 1)

            def invert(b, tile):
                u, j, _ = tile
                dve.wait_ge(std_ready[b], u + 1)
                dve.reciprocal(rstd[b][j][:, :], std[b][j][:, :]).then_inc(rstd_ready[b], 1)

            def body(at):
                norm, end, ffn, make, route = at(2), at(-2), at(0), at(-4), at(-5)
                after, weigh, residual, join_x = at(-1), at(5), at(3), at(-3)
                if ffn:
                    u, j, _ = ffn
                    dve.wait_ge(biased, u + 1)
                    dve.scalar_tensor_tensor(low[:, :, :], hid[j][:, :, :], 0.0, bcast(cols[:, 1, :].unsqueeze(2), 128, HB, TP),
                                             ALU.min, ALU.mult).then_inc(low_ready, 1)
                if make:
                    invert(2, make)
                if route:
                    invert(3, route)
                if ffn:
                    u, j, _ = ffn
                    dve.wait_ge(low_ready, u + 1)
                    dve.scalar_tensor_tensor(hid[j][:, :, :], hid[j][:, :, :], 0.0, low[:, :, :], ALU.max, ALU.add
                                             ).then_inc(act_ready, 1)
                if make:
                    u, j, _ = make
                    dve.wait_ge(rstd_ready[2], u + 1)
                    dve.tensor_scalar(z[j][:, :], t.x_all[:, u, :], mv[2][j][:, 0:1], rstd[2][j][:, :], ALU.subtract,
                                      ALU.mult).then_inc(z_ready, 1)
                if route:
                    u, j, _ = route
                    dve.wait_ge(rstd_ready[3], u + 1)
                    dve.tensor_scalar(t.xn_all[:, u, :], z[j][:, :], mv[3][j][:, 0:1], rstd[3][j][:, :], ALU.subtract,
                                      ALU.mult).then_inc(xn_ready, 1)
                if norm:
                    u, j, _ = norm
                    invert(0, norm)
                    dve.scalar_tensor_tensor(scaled1[:, :], s0[j][:, :], mv[0][j][:, 0:1], gamma[:, :], ALU.subtract,
                                             ALU.mult).then_inc(scaled1_ready, 1)
                if end:
                    u, j, _ = end
                    invert(1, end)
                    dve.scalar_tensor_tensor(scaled2[:, :], s1[j][:, :], mv[1][j][:, 0:1], gamma[:, :], ALU.subtract,
                                             ALU.mult).then_inc(scaled2_ready, 1)
                if norm:
                    u, j, _ = norm
                    dve.wait_ge(rstd_ready[0], u + 1)
                    dve.wait_ge(scaled1_ready, u + 1)
                    dve.scalar_tensor_tensor(r1[j][:, :], scaled1[:, :], rstd[0][j][:, :], beta[:, :], ALU.mult,
                                             ALU.add).then_inc(r1_ready, 1)
                if end:
                    u, j, _ = end
                    dve.wait_ge(rstd_ready[1], u + 1)
                    dve.wait_ge(scaled2_ready, u + 1)
                    dve.scalar_tensor_tensor(fin[:, :], scaled2[:, :], rstd[1][j][:, :], beta[:, :], ALU.mult,
                                             ALU.add).then_inc(fin_ready, 1)
                if after:
                    u, j, _ = after
                    dve.wait_ge(y_ready, u + 1)
                    dve.tensor_tensor(plus[:, :], y_ps[:, :], b2[:, :], ALU.add).then_inc(plus_ready, 1)
                if end:
                    u, j, _ = end
                    dve.wait_ge(fin_ready, u + 1)
                    dve.tensor_tensor(t.x_all[:, u, :], t.x_all[:, u, :], fin[:, :], ALU.add).then_inc(x_ready, 1)
                if make:
                    count(3, make, z[make[1]][:, :], z_ready)
                if after:
                    u, j, _ = after
                    dve.wait_ge(plus_ready, u + 1)
                    dve.tensor_tensor(s1[j][:, :], plus[:, :], r1[j][:, :], ALU.add).then_inc(s1_ready, 1)
                if make:
                    join(3, make)
                if weigh:
                    u, j, _ = weigh
                    dve.tensor_scalar(den[j][:, 0, :], t.acc[:, u, F:F + HG], 1e-30, None, ALU.max).then_inc(den_max, 1)
                if after:
                    count(1, after, s1[after[1]][:, :], s1_ready)
                if weigh:
                    u, j, _ = weigh
                    dve.wait_ge(den_max, u + 1)
                    dve.reciprocal(den[j][:, 1, :], den[j][:, 0, :]).then_inc(den_inv, 1)
                if after:
                    join(1, after)
                if join_x:
                    u, j, _ = join_x
                    dve.wait_ge(x_ready, u + 1)
                    dve.sem_inc(carrier, 1)
                    dve.bn_stats(st[2][j][:, :], t.x_all[:, u, :]).then_inc(counted[2], 1)
                if residual:
                    u, j, i = residual
                    dve.wait_ge(xn_first if isinstance(i, int) and i == 0 else xn_rest, 16)
                    dve.wait_ge(weighted, u + 1)
                    dve.tensor_tensor(s0[j][:, :], branch[j][:, :], t.xn_all[:, u, :], ALU.add).then_inc(s0_ready, 1)
                if join_x:
                    join(2, join_x)
                if residual:
                    count(0, residual, s0[residual[1]][:, :], s0_ready)
                if route:
                    u, j, _ = route
                    dve.wait_ge(logit_ready, u + 1)
                    dve.tensor_tensor(t.logits[:, u, :], logit_ps[:, :], br[:, :], ALU.add).then_inc(logit_read, 1)
                if residual:
                    join(0, residual)
            dve.wait_ge(small_in, 6 * 16)
            dve.memset(eps[:, :], EPS)
            dve.wait_ge(cols_turned, 1)
            dve.tensor_copy(cols[:, :, :], z_ps[:, 0, 0:2 * HB].rearrange("p (c b) -> p c b", c=2)).then_inc(cols_ready, 1)
            dve.wait_ge(cols_ready, 1)
            over_pipeline(dve, body)

        @block.scalar
        def _(act):
            act.preload_act_table(ACT.Sqrt)

            def root(b, tile):
                if tile:
                    u, j, _ = tile
                    act.wait_ge(var_ready[b], u + 1)
                    act.activation(std[b][j][:, :], mv[b][j][:, 1:2], ACT.Sqrt, bias=eps[:, :]).then_inc(std_ready[b], 1)

            def body(at):
                if at(-5):
                    u, j, _ = at(-5)
                    act.wait_ge(z_turned, u + 1)
                    act.activation(zT[:, :, :], z_ps[:, :, :], ACT.Copy).then_inc(zT_ready, 1)
                if at(1):
                    u, j, _ = at(1)
                    act.wait_ge(r1_turned, u + 1)
                    act.activation(r1T[:, :, :], r1_ps[:, :, :], ACT.Copy).then_inc(r1T_ready, 1)
                if at(4):
                    u, j, _ = at(4)
                    act.wait_ge(den_inv, u + 1)
                    for h in range(HG):
                        one = act.activation(branch[j][:, h * DG:(h + 1) * DG], t.acc[:, u, h * DG:(h + 1) * DG], ACT.Copy,
                                             scale=den[j][:, 1, h:h + 1])
                    one.then_inc(weighted, 1)
                if at(1):
                    u, j, i = at(1)
                    act.wait_ge(h_ready, u + 1)
                    for b in range(HB):
                        one = act.activation(hid[j][:, b, :], hid_ps[j % 2][:, b // 4, (b % 4) * TP:(b % 4 + 1) * TP],
                                             ACT.Identity, bias=cols[:, 0, b:b + 1])
                    one.then_inc(biased, 1)
                root(3, at(-4))
                root(1, at(-1))
                root(2, at(-3))
                root(0, at(3))
            over_pipeline(act, body)

        @block.tensor
        def _(pe):
            pe.wait_ge(small_in, 6 * 16)
            pe.transpose(z_ps[:, 0, 0:2 * HB], cols_in[:, :], t.ident[0:2 * HB, 0:2 * HB]).then_inc(cols_turned, 1)
            pe.wait_ge(cols_ready, 1)
            pe.wait_ge(w_in, 3 * 16)

            def body(at):
                if at(-5):
                    u, j, _ = at(-5)
                    pe.wait_ge(z_ready, u + 1)
                    wait(pe, zT_ready, u)
                    for k in range(FC):
                        mm = pe.transpose(z_ps[:, k, :], z[j][:, k * 128:(k + 1) * 128], t.ident[0:TP, 0:TP])
                    mm.then_inc(z_turned, 1)
                if at(1):
                    u, j, _ = at(1)
                    pe.wait_ge(r1_ready, u + 1)
                    wait(pe, r1T_ready, u)
                    for k in range(FC):
                        mm = pe.transpose(r1_ps[:, k, :], r1[j][:, k * 128:(k + 1) * 128], t.ident[0:TP, 0:TP])
                    mm.then_inc(r1_turned, 1)
                if at(-5):
                    u, j, _ = at(-5)
                    pe.wait_ge(zT_ready, u + 1)
                    wait(pe, logit_read, u)
                    for k in range(FC):
                        mm = pe.matmul(logit_ps[:, :], zT[:, k, :], wr[:, k, :], start=(k == 0), stop=(k == FC - 1))
                    mm.then_inc(logit_ready, 1)
                if at(1):
                    u, j, _ = at(1)
                    pe.wait_ge(r1T_ready, u + 1)
                    wait(pe, biased, psum_turn(u, j))
                    for b in range(HB):
                        for k in range(FC):
                            mm = pe.matmul(hid_ps[j % 2][:, b // 4, (b % 4) * TP:(b % 4 + 1) * TP], w1[:, k, b * 128:(b + 1) * 128],
                                           r1T[:, k, :], start=(k == 0), stop=(k == FC - 1))
                    mm.then_inc(h_ready, 1)
                if at(0):
                    u, j, _ = at(0)
                    pe.wait_ge(act_ready, u + 1)
                    wait(pe, plus_ready, u)
                    for b in range(HB):
                        mm = pe.matmul(y_ps[:, :], hid[j][:, b, :], w2[:, b, :], start=(b == 0), stop=(b == HB - 1))
                    mm.then_inc(y_ready, 1)
            over_pipeline(pe, body)


def stage_experts(nc, a, t, out):
    with Memory(nc) as m:
        tile_ex = m.sb("tile_ex", [1, NMT], I32)
        table = m.sb("ex_table", [128, NEX, HB + 2 * FC])

        w1 = [m.sb(f"e_w1{i}", [128, FC, HID]) for i in range(2)]
        w2 = [m.sb(f"e_w2{i}", [128, HB, F]) for i in range(2)]
        b2 = [m.sb(f"e_b2{i}", [128, F]) for i in range(2)]
        w1_in, w2_in, b2_in = (m.sems("e_" + x, 2) for x in ("w1_in", "w2_in", "b2_in"))

        def load_first(sp, ex, par):
            sp.dma_start(w1[par][:, :, :], a["L0_ffn_W1"].rearrange("e (k p) n -> e p k n", p=128)[ex]).then_inc(w1_in[par], 16)

        def load_second(sp, ex, par):
            sp.dma_start(w2[par][:, :, :], a["L0_ffn_W2"].rearrange("e (b p) n -> e p b n", p=128)[ex]).then_inc(w2_in[par], 16)
            sp.dma_start(b2[par][:, :], a["L0_ffn_b2"][ex].partition_broadcast(128)).then_inc(b2_in[par], 16)

        with Memory(nc) as s:
            before = s.sb("e_before", [TP, NEX * NEX])
            keep = s.sb("keep", [TP, NEX * NT])
            tri = s.sb("tri", [TP, TP])
            tile_at = s.sb("tile_at", [1, NMT])
            tab_in = s.sb("tab_in", [NEX * HB + 2 * NEX * FC, 128])
            more, same = s.sb("more", [TP, NT, NEX, NEX]), s.sb("same", [TP, NT, NEX, NEX])
            rank = s.sb("rank", [TP, NT, NEX])
            pick = s.sb("pick", [TP, 3, NT, NEX])
            prod = s.sb("r_prod", [TP, 2, NT, NEX])
            best = s.sb("best", [TP, 2, NT])
            diff, p2, den = s.sb("diff", [TP, NT]), s.sb("p2", [TP, NT]), s.sb("r_den", [TP, NT])
            tot, upto, at = s.sb("tot", [TP, NEX, NT]), s.sb("upto", [TP, NEX, NT]), s.sb("at", [TP, NEX, NT])
            size, size_i = s.sb("size", [TP, 4, NEX]), s.sb("size_i", [TP, 2, NEX], I32)
            pos_f = s.sb("pos_f", [TP, 2, NT])
            past = s.sb("past", [1, NMT, NEX])
            tile_f = s.sb("tile_f", [1, 2, NMT])
            weight = s.sb("weight", [TP, 2, NT])
            pos = s.sb("pos", [TP, NT, 2], I32)
            node = s.sb("node", [TP, NT])
            tail = s.sb("tail", [TP, NT, 2, 2])
            rows = [s.sb(f"rows{j}", [TP, 2, RW]) for j in range(U)]
            idx = [s.sb(f"s_idx{j}", [TP, 2], I32) for j in range(U)]
            pre_ps, tot_ps = s.ps("pre_ps", [TP, NT, NEX]), s.ps("tot_ps", [TP, NT, NEX])
            tab_ps = s.ps("tab_ps", [128, 128])
            c_in, dve_order, picked, counted, diff_ready, p2_ready, tab_turned = (
                s.sem("r_" + x) for x in ("c_in", "order", "picked", "counted", "diff", "p2", "tab"))
            rows_ready, idx_ready, carrier = s.sem("rows_ready"), s.sem("s_idx_ready"), s.sem("s_carrier")
            tail_ready, tiles_known, sum_out = s.sem("tail_ready"), s.sem("tiles_known"), s.sem("sum_out")
            row_out = s.gather_sems("row_out", U)
            block = s.block()

            @block.sync
            def _(sp):
                for ap, name in ((before, "c_before"), (keep, "c_keep")):
                    sp.dma_start(ap[:, :], a[name][0, :].partition_broadcast(TP)).then_inc(c_in, 16)
                sp.dma_start(tri[:, :], a["c_tri"]).then_inc(c_in, 16)
                sp.dma_start(tile_at[:, :], a["c_tile_at"]).then_inc(c_in, 16)
                sp.dma_start(node[:, :], a["c_win_node"]).then_inc(c_in, 16)
                lo = NEX * HB
                sp.dma_start(tab_in[0:lo, :], a["L0_ffn_b1"].rearrange("e (b p) -> (e b) p", p=128)).then_inc(c_in, 16)
                sp.dma_start(tab_in[lo:lo + NEX * FC, :], a["L0_ffn_ln_g"].rearrange("e (k p) -> (e k) p", p=128)).then_inc(c_in, 16)
                sp.dma_start(tab_in[lo + NEX * FC:, :], a["L0_ffn_ln_b"].rearrange("e (k p) -> (e k) p", p=128)).then_inc(c_in, 16)
                sp.dma_start(t.x_sum[1:1 + N, :].rearrange("(t p) f -> p t f", p=TP), t.x_all[:, :, :]).then_inc(sum_out, 16)
                sp.wait_ge(tiles_known, 1)
                for n in range(2):
                    ex = sp.value_load(tile_ex[0:1, n:n + 1], min_val=0, max_val=NEX - 1)
                    load_first(sp, ex, n)
                    if n == 0:
                        load_second(sp, ex, n)
                sp.wait_ge(sum_out, 16)

            @block.tensor
            def _(pe):
                pe.wait_ge(c_in, 8 * 16)
                rows_ = NEX * HB + 2 * NEX * FC
                pe.transpose(tab_ps[:, 0:rows_], tab_in[:, :], t.ident[0:rows_, 0:rows_]).then_inc(tab_turned, 1)
                pe.wait_ge(picked, 1)
                flat = pick[:, 2, :, :].rearrange("p t e -> p (t e)")
                pe.matmul(pre_ps[:, :, :].rearrange("p t e -> p (t e)"), tri[:, :], flat, start=True, stop=True)
                pe.matmul(tot_ps[:, :, :].rearrange("p t e -> p (t e)"), t.ones[0:TP, 0:TP], flat, start=True, stop=True
                          ).then_inc(counted, 1)

            @block.scalar
            def _(act):
                act.preload_act_table(ACT.Exp)
                act.wait_ge(diff_ready, 1)
                act.activation(p2[:, :], diff[:, :], ACT.Exp).then_inc(p2_ready, 1)

            @block.vector
            def _(dve):
                order = Order(dve, dve_order)
                L = t.logits
                full = (TP, NT, NEX, NEX)
                mine, other = bcast(L[:, :, :].unsqueeze(3), *full), bcast(L[:, :, :].unsqueeze(2), *full)
                order(dve.tensor_tensor(more[:, :, :, :], other, mine, ALU.is_gt))
                order(dve.tensor_tensor(same[:, :, :, :], other, mine, ALU.is_equal))
                dve.wait_ge(c_in, 8 * 16)
                flat = lambda x: x[:, :, :, :].rearrange("p t i j -> p t (i j)")
                order(dve.tensor_tensor(flat(same), flat(same), bcast(before[:, :].unsqueeze(1), TP, NT, NEX * NEX), ALU.mult))
                order(dve.tensor_tensor(flat(more), flat(more), flat(same), ALU.add))
                order(dve.tensor_reduce(rank[:, :, :], more[:, :, :, :], AX.X, ALU.add))
                order(dve.tensor_scalar(pick[:, 0, :, :], rank[:, :, :], 0.0, None, ALU.is_equal))
                order(dve.tensor_scalar(pick[:, 1, :, :], rank[:, :, :], 1.0, None, ALU.is_equal))
                order(dve.tensor_tensor(pick[:, 2, :, :], pick[:, 0, :, :], pick[:, 1, :, :], ALU.add))
                dve.sem_inc(picked, 1)
                for c in range(2):
                    order(dve.tensor_tensor(prod[:, c, :, :], L[:, :, :], pick[:, c, :, :], ALU.mult))
                order(dve.tensor_reduce(best[:, :, :], prod[:, :, :, :], AX.X, ALU.add))
                order(dve.tensor_tensor(diff[:, :], best[:, 1, :], best[:, 0, :], ALU.subtract))
                dve.sem_inc(diff_ready, 1)
                dve.wait_ge(p2_ready, 1)
                order(dve.tensor_scalar(den[:, :], p2[:, :], 1.0, None, ALU.add))
                order(dve.reciprocal(weight[:, 0, :], den[:, :]))
                order(dve.tensor_tensor(weight[:, 1, :], p2[:, :], weight[:, 0, :], ALU.mult))
                dve.wait_ge(counted, 1)
                order(dve.tensor_copy(tot[:, :, :], tot_ps[:, :, :].rearrange("p t e -> p e t")))
                order(dve.tensor_tensor_scan(upto[:, :, :].rearrange("p e t -> p (e t)"), keep[:, :],
                                             tot[:, :, :].rearrange("p e t -> p (e t)"), 0.0, ALU.mult, ALU.add))
                order(dve.tensor_scalar(size[:, 0, :], upto[:, :, NT - 1], float(MT - 1), None, ALU.add))
                order(dve.tensor_copy(size_i[:, 0, :], size[:, 0, :]))
                bits = MT.bit_length() - 1
                order(dve.tensor_scalar(size_i[:, 1, :], size_i[:, 0, :], bits, bits, ALU.logical_shift_right, ALU.logical_shift_left))
                order(dve.tensor_copy(size[:, 1, :], size_i[:, 1, :]))
                order(dve.tensor_tensor_scan(size[:, 2, :], t.ones[0:TP, 0:NEX], size[:, 1, :], 0.0, ALU.mult, ALU.add))
                order(dve.tensor_tensor(size[:, 3, :], size[:, 2, :], size[:, 1, :], ALU.subtract))
                order(dve.tensor_tensor(at[:, :, :], upto[:, :, :], tot[:, :, :], ALU.subtract))
                order(dve.tensor_tensor(at[:, :, :], at[:, :, :], bcast(size[:, 3, :].unsqueeze(2), TP, NEX, NT), ALU.add))
                order(dve.tensor_tensor(at[:, :, :], at[:, :, :], pre_ps[:, :, :].rearrange("p t e -> p e t"), ALU.add))
                for c in range(2):
                    order(dve.tensor_tensor(prod[:, c, :, :], at[:, :, :].rearrange("p e t -> p t e"), pick[:, c, :, :], ALU.mult))
                order(dve.tensor_reduce(pos_f[:, :, :], prod[:, :, :, :], AX.X, ALU.add))
                order(dve.tensor_copy(pos[:, :, :], pos_f[:, :, :].rearrange("p c t -> p t c")))
                order(dve.tensor_tensor(past[:, :, :], bcast(size[0:1, 2, :].unsqueeze(1), 1, NMT, NEX),
                                        bcast(tile_at[:, :].unsqueeze(2), 1, NMT, NEX), ALU.is_le))
                order(dve.tensor_reduce(tile_f[:, 0, :], past[:, :, :], AX.X, ALU.add))
                order(dve.tensor_scalar(tile_f[:, 1, :], tile_f[:, 0, :], float(NEX - 1), None, ALU.min))
                order(dve.tensor_copy(tile_ex[:, :], tile_f[:, 1, :]))
                dve.sem_inc(tiles_known, 1)
                dve.tensor_copy(tail[:, :, :, 1], weight[:, :, :].rearrange("p c t -> p t c")).then_inc(tail_ready, 1)
                dve.tensor_scalar(tail[:, :, :, 0], bcast(node[:, :].unsqueeze(2), TP, NT, 2), -1.0, 1.0, ALU.mult, ALU.add
                                  ).then_inc(tail_ready, 1)
                dve.wait_ge(tab_turned, 1)
                lo = NEX * HB
                dve.tensor_copy(table[:, :, 0:HB], tab_ps[:, 0:lo].rearrange("p (e b) -> p e b", b=HB))
                for c in range(2):
                    dve.tensor_copy(table[:, :, HB + c * FC:HB + (c + 1) * FC],
                                    tab_ps[:, lo + c * NEX * FC:lo + (c + 1) * NEX * FC].rearrange("p (e k) -> p e k", k=FC))

                dve.wait_ge(tail_ready, 2)

                def make_rows(u, j, i, last):
                    wait(dve, row_out[j], i * 32)
                    dve.tensor_scalar(idx[j][:, :], pos[:, u, :], 0.0, None, ALU.add).then_inc(idx_ready, 1)
                    dve.tensor_scalar(rows[j][:, :, F:RW], tail[:, u, :, :], 0.0, None, ALU.add).then_inc(rows_ready, 1)
                    dve.tensor_scalar(rows[j][:, :, 0:F], bcast(t.xn_all[:, u, :].unsqueeze(1), TP, 2, F), 0.0, None, ALU.add
                                      ).then_inc(rows_ready, 1)
                over_tiles(dve, make_rows)

            @block.gpsimd
            def _(pool):
                def scatter(u, j, i, last):
                    pool.wait_ge(idx_ready, u + 1)
                    pool.wait_ge(rows_ready, u * 2 + 2)
                    pool.sem_inc(carrier, 1)
                    for c in range(2):
                        pool.indirect_dma_start(out=t.x_rows, out_offset=bass.IndirectOffsetOnAxis(ap=idx[j][:, c:c + 1], axis=0),
                                                in_=rows[j][:, c, :], in_offset=None).then_inc(row_out[j], 16)
                over_tiles(pool, scatter)
                for j in range(U):
                    pool.wait_ge(row_out[j], NT // U * 32)

        with Memory(nc) as s:
            xr = [s.sb(f"xr{i}", [128, 2, RW]) for i in range(2)]
            tails = s.sb("tails", [128, NMT, 2, 2])
            unused = s.sb("unused", [128, 1])
            to = [s.sb(f"to{i}", [128, 2], I32) for i in range(2)]
            to_f = s.sb("to_f", [128, 2])
            yw = [s.sb(f"e_yw{i}", [128, 2, F]) for i in range(2)]
            small = [s.sb(f"small{i}", [128, HB + 2 * FC]) for i in range(2)]
            xT = [s.sb(f"e_xT{i}", [128, FC, MT]) for i in range(2)]
            hT = [s.sb(f"e_hT{i}", [128, HB, MT]) for i in range(2)]
            y = s.sb("e_y", [128, 2, F])
            turn_ps = [s.ps(f"e_turn{i}", [128, FC, MT]) for i in range(2)]
            h_ps = s.ps("e_h", [128, HB, MT])
            y_ps = s.ps("e_yps", [128, 2, 512])
            x_in, y_out, copied, unused_in = s.sems("e_x_in", 2), s.gather_sems("e_y_out", 2), s.sem("copied"), s.sem("unused_in")
            tail_kept, to_f_ready, to_ready, y_weighted, carrier = (
                s.sem("e_" + x) for x in ("tail_kept", "to_f", "to", "y_weighted", "carrier"))
            small_ready, turned, xT_ready, h_ready, h_read, y_ready, y_read = (
                s.sem("e_" + x) for x in ("small", "turned", "xT", "h", "h_read", "y", "y_read"))
            block = s.block()

            def over_experts(eng, body):
                for par in range(2):
                    body(par, par, 0, False)
                with eng.Fori(1, NMT // 2 - 1) as i:
                    for par in range(2):
                        body(i * 2 + par, par, i, False)
                for par in range(2):
                    body(NMT - 2 + par, par, NMT // 2 - 1, par == 1)

            @block.sync
            def _(sp):
                def rows_and_first(n, par):
                    wait(sp, tail_kept, n - 1)
                    wait(sp, turned, n - 1)
                    sp.dma_start(xr[par][:, :, :], t.x_rows[ds(n * MT, MT), :].rearrange("(s p) f -> p s f", p=128)
                                 ).then_inc(x_in[par], 16)
                    if isinstance(n, int) and n < 2:
                        return
                    ex = sp.value_load(tile_ex[0:1, ds(n, 1)], min_val=0, max_val=NEX - 1)
                    wait(sp, h_ready, (n - 1) * (HB // 2))
                    load_first(sp, ex, par)

                def body(n, par, i, last):
                    if not last:
                        rows_and_first(n + 1, 1 - par)
                    if isinstance(n, int) and n < 1:
                        return
                    ex = sp.value_load(tile_ex[0:1, ds(n, 1)], min_val=0, max_val=NEX - 1)
                    wait(sp, y_read, n - 1)
                    load_second(sp, ex, par)
                rows_and_first(0, 0)
                sp.dma_start(unused[:, :], a["c_unused"]).then_inc(unused_in, 16)
                over_experts(sp, body)
                for par in range(2):
                    sp.wait_ge(y_out[par], NMT // 2 * 32)
                sp.dma_start(out[:, :].rearrange("(p c) f -> p (c f)", p=TP), t.x_sum[1:1 + N, :].rearrange("(p c) f -> p (c f)", p=TP)
                             ).then_inc(copied, 16)
                sp.wait_ge(copied, 16)

            @block.gpsimd
            def _(pool):
                def body(n, par, i, last):
                    pool.wait_ge(to_ready, n + 1)
                    pool.wait_ge(y_weighted, n * 2 + 2)
                    for half in range(2):
                        if half:
                            pool.wait_ge(y_out[par], i * 32 + 16)
                        else:
                            wait(pool, y_out[1 - par], (i + par) * 32)
                        pool.sem_inc(carrier, 1)
                        pool.indirect_dma_start(out=t.x_sum, out_offset=bass.IndirectOffsetOnAxis(ap=to[par][:, half:half + 1], axis=0),
                                                in_=yw[par][:, half, :], in_offset=None, compute_op=ALU.add).then_inc(y_out[par], 16)
                over_experts(pool, body)

            @block.vector
            def _(dve):
                def prepare(n, par, i):
                    ex = dve.value_load(tile_ex[0:1, ds(n, 1)], min_val=0, max_val=NEX - 1)
                    dve.wait_ge(h_read, n * (HB // 2))
                    dve.wait_ge(turned, n + 1)
                    dve.tensor_scalar(small[par][:, :], table[:, ex, :], 0.0, None, ALU.add).then_inc(small_ready, 1)
                    dve.wait_ge(small_ready, n + 1)
                    for k in range(FC):
                        one = dve.tensor_scalar(xT[par][:, k, :], turn_ps[par][:, k, :], small[par][:, HB + k:HB + k + 1],
                                                small[par][:, HB + FC + k:HB + FC + k + 1], ALU.mult, ALU.add)
                    one.then_inc(xT_ready, 1)
                    dve.wait_ge(x_in[par], i * 16 + 16)
                    dve.tensor_scalar(tails[:, n, :, :], xr[par][:, :, F:RW], 0.0, None, ALU.add).then_inc(tail_kept, 1)

                def body(n, par, i, last):
                    if within(n + 2, NMT):
                        prepare(n + 2, par, i + 1)
                    wait(dve, y_out[par], i * 32)
                    dve.wait_ge(tail_kept, n + 1)
                    dve.scalar_tensor_tensor(to_f[:, :], tails[:, n, :, 0], 0.0, bcast(unused[:, :], 128, 2), ALU.is_equal,
                                             ALU.mult).then_inc(to_f_ready, 1)
                    dve.wait_ge(to_f_ready, n + 1)
                    dve.tensor_tensor(to[par][:, :], to_f[:, :], tails[:, n, :, 0], ALU.add).then_inc(to_ready, 1)
                    dve.wait_ge(b2_in[par], i * 16 + 16)
                    dve.wait_ge(y_ready, n + 1)
                    dve.tensor_tensor(y[:, :, :], y_ps[:, :, 0:F], bcast(b2[par][:, :].unsqueeze(1), 128, 2, F), ALU.add
                                      ).then_inc(y_read, 1)
                    dve.wait_ge(y_read, n + 1)
                    for half in range(2):
                        dve.tensor_scalar(yw[par][:, half, :], y[:, half, :], tails[:, n, half, 1:2], None, ALU.mult
                                          ).then_inc(y_weighted, 1)
                for n in range(2):
                    prepare(n, n, 0)
                dve.wait_ge(unused_in, 16)
                over_experts(dve, body)

            @block.scalar
            def _(act):
                act.preload_act_table(ACT.Gelu)
                act.sem_inc(h_read, HB // 2)

                def gelus(n, par):
                    act.wait_ge(small_ready, n + 1)
                    for b in range(HB):
                        if b % 2 == 0:
                            act.wait_ge(h_ready, n * (HB // 2) + b // 2 + 1)
                        gelu = act.activation(hT[par][:, b, :], h_ps[:, b, :], ACT.Gelu, bias=small[par][:, b:b + 1])
                        if b % 2:
                            gelu.then_inc(h_read, 1)

                def body(n, par, i, last):
                    if not last:
                        gelus(n + 1, 1 - par)
                gelus(0, 0)
                over_experts(act, body)

            @block.tensor
            def _(pe):
                def turn(n, par, i):
                    pe.wait_ge(x_in[par], i * 16 + 16)
                    for half in range(2):
                        for k in range(FC):
                            mm = pe.transpose(turn_ps[par][:, k, half * 128:(half + 1) * 128], xr[par][:, half, k * 128:(k + 1) * 128],
                                              t.ident[:, :])
                    mm.then_inc(turned, 1)

                def hidden(n, par, i):
                    pe.wait_ge(w1_in[par], i * 16 + 16)
                    pe.wait_ge(xT_ready, n + 1)
                    for b in range(HB):
                        if b % 2 == 0:
                            pe.wait_ge(h_read, n * (HB // 2) + b // 2 + 1)
                        for k in range(FC):
                            mm = pe.matmul(h_ps[:, b, :], w1[par][:, k, b * 128:(b + 1) * 128], xT[par][:, k, :],
                                           start=(k == 0), stop=(k == FC - 1))
                        if b % 2:
                            mm.then_inc(h_ready, 1)

                def body(n, par, i, last):
                    if within(n + 2, NMT):
                        turn(n + 2, par, i + 1)
                    if not last:
                        hidden(n + 1, 1 - par, i + par)
                    pe.wait_ge(w2_in[par], i * 16 + 16)
                    wait(pe, y_read, n)
                    for b in range(HB):
                        if b % 2 == 0:
                            pe.wait_ge(h_read, (n + 1) * (HB // 2) + b // 2 + 1)
                        for half in range(2):
                            mm = pe.matmul(y_ps[:, half, 0:F], hT[par][:, b, half * 128:(half + 1) * 128], w2[par][:, b, :],
                                           start=(b == 0), stop=(b == HB - 1))
                    mm.then_inc(y_ready, 1)
                for n in range(2):
                    turn(n, n, 0)
                hidden(0, 0, 0)
                over_experts(pe, body)


def mix_memory(m):
    x = Shared()
    x.pair3 = m.sb("pair3", [3 * DM, NPAIR], BF16)
    x.pair4 = m.sb("pair4", [128, NPAIR])
    x.pairT = m.sb("pairT", [PB, NPB, DM])
    x.g_acc = m.sb("g_acc", [PB, HM, NPB, V1])
    x.slv_acc = m.sb("slv_acc", [128, 3, 2, HW])
    x.coef = m.sb("coef", [128, 2, 2, HW])
    x.k_factor, x.q_factor = m.sb("k_factor", [TP, HM]), m.sb("q_factor", [TP, HM])
    x.proj_bias = m.sb("proj_bias", [TP, F])
    return x


def build(nc, a, out):
    def dram(name, shape, dt=F32):
        return nc.dram_tensor(name, shape, dt, kind="Internal").ap()

    t = Shared()
    t.k_tab, t.v_tab = dram("k_tab", (N, F)), dram("v_tab", (N, F))
    t.mix_q, t.xn_dram = dram("mix_q", (N, F)), dram("xn_dram", (N, F))
    t.dst_pad = dram("dst_pad", (E_PAD + 2,), I32)
    t.e_dram, t.ex_dram = dram("e_dram", (HG, E_PAD)), dram("ex_dram", (HG, E_PAD))
    t.x_rows = dram("x_rows", (ROWS, RW))
    t.x_sum = dram("x_sum", (1 + N + 128, F))
    with Memory(nc) as m:
        x_buf = m.sb("x_buf", [128, NT, F])
        t.x_all, t.xnT = x_buf[0:TP, :, :], x_buf[:, :, 0:FC * TP]
        xn_buf = m.sb("xn_buf", [128, NT, F])
        t.xn_all = xn_buf[0:TP, :, :]
        t.x_buf, t.xn_buf = x_buf, xn_buf
        t.w_late = xn_buf[:, 0:4 * FC, :].rearrange("p (k b) f -> p k (b f)", k=FC)
        t.late_bias = xn_buf[0:TP, 4 * FC:4 * FC + 4, :].rearrange("p b f -> p (b f)")
        t.late = xn_buf[:, 4 * FC + 4:, :]
        t.ident, t.identb = m.sb("ident", [128, 128]), m.sb("identb", [128, 128], BF16)
        t.ones = m.sb("ones", [128, 128])
        t.wproj = m.sb("wproj", [128, FC, F])
        t.logits = m.sb("logits", [TP, NT, NEX])
        with Memory(nc) as e:
            t.win_node = e.sb("win_node", [TP, NT])
            t.dst_all = e.sb("dst_all", [128, G_PAD, EJ])
            t.src_all = e.sb("src_all", [128, G_PAD, EJ], I32)
            t.step_g = e.sb("step_g", [1, N_STEPS], I32)
            t.step_w = e.sb("step_w", [1, N_STEPS], I32)
            t.need_k = e.sb("need_k", [1, N_GROUPS], I32)
            t.need_v = e.sb("need_v", [1, N_GROUPS], I32)
            t.e_all = e.sb("e_all", [128, HG, ET_PAD])
            t.e_flat = t.e_all[:, :, :].rearrange("p h t -> p (h t)")
            t.mix = mix_memory(e)
            with Memory(nc) as q:
                t.q3 = q.sb("q3", [TP, NT, 3 * F], BF16)
                stage_project(nc, a, t, q)
                stage_scores_and_sums(nc, a, t)
            t.iota_n = e.sb("iota_n", [128, N])
            t.v_rows = Gather(e, "v", t.v_tab, V_RING)
            stage_edge_softmax(nc, a, t)
            t.acc = e.sb("acc", [TP, NT, F + HG])
            stage_aggregate_and_mix(nc, a, t)
            stage_graph_ffn(nc, a, t)
        stage_experts(nc, a, t, out)


_INS = ["x", "src", "dst", "L0_gnn_Wq", "L0_gnn_Wk", "L0_gnn_Wv", "L0_gnn_ln_g", "L0_gnn_ln_b", "L0_gnn_W1", "L0_gnn_b1",
        "L0_gnn_alpha", "L0_gnn_W2", "L0_gnn_b2", "L0_mix_Wqkv", "L0_mix_bqkv", "L0_mix_Wproj", "L0_mix_bproj",
        "L0_mix_temperature", "L0_ffn_Wr", "L0_ffn_br", "L0_ffn_ln_g", "L0_ffn_ln_b", "L0_ffn_W1", "L0_ffn_b1",
        "L0_ffn_W2", "L0_ffn_b2"]


def constants():
    f32 = np.float32
    i, j = np.triu_indices(DM, 1)
    pair = np.zeros((DM, NPAIR), f32)
    pair[i, np.arange(NPAIR)] = 1
    pair[j, np.arange(NPAIR)] = 1
    low = pair.astype(mybir.dt.np(BF16))
    tail = np.zeros((2, E_PAD + 1 - EDGES), np.int32)
    tail[0] = PAD_DST
    tail[0, -1] = -2
    keep = np.ones((NEX, NT), f32)
    keep[:, 0] = 0
    return {
        "c_ident": np.eye(128, dtype=f32), "c_identb": np.eye(128).astype(low.dtype),
        "c_iota": np.arange(N, dtype=f32)[None, :],
        "c_win_node": -(np.arange(NT)[None, :] * TP + np.arange(TP)[:, None]).astype(f32),
        "c_win_end": ((np.arange(NT)[:, None] + 1) * TP).astype(f32), "c_win_id": np.arange(NT, dtype=f32)[:, None],
        "c_count": np.arange(N_STEPS, dtype=f32)[None, :],
        "c_head": np.array([[-1], [0]], np.int32), "c_tail": tail,
        "c_pair3": np.concatenate([low] * 3), "c_pair4": np.concatenate([pair] * 4),
        "c_pairT": np.ascontiguousarray(pair.T.reshape(NPB, PB, DM).transpose(1, 0, 2)),
        "c_before": np.tri(NEX, k=-1, dtype=f32).reshape(1, -1), "c_keep": keep.reshape(1, -1),
        "c_tri": np.triu(np.ones((TP, TP), f32), 1), "c_unused": (1 + N + np.arange(128)).astype(f32)[:, None],
        "c_tile_at": (np.arange(NMT) * MT).astype(f32)[None, :],
    }


def kernel(**inputs):
    import concourse.bacc as bacc
    from concourse.bass_utils import run_bass_kernel_spmd

    nc = bacc.Bacc("TRN2", target_bir_lowering=False, num_devices=1)
    arrays = {name: np.ascontiguousarray(inputs[name]) for name in _INS}
    arrays.update(constants())
    aps = {name: nc.dram_tensor(name, x.shape, mybir.dt.from_np(x.dtype), kind="ExternalInput").ap() for name, x in arrays.items()}
    out = nc.dram_tensor("out", (N, F), F32, kind="ExternalOutput").ap()
    build(nc, aps, out)
    result = run_bass_kernel_spmd(nc, [arrays], core_ids=[0])
    return result.results[0]["out"]
```
